# Optimizing a Trainium2 kernel written in Bass

```python
import numpy as np
import jax
import jax.numpy as jnp

def _softmax(x, axis=-1):
    return jax.nn.softmax(x, axis=axis)

def _gelu(x):
    return jax.nn.gelu(x, approximate=True)

def _silu(x):
    return jax.nn.silu(x)

def _sigmoid(x):
    return jax.nn.sigmoid(x)

def _layernorm(x, axis=-1, eps=1e-05):
    m = jnp.mean(x, axis=axis, keepdims=True)
    v = jnp.var(x, axis=axis, keepdims=True)
    return (x - m) / jnp.sqrt(v + eps)

def _scatter_add(tgt, idx, src, axis=0):
    return tgt.at[idx].add(src)

def _segment_sum(src, seg, n):
    return jax.ops.segment_sum(src, seg, n)
kernel_name = 'mk_metaformer_d1_conv_nhwc256_r2_c9ecb4'

def setup_inputs(seed: int=0):
    np.random.seed(seed)
    _w = jnp.asarray

    def _rec_inputs():
        import jax
        import jax.numpy as jnp
        _gk = jax.random.key(seed)
        x = -0.0003929 + 0.9999 * jax.random.normal(jax.random.fold_in(_gk, 1), (16, 32, 32, 128), jnp.float32)
        return x
    x = _rec_inputs()

    def _L0_conv_setup():
        import jax, jax.numpy as jnp
        import numpy as np
        from jax import lax
        EXPAND = 32
        CHANNELS = 128

        def _conv(A, W, padding):
            return lax.conv_general_dilated(A, W, (1, 1), padding, dimension_numbers=('NHWC', 'HWIO', 'NHWC'))
        key = jax.random.key(seed)
        ks = jax.random.split(key, 7)
        x = jax.random.normal(ks[0], (16, 32, 32, 128), dtype=jnp.float32)
        s = 0.05
        w1 = jax.random.normal(ks[1], (1, 1, CHANNELS, EXPAND), dtype=jnp.float32) * s
        b1 = jax.random.normal(ks[2], (1, 1, 1, EXPAND), dtype=jnp.float32) * s
        w2 = jax.random.normal(ks[3], (3, 3, CHANNELS, EXPAND), dtype=jnp.float32) * s
        b2 = jax.random.normal(ks[4], (1, 1, 1, EXPAND), dtype=jnp.float32) * s
        w3 = jax.random.normal(ks[5], (1, 1, CHANNELS, 1), dtype=jnp.float32) * s
        b3 = jax.random.normal(ks[6], (1, 1, 1, 1), dtype=jnp.float32) * s
        return {'x': x, 'w1': w1, 'b1': b1, 'w2': w2, 'b2': b2, 'w3': w3, 'b3': b3}
    _L0_conv_all = _L0_conv_setup()
    _L0_conv_in = {k: v for k, v in _L0_conv_all.items() if k in ('w1', 'b1', 'w2', 'b2', 'w3', 'b3')}
    del _L0_conv_all

    def _L0_ffn_setup():
        import jax, jax.numpy as jnp
        import numpy as np
        B, N, D = (16, 2048, 128)
        NUM_EXPERTS, TOP_K, HEADS = (4, 2, 4)
        N_EDGES = 524288
        LN_EPS = 1e-05

        def _layernorm(x, g, b):
            mu = x.mean(-1, keepdims=True)
            var = ((x - mu) ** 2).mean(-1, keepdims=True)
            return (x - mu) * jax.lax.rsqrt(var + LN_EPS) * g + b

        def _forward(x, edge_index, W_gat, att_src, att_dst, b_gat, ln_gamma, ln_beta, W1, b1, W2, b2):
            Bc, Nc, Dc = x.shape
            M = Bc * Nc
            x_flat = x.reshape(M, Dc)
            h = (x_flat @ W_gat).reshape(M, HEADS, NUM_EXPERTS)
            loops = jnp.arange(M, dtype=edge_index.dtype)
            src = jnp.concatenate([edge_index[0], loops])
            dst = jnp.concatenate([edge_index[1], loops])
            a_src = (h * att_src).sum(-1)
            a_dst = (h * att_dst).sum(-1)
            e = jax.nn.leaky_relu(a_src[src] + a_dst[dst], negative_slope=0.2)
            e_max = jax.ops.segment_max(e, dst, num_segments=M)
            ee = jnp.exp(e - e_max[dst])
            denom = jax.ops.segment_sum(ee, dst, num_segments=M)
            alpha = ee / (denom[dst] + 1e-16)
            msg = h[src] * alpha[:, :, None]
            agg = jax.ops.segment_sum(msg, dst, num_segments=M).reshape(M, HEADS * NUM_EXPERTS) + b_gat
            scores = _layernorm(agg, ln_gamma, ln_beta).reshape(M, HEADS, NUM_EXPERTS).mean(1)
            scores = scores.reshape(Bc, Nc, NUM_EXPERTS)
            topk_s, topk_i = jax.lax.top_k(scores, TOP_K)
            w = jax.nn.softmax(topk_s, axis=-1)
            out = jnp.zeros_like(x)
            for ei in range(NUM_EXPERTS):
                g = jnp.where(topk_i == ei, w, 0.0).sum(-1)
                hh = jax.nn.gelu(x @ W1[ei] + b1[ei], approximate=False)
                out = out + g[..., None] * (hh @ W2[ei] + b2[ei])
            return out
        key = jax.random.key(seed)
        ks = jax.random.split(key, 8)
        s = 0.05
        return {'x': jax.random.normal(ks[0], (B, N, D), jnp.float32), 'W_gat': jax.random.normal(ks[1], (D, HEADS * NUM_EXPERTS), jnp.float32) * s, 'att_src': jax.random.normal(ks[2], (HEADS, NUM_EXPERTS), jnp.float32) * s, 'att_dst': jax.random.normal(ks[3], (HEADS, NUM_EXPERTS), jnp.float32) * s, 'b_gat': jnp.zeros((HEADS * NUM_EXPERTS,), jnp.float32), 'ln_gamma': jnp.ones((HEADS * NUM_EXPERTS,), jnp.float32), 'ln_beta': jnp.zeros((HEADS * NUM_EXPERTS,), jnp.float32), 'W1': jax.random.normal(ks[4], (NUM_EXPERTS, D, 2 * D), jnp.float32) * s, 'b1': jnp.zeros((NUM_EXPERTS, 2 * D), jnp.float32), 'W2': jax.random.normal(ks[5], (NUM_EXPERTS, 2 * D, D), jnp.float32) * s, 'b2': jnp.zeros((NUM_EXPERTS, D), jnp.float32), 'edge_index': jax.random.randint(ks[6], (2, N_EDGES), 0, B * N, jnp.int32)}
    _L0_ffn_all = _L0_ffn_setup()
    _L0_ffn_in = {k: v for k, v in _L0_ffn_all.items() if k in ('W_gat', 'att_src', 'att_dst', 'b_gat', 'ln_gamma', 'ln_beta', 'W1', 'b1', 'W2', 'b2', 'edge_index')}
    del _L0_ffn_all
    return {'x': x, 'L0_conv_w1': _L0_conv_in['w1'], 'L0_conv_b1': _L0_conv_in['b1'], 'L0_conv_w2': _L0_conv_in['w2'], 'L0_conv_b2': _L0_conv_in['b2'], 'L0_conv_w3': _L0_conv_in['w3'], 'L0_conv_b3': _L0_conv_in['b3'], 'L0_ffn_W_gat': _L0_ffn_in['W_gat'], 'L0_ffn_att_src': _L0_ffn_in['att_src'], 'L0_ffn_att_dst': _L0_ffn_in['att_dst'], 'L0_ffn_b_gat': _L0_ffn_in['b_gat'], 'L0_ffn_ln_gamma': _L0_ffn_in['ln_gamma'], 'L0_ffn_ln_beta': _L0_ffn_in['ln_beta'], 'L0_ffn_W1': _L0_ffn_in['W1'], 'L0_ffn_b1': _L0_ffn_in['b1'], 'L0_ffn_W2': _L0_ffn_in['W2'], 'L0_ffn_b2': _L0_ffn_in['b2'], 'L0_ffn_edge_index': _L0_ffn_in['edge_index']}

def reference(x, L0_conv_w1, L0_conv_b1, L0_conv_w2, L0_conv_b2, L0_conv_w3, L0_conv_b3, L0_ffn_W_gat, L0_ffn_att_src, L0_ffn_att_dst, L0_ffn_b_gat, L0_ffn_ln_gamma, L0_ffn_ln_beta, L0_ffn_W1, L0_ffn_b1, L0_ffn_W2, L0_ffn_b2, L0_ffn_edge_index):
    import jax
    import jax.numpy as jnp

    def _L0_conv_ref(x, w1, b1, w2, b2, w3, b3):
        import jax, jax.numpy as jnp
        import numpy as np
        from jax import lax
        EXPAND = 32
        CHANNELS = 128

        def _conv(A, W, padding):
            return lax.conv_general_dilated(A, W, (1, 1), padding, dimension_numbers=('NHWC', 'HWIO', 'NHWC'))
        depth_batch = CHANNELS // EXPAND

        def step1(A, i):
            Z = _conv(A, w1, 'VALID') + b1
            A = lax.dynamic_update_slice(A, Z, (0, 0, 0, i * EXPAND))
            return (A, None)

        def step2(A, i):
            Z = _conv(A, w2, 'SAME') + b2
            A = lax.dynamic_update_slice(A, Z, (0, 0, 0, i * EXPAND))
            return (A, None)

        def step3(A, i):
            Z = _conv(A, w3, 'VALID') + b3
            A = lax.dynamic_update_slice(A, Z, (0, 0, 0, i))
            return (A, None)
        A = x
        A, _ = lax.scan(step1, A, jnp.arange(depth_batch))
        A = jax.nn.relu(A)
        A, _ = lax.scan(step2, A, jnp.arange(depth_batch))
        A = jax.nn.relu(A)
        A, _ = lax.scan(step3, A, jnp.arange(CHANNELS))
        return A + x

    def _L0_ffn_ref(x, W_gat, att_src, att_dst, b_gat, ln_gamma, ln_beta, W1, b1, W2, b2, edge_index):
        import jax, jax.numpy as jnp
        import numpy as np
        B, N, D = (16, 2048, 128)
        NUM_EXPERTS, TOP_K, HEADS = (4, 2, 4)
        N_EDGES = 524288
        LN_EPS = 1e-05

        def _layernorm(x, g, b):
            mu = x.mean(-1, keepdims=True)
            var = ((x - mu) ** 2).mean(-1, keepdims=True)
            return (x - mu) * jax.lax.rsqrt(var + LN_EPS) * g + b

        def _forward(x, edge_index, W_gat, att_src, att_dst, b_gat, ln_gamma, ln_beta, W1, b1, W2, b2):
            Bc, Nc, Dc = x.shape
            M = Bc * Nc
            x_flat = x.reshape(M, Dc)
            h = (x_flat @ W_gat).reshape(M, HEADS, NUM_EXPERTS)
            loops = jnp.arange(M, dtype=edge_index.dtype)
            src = jnp.concatenate([edge_index[0], loops])
            dst = jnp.concatenate([edge_index[1], loops])
            a_src = (h * att_src).sum(-1)
            a_dst = (h * att_dst).sum(-1)
            e = jax.nn.leaky_relu(a_src[src] + a_dst[dst], negative_slope=0.2)
            e_max = jax.ops.segment_max(e, dst, num_segments=M)
            ee = jnp.exp(e - e_max[dst])
            denom = jax.ops.segment_sum(ee, dst, num_segments=M)
            alpha = ee / (denom[dst] + 1e-16)
            msg = h[src] * alpha[:, :, None]
            agg = jax.ops.segment_sum(msg, dst, num_segments=M).reshape(M, HEADS * NUM_EXPERTS) + b_gat
            scores = _layernorm(agg, ln_gamma, ln_beta).reshape(M, HEADS, NUM_EXPERTS).mean(1)
            scores = scores.reshape(Bc, Nc, NUM_EXPERTS)
            topk_s, topk_i = jax.lax.top_k(scores, TOP_K)
            w = jax.nn.softmax(topk_s, axis=-1)
            out = jnp.zeros_like(x)
            for ei in range(NUM_EXPERTS):
                g = jnp.where(topk_i == ei, w, 0.0).sum(-1)
                hh = jax.nn.gelu(x @ W1[ei] + b1[ei], approximate=False)
                out = out + g[..., None] * (hh @ W2[ei] + b2[ei])
            return out
        return _forward(x, edge_index, W_gat, att_src, att_dst, b_gat, ln_gamma, ln_beta, W1, b1, W2, b2)

    def _gn(v, G=32, eps=1e-05):
        B_, H_, W_, C_ = v.shape
        g = v.reshape(B_, H_, W_, G, C_ // G)
        m = jnp.mean(g, axis=(1, 2, 4), keepdims=True)
        s = jnp.var(g, axis=(1, 2, 4), keepdims=True)
        return ((g - m) / jnp.sqrt(s + eps)).reshape(v.shape)

    def _ln_c(v, eps=1e-06):
        m = jnp.mean(v, axis=-1, keepdims=True)
        s = jnp.var(v, axis=-1, keepdims=True)
        return (v - m) / jnp.sqrt(s + eps)

    def _ln_t(v, eps=1e-05):
        m = jnp.mean(v, axis=-1, keepdims=True)
        s = jnp.var(v, axis=-1, keepdims=True)
        return (v - m) / jnp.sqrt(s + eps)

    def _to_tokens(v):
        B_, H_, W_, C_ = v.shape
        return v.reshape(B_, H_ * W_, C_)

    def _from_tokens(t, like):
        return t.reshape(like.shape)
    x = x + _L0_conv_ref(_ln_c(x), L0_conv_w1, L0_conv_b1, L0_conv_w2, L0_conv_b2, L0_conv_w3, L0_conv_b3)
    t = _to_tokens(x)
    t = t + _L0_ffn_ref(_ln_t(t), L0_ffn_W_gat, L0_ffn_att_src, L0_ffn_att_dst, L0_ffn_b_gat, L0_ffn_ln_gamma, L0_ffn_ln_beta, L0_ffn_W1, L0_ffn_b1, L0_ffn_W2, L0_ffn_b2, L0_ffn_edge_index)
    x = _from_tokens(t, x)
    return x

_drawn_inputs = setup_inputs


def setup_inputs(seed=0):
    import zlib

    import numpy as np

    out = dict(_drawn_inputs(seed))
    spreads = {'L0_ffn_b_gat': (0.0, 0.1),
     'L0_ffn_ln_gamma': (1.0, 0.2),
     'L0_ffn_ln_beta': (0.0, 0.309),
     'L0_ffn_b1': (0.0, 0.471),
     'L0_ffn_b2': (0.0, 0.1)}
    factors = {'L0_conv_b2': 4.194, 'L0_ffn_att_src': 5.257, 'L0_ffn_att_dst': 7.69}
    for name, (base, spread) in spreads.items():
        noise = np.random.default_rng([zlib.crc32(name.encode()), seed]).standard_normal(out[name].shape)
        drawn = base * np.exp(spread * noise) if base else spread * noise
        out[name] = jnp.asarray(drawn.astype(out[name].dtype))
    for name, factor in factors.items():
        out[name] = (out[name] * factor).astype(out[name].dtype)
    return out
```

```python
from contextlib import ExitStack

import concourse.bass as bass
from concourse import mybir

F32, I32, BF16 = mybir.dt.float32, mybir.dt.int32, mybir.dt.bfloat16
ALU, ACT, AX = mybir.AluOpType, mybir.ActivationFunctionType, mybir.AxisListType

P = 128
N_IMG, IMG_H, IMG_W, C = 16, 32, 32, 128
M = N_IMG * IMG_H * IMG_W
E = 524288
HEADS, EXPERTS = 4, 4
HE = HEADS * EXPERTS
HID = 2 * C

GROUPS, IMGS = 4, 4
TILES = IMGS * IMG_H * IMG_W // P
CHUNK = 512
CHUNKS = TILES * P // CHUNK
TPC = CHUNK // P
PADH, PADW = IMG_H + 2, IMG_W + 2
QUAD = 32
TAPS = [(dy, dx) for dy in range(3) for dx in range(3)]
FFN_CHUNKS = M // CHUNK

ROW = E // P
SRC_BITS = 14
KEY_BIAS = 512
REAL_END, VALID_END = M, 2 * M
BLOCKS = ROW // P
LEVELS = 7
BANK_T = 4
EVACS = BLOCKS // BANK_T
STRIDE = 64
PIVOTS = ROW // STRIDE
WIN_COLS = 64
WIN_BATCHES = 2 * P // WIN_COLS

WIDTH = HEADS + HE
COLS = 16
SLOTS = 24
NODES = 4
STEPS = P // (2 * NODES)
NEG = -1e30
ROUND_MAGIC = 12582912.0


def key_bits_as_float(j):
    import numpy as np
    return float(np.array((j + KEY_BIAS) << SRC_BITS, np.int32).view(np.float32))


def program(nc, x, w1, b1, w2, b2, w3, b3, w_gat, att_src, att_dst, b_gat, ln_gamma, ln_beta,
            ffn_w1, ffn_b1, ffn_w2, ffn_b2, edge_index, out):
    ctx = ExitStack()
    with ctx:
        def sb(name, shape, dt=F32):
            return ctx.enter_context(nc.sbuf_tensor(name, shape, dt))

        def ps(name, shape, dt=F32):
            return ctx.enter_context(nc.psum_tensor(name, shape, dt))

        def sem(name):
            return ctx.enter_context(nc.semaphore(name))

        def bc(ap, axis, shape):
            return ap.unsqueeze(axis).to_broadcast(shape)

        x1_dram = nc.dram_tensor("x1_dram", [M, C], F32).ap()
        expert_dram = nc.dram_tensor("expert_dram", [M, EXPERTS * C], F32).ap()
        node_dram = nc.dram_tensor("node_dram", [M, WIDTH], F32).ap()
        adst_dram = nc.dram_tensor("adst_dram", [M, HEADS], F32).ap()
        keys_dram = nc.dram_tensor("keys_dram", [E], F32).ap()
        payload = nc.dram_tensor("payload", [E + SLOTS, WIDTH], F32).ap()

        KA, KB, KC = sb("KA", [P, ROW]), sb("KB", [P, ROW]), sb("KC", [P, ROW])
        XT = sb("XT", [P, M])
        XG = sb("XG", [P, TILES * C])
        ARENA_A = sb("ARENA_A", [P, IMGS * PADH * PADW])
        ARENA_D = sb("ARENA_D", [P, IMGS * PADH * PADW])
        ARENA_Y = sb("ARENA_Y", [P, 4 * CHUNK])
        x_tiles = XG[:, :].rearrange("p (t c) -> p t c", c=C)
        A1 = ARENA_A[:, :].rearrange("p (i a b) -> p i a b", i=IMGS, b=PADW)
        DZ = ARENA_D[:, :].rearrange("p (i a b) -> p i a b", i=IMGS, b=PADW)
        Y = [ARENA_Y[:, i * CHUNK:(i + 1) * CHUNK].rearrange("p (t c) -> p t c", c=C) for i in range(2)]
        YT = [ARENA_Y[:, (2 + i) * CHUNK:(3 + i) * CHUNK] for i in range(2)]
        HH = ARENA_A[:, 0:8 * CHUNK].rearrange("p (m n) -> p m n", n=CHUNK)
        YE = ARENA_D[:, 0:TPC * CHUNK].rearrange("p (t n) -> p t n", n=CHUNK)
        zeros = XT[:, (GROUPS - 1) * TILES * P:(GROUPS - 1) * TILES * P + P * WIDTH]
        node_rows = XG[:, 0:P * WIDTH].rearrange("p (l f) -> p l f", f=WIDTH)

        def node4(arena, at):
            return arena[:, at:at + P * HEADS].rearrange("p (l g) -> p l g", g=HEADS)

        a_dst, run_max, denom = (node4(XG, P * WIDTH + i * P * HEADS) for i in range(3))
        agg = ARENA_D[:, TPC * CHUNK:TPC * CHUNK + P * HE].rearrange("p (l f) -> p l f", f=HE)
        tmp_a = node4(ARENA_D, TPC * CHUNK + P * HE)
        tmp16 = ARENA_Y[:, 0:P * HE].rearrange("p (l f) -> p l f", f=HE)
        tmp_b = node4(ARENA_A, 8 * CHUNK)
        slot_rows = [KA[:, h * 2048:h * 2048 + NODES * SLOTS * WIDTH] for h in range(2)]
        msg = KC[:, 0:NODES * SLOTS * HE].rearrange("p (c k f) -> p c k f", c=NODES, f=HE)
        EB_W = NODES * SLOTS * HEADS + NODES * HEADS
        e_buf = [KC[:, 1536 + h * 512:1536 + h * 512 + EB_W] for h in range(2)]
        slot_mask = [KC[:, 2560 + h * 128:2560 + h * 128 + NODES * SLOTS].rearrange("p (c k) -> p c k", c=NODES)
                     for h in range(2)]
        step_max = [KC[:, 2816 + h * 16:2832 + h * 16].rearrange("p (c g) -> p c g", g=HEADS) for h in range(2)]
        step_sum = KC[:, 2848:2864].rearrange("p (c g) -> p c g", g=HEADS)
        step_agg = KC[:, 2880:2880 + NODES * HE].rearrange("p (c f) -> p c f", f=HE)
        tail_y = [KA[:, i * 2048:(i + 1) * 2048].rearrange("p (t n) -> p t n", n=CHUNK) for i in range(2)]
        tail_x = [KC[:, i * CHUNK:(i + 1) * CHUNK].rearrange("p (t c) -> p t c", c=C) for i in range(2)]
        windows = [k[:, :].rearrange("p (c w) -> p c w", w=STRIDE) for k in (KA, KC)]

        ident, ones = sb("ident", [P, P]), sb("ones", [P, P])
        before = sb("before", [P, P])
        signs, part_i = sb("signs", [P, 9]), sb("part_i", [P, 1], I32)
        sign_bits = sb("sign_bits", [P, 8], I32)
        cw1, cw1_blocks = sb("cw1", [P, QUAD]), sb("cw1_blocks", [QUAD, 4, QUAD])
        comp, comp_d = (KC[0:QUAD, i * 1024:i * 1024 + 4 * (P + 4)].rearrange("p (i n) -> p i n", i=4) for i in range(2))
        w3_row, rec_a, rec_b = (KC[:, 2048 + i * P:2048 + (i + 1) * P] for i in range(3))
        E1, e1_bias = sb("E1", [P, P]), sb("e1_bias", [P, 1])
        cw2, cb2 = sb("cw2", [P, 9, QUAD]), sb("cb2", [P, 1])
        w3_col, b3_in = sb("w3_col", [P, 1]), sb("b3_in", [1, P])
        T3, b3_row = sb("T3", [P, P]), sb("b3_row", [1, P])
        node_w = sb("node_w", [P, 2 * HEADS + HE])
        att, att_w = sb("att", [P, 2, HE]), sb("att_w", [P, 2, HE])
        W1, b1c = sb("W1", [P, EXPERTS, HID]), sb("b1c", [P, 8])
        W2, b2r = sb("W2", [P, 8, C]), sb("b2r", [1, EXPERTS * C])
        bn, mean_var = sb("bn", [P, TILES, 6]), sb("mean_var", [P, TILES, 2])
        rstd, rstd1, shift, std = (sb(n, [P, TILES]) for n in ("rstd", "rstd1", "shift", "std"))
        node_out = sb("node_out", [P, TILES, 2 * HEADS + HE])
        key_counts, key_totals = sb("key_counts", [P, 2]), sb("key_totals", [P, 2])
        counts_f, counts_i = sb("counts_f", [1, 4]), sb("counts_i", [1, 4], I32)
        iota_i, iota_f = sb("iota_i", [P, 2 * P], I32), sb("iota_f", [P, 2 * P])
        piv_i, piv_f = sb("piv_i", [P, 3, PIVOTS], I32), sb("piv_f", [P, 2, PIVOTS])
        hot_hi, hot_lo = sb("hot_hi", [P, 2, 2 * P], BF16), sb("hot_lo", [P, 2, P], BF16)
        hist = sb("hist", [P, 2, P])
        cum = KC[:, 2048:2048 + 2 * P].rearrange("p (g l) -> p g l", l=P)
        hist_tot, hist_off = sb("hist_tot", [P, 2]), sb("hist_off", [P, 2])
        win_i, win_f, thresholds = sb("win_i", [P, 2 * P], I32), sb("win_f", [P, 2 * P]), sb("thresholds", [P, 2 * P])
        starts, degree, max_deg = sb("starts", [P, 2, P + 1]), sb("degree", [P, 2, P]), sb("max_deg", [P, 1])
        src_buf = [sb(f"src_buf{h}", [P, COLS], I32) for h in range(2)]
        row_buf = [KC[:, h * COLS * WIDTH:(h + 1) * COLS * WIDTH].rearrange("p (t f) -> p t f", f=WIDTH) for h in range(2)]
        last_row = sb("last_row", [P, WIDTH])
        slot_iota = sb("slot_iota", [P, SLOTS])
        slot_at, slot_end, slot_left = (sb(n, [P, P]) for n in ("slot_at", "slot_end", "slot_left"))
        slot_i = sb("slot_i", [P, P + 2 * NODES], I32)
        slot_idx = [sb(f"slot_idx{h}", [P, NODES], I32) for h in range(2)]
        gat_par = sb("gat_par", [P, 3, HE])
        rank = KC[:, 1536:2048].rearrange("p (x l) -> p x l", x=EXPERTS)
        beat, node1, node2 = sb("beat", [P, P]), sb("node1", [P, P]), sb("node2", [P, P])
        gate = node4(KC, 2048)
        gate_t = KC[:, 1024:1536].rearrange("p (x l) -> p x l", x=EXPERTS)

        TA = [ps(f"TA{i}", [P, CHUNK]) for i in range(2)]
        MB = [ps(f"MB{i}", [P, CHUNK]) for i in range(2)]
        Z = ps("Z", [P, 2, CHUNK])
        PF = [ps(f"PF{i}", [P, CHUNK]) for i in range(2)]
        H = MB[0][:, 0:2 * P].rearrange("p (g l) -> p g l", l=P)
        PO = MB[1]

        names = """weights_in consts edges_in x_in comp_pe comp_dve
            var_ready std_ready norm_ready y_ready xres_ready yt_ready yt_out step1_ready a1_out
            conv_stage dz_out relu_out step3_ready x1_ready node_ready node_out_done node_stored x1_stored
            zeros_stored hid_ready hid_out exp_ready exp_out exp_stored
            dve_chain counted counts_ready totals_ready
            swap_ready swapped rows_sorted keys_transposed keys_evacuated keys_stored sources_ready
            hot_ready hist_done hist_tot_ready offsets_ready win_idx_ready windows_counted starts_ready
            boundary_in max_deg_ready max_deg_t rounds_ready
            gpsimd_turns nodes_in init_args init_exps round_chain slot_chain
            score_var score_std logits_ready logits_exp gate_ready gate_tr tail_done""".split()
        S = {n: sem(n) for n in names}
        src_copied, rows_gathered, rows_stored, slot_idx_ready, slots_gathered, slots_used, e_ready, e_exp, tail_in, tail_out = (
            [sem(f"{n}{h}") for h in range(2)]
            for n in ("src_copied", "rows_gathered", "rows_stored", "slot_idx_ready", "slots_gathered",
                      "slots_used", "e_ready", "e_exp", "tail_in", "tail_out"))
        win_in = [sem(f"win_in{i}") for i in range(WIN_BATCHES)]
        block = ctx.enter_context(nc.Block())

        x_groups = x.rearrange("b h w c -> (b h w) c").rearrange("(g t p) c -> g p t c", t=TILES, p=P)
        x1_groups = x1_dram.rearrange("(g t p) c -> g p t c", t=TILES, p=P)
        x1_chunks = x1_dram.rearrange("(s t p) c -> s p t c", t=TPC, p=P)
        out_chunks = out.rearrange("b h w c -> (b h w) c").rearrange("(s t p) c -> s p t c", t=TPC, p=P)
        exp_chunks = expert_dram.rearrange("(s t p) c -> s p t c", t=TPC, p=P)
        node_groups = node_dram.rearrange("(g t p) c -> g p t c", t=TILES, p=P)
        adst_groups = adst_dram.rearrange("(g t p) c -> g p t c", t=TILES, p=P)
        payload_cols = payload[0:E].rearrange("(c t q) f -> c q t f", t=COLS, q=P)
        key_windows = keys_dram.rearrange("(r w) -> r w", w=STRIDE)
        keys_t = KB[:, :].rearrange("q (p j) -> q j p", j=BLOCKS)
        by_head = lambda ap: ap.rearrange("p l (g x) -> p l g x", g=HEADS)
        N_WEIGHTS = 24
        NORMS = GROUPS * 2 * CHUNKS

        def gather_trips(eng):
            eng.wait_ge(S["counts_ready"], 1)
            return eng.value_load(counts_i[0:1, 0:1], min_val=1, max_val=ROW // (2 * COLS))

        def slot_rounds(eng):
            eng.wait_ge(S["rounds_ready"], 1)
            return eng.value_load(counts_i[0:1, 1:2], min_val=1, max_val=-(-E // SLOTS))

        @block.sync
        def _(sp):
            sp.dma_start(x_tiles, x_groups[0]).then_inc(S["x_in"], 16)
            edge_rows = edge_index.rearrange("a (p f) -> a p f", p=P)
            sp.dma_start(KA[:, :].bitcast(I32), edge_rows[0]).then_inc(S["edges_in"], 16)
            sp.dma_start(KB[:, :].bitcast(I32), edge_rows[1]).then_inc(S["edges_in"], 16)
            loads = [
                (cw1[:, :], w1.rearrange("a b c n -> (a b c) n")),
                (cw1_blocks[:, :, :], w1.rearrange("a b (j k) n -> k (a b j) n", k=QUAD)),
                (comp[:, 0, P:P + 1], b1.rearrange("a b c n -> n (a b c)")),
                (cw2[:, :, :], w2.rearrange("a b c n -> c (a b) n")),
            ] + [(cb2[QUAD * q:QUAD * (q + 1), :], b2.rearrange("a b c n -> n (a b c)")) for q in range(4)] + [
                (w3_row, w3.rearrange("a b c n -> (a b n) c").to_broadcast([P, P])),
                (w3_col[:, :], w3.rearrange("a b c n -> c (a b n)")),
                (b3_in[0:1, 0:1], b3.rearrange("a b c n -> (a b c) n")),
                (node_w[:, HEADS:HEADS + HE], w_gat),
                (att[:, 0, :], att_src.rearrange("a b -> (a b)").unsqueeze(0).to_broadcast([P, HE])),
                (att[:, 1, :], att_dst.rearrange("a b -> (a b)").unsqueeze(0).to_broadcast([P, HE])),
                (W1[:, :, :], ffn_w1.rearrange("e k n -> k e n")),
                (b1c[:, :], ffn_b1.rearrange("e (m p) -> p (e m)", p=P)),
                (W2[:, 0:4, :], ffn_w2[0:2].rearrange("e (k p) n -> p (e k) n", p=P)),
                (W2[:, 4:8, :], ffn_w2[2:4].rearrange("e (k p) n -> p (e k) n", p=P)),
                (b2r[:, 0:2 * C], ffn_b2[0:2].rearrange("e n -> (e n)").unsqueeze(0)),
                (b2r[:, 2 * C:], ffn_b2[2:4].rearrange("e n -> (e n)").unsqueeze(0)),
            ] + [(gat_par[:, i, :], a.unsqueeze(0).to_broadcast([P, HE]))
                 for i, a in enumerate((b_gat, ln_gamma, ln_beta))]
            for dst, src in loads:
                sp.dma_start(dst, src, allow_slow_non_contiguous=True).then_inc(S["weights_in"], 16)
            assert len(loads) == N_WEIGHTS - 1
            sp.wait_ge(S["consts"], 1)
            sp.dma_start(payload[0:E].rearrange("(a p b) f -> p a (b f)", p=P, b=P),
                         bc(zeros, 1, [P, E // (P * P), P * WIDTH])).then_inc(S["zeros_stored"], 16)
            sp.dma_start(payload[E:E + SLOTS], zeros[0:SLOTS, 0:WIDTH]).then_inc(S["zeros_stored"], 16)
            for g in range(GROUPS):
                sp.wait_ge(S["x1_ready"], CHUNKS * (g + 1))
                sp.dma_start(x1_groups[g], x_tiles).then_inc(S["x1_stored"], 16)
                sp.wait_ge(S["node_out_done"], CHUNKS * (g + 1))
                sp.dma_start(node_groups[g], node_out[:, :, 0:WIDTH]).then_inc(S["node_stored"], 16)
                sp.dma_start(adst_groups[g], node_out[:, :, WIDTH:]).then_inc(S["node_stored"], 16)
                sp.wait_ge(S["x1_stored"], 16 * (g + 1))
                sp.wait_ge(S["y_ready"], 2 * CHUNKS * (g + 1))
                if g + 1 < GROUPS:
                    sp.dma_start(x_tiles, x_groups[g + 1]).then_inc(S["x_in"], 16)
            sp.wait_ge(S["node_stored"], 32 * GROUPS)
            sp.dma_start(node_rows, node_dram.rearrange("(p l) f -> p l f", l=P)).then_inc(S["nodes_in"], 16)
            sp.dma_start(a_dst, adst_dram.rearrange("(p l) f -> p l f", l=P)).then_inc(S["nodes_in"], 16)
            sp.dma_start(last_row[:, :], node_dram[M - 1:M, :].to_broadcast([P, WIDTH])).then_inc(S["nodes_in"], 16)
            sp.wait_ge(S["rows_sorted"], 1)
            sp.dma_start(keys_dram.rearrange("(p f) -> p f", p=P), KA[:, :]).then_inc(S["keys_stored"], 16)
            trips = gather_trips(sp)
            sp.wait_ge(S["zeros_stored"], 32)
            for h in range(2):
                sp.sem_inc(rows_stored[h], 16)
            with sp.Fori(0, trips) as i:
                for h in range(2):
                    sp.wait_ge(rows_gathered[h], (i + 1) * (16 * COLS))
                    sp.dma_start(payload_cols[i * 2 + h], row_buf[h][:, :, :]).then_inc(rows_stored[h], 16)
            sp.wait_ge(S["starts_ready"], 1)
            sp.dma_start(starts[0:P - 1, :, P:P + 1], starts[1:P, :, 0:1],
                         allow_slow_non_contiguous=True).then_inc(S["boundary_in"], 16)
            sp.dma_start(starts[P - 1:P, 0, P:P + 1], starts[0:1, 1, 0:1]).then_inc(S["boundary_in"], 16)
            sp.dma_start(starts[P - 1:P, 1, P:P + 1], key_totals[P - 1:P, 1:2]).then_inc(S["boundary_in"], 16)
            sp.wait_ge(S["gate_ready"], 1)
            sp.wait_ge(S["exp_stored"], 16 + 16 * FFN_CHUNKS)
            for s in range(FFN_CHUNKS):
                if s >= 2:
                    sp.wait_ge(S["tail_done"], s - 1)
                    sp.wait_ge(tail_out[s % 2], 16 * (s // 2))
                sp.dma_start(tail_y[s % 2], exp_chunks[s]).then_inc(tail_in[s % 2], 16)
                sp.dma_start(tail_x[s % 2], x1_chunks[s]).then_inc(tail_in[s % 2], 16)

        @block.gpsimd
        def _(pool):
            pool.memset(zeros, 0.0).then_inc(S["consts"], 1)
            pool.memset(ident[:, :], 0.0).then_inc(S["consts"], 1)
            pool.memset(before[:, :], 1.0).then_inc(S["consts"], 1)
            pool.wait_ge(S["consts"], 3)
            pool.affine_select(out=ident[:, :], in_=ident[:, :], compare_op=ALU.not_equal, fill=1.0,
                               base=0, pattern=[[-1, P]], channel_multiplier=1).then_inc(S["consts"], 1)
            pool.affine_select(out=before[:, :], in_=before[:, :], compare_op=ALU.is_gt, fill=0.0,
                               base=0, pattern=[[1, P]], channel_multiplier=-1).then_inc(S["consts"], 1)
            pool.memset(ones[:, :], 1.0).then_inc(S["consts"], 1)
            pool.iota(part_i[:, :], [[0, 1]], 0, 1).then_inc(S["consts"], 1)
            pool.iota(iota_i[:, :], [[1, 2 * P]], 0, 0).then_inc(S["consts"], 1)
            pool.iota(win_i[:, :], [[M, 2], [1, P]], KEY_BIAS, P).then_inc(S["consts"], 1)
            pool.memset(ARENA_A[:, :], 0.0).then_inc(S["consts"], 1)
            pool.memset(ARENA_D[:, :], 0.0).then_inc(S["consts"], 1)

            for n, dist in enumerate((1, 2, 1)):
                pool.wait_ge(S["swap_ready"], n + 1)
                for q in range(4):
                    a, b = QUAD * q, QUAD * (q ^ dist)
                    pool.dma_start(KB[a:a + QUAD, :], KA[b:b + QUAD, :]).then_inc(S["swapped"], 16)

            def settled(eng):
                eng.sem_inc(S["gpsimd_turns"], 1)

            trips = gather_trips(pool)
            pool.wait_ge(S["sources_ready"], 1)
            pool.wait_ge(S["node_stored"], 32 * GROUPS)
            with pool.Fori(0, trips) as i:
                for h in range(2):
                    pool.wait_ge(rows_stored[h], 16 + i * 16)
                    settled(pool)
                    pool.tensor_copy(src_buf[h][:, :], KB[:, bass.ds(i * (2 * COLS) + h * COLS, COLS)].bitcast(I32)
                                     ).then_inc(src_copied[h], 1)
                    pool.wait_ge(src_copied[h], i + 1)
                    settled(pool)
                    for t in range(COLS):
                        pool.indirect_dma_start(
                            row_buf[h][:, t, :], None, node_dram,
                            bass.IndirectOffsetOnAxis(ap=src_buf[h][:, t:t + 1], axis=0)).then_inc(rows_gathered[h], 16)

            pool.wait_ge(S["win_idx_ready"], 1)
            pool.wait_ge(S["keys_stored"], 16)
            for h in range(2):
                pool.wait_ge(rows_stored[h], 16 + trips * 16)
            settled(pool)
            for b in range(WIN_BATCHES):
                if b >= 2:
                    pool.wait_ge(S["windows_counted"], b - 1)
                for k in range(WIN_COLS):
                    col = b * WIN_COLS + k
                    pool.indirect_dma_start(
                        windows[b % 2][:, k, :], None, key_windows,
                        bass.IndirectOffsetOnAxis(ap=win_i[:, col:col + 1], axis=0)).then_inc(win_in[b], 16)

            rounds = slot_rounds(pool)
            with pool.Fori(0, rounds) as r:
                with pool.Fori(0, STEPS) as i:
                    for h in range(2):
                        pool.wait_ge(slot_idx_ready[h], r * (STEPS + 1) + i + 1)
                        pool.wait_ge(slots_used[h], r * STEPS + i + 1)
                        settled(pool)
                        for t in range(NODES):
                            w = SLOTS * WIDTH
                            pool.indirect_dma_start(
                                slot_rows[h][:, t * w:(t + 1) * w], None, payload,
                                bass.IndirectOffsetOnAxis(ap=slot_idx[h][:, t:t + 1], axis=0)
                            ).then_inc(slots_gathered[h], 16)

            for s in range(FFN_CHUNKS):
                pool.wait_ge(S["tail_done"], s + 1)
                pool.dma_start(out_chunks[s], tail_x[s % 2]).then_inc(tail_out[s % 2], 16)
            for h in range(2):
                pool.wait_ge(tail_out[h], 16 * (FFN_CHUNKS // 2))

        @block.tensor
        def _(pe):
            pe.wait_ge(S["consts"], 11)
            pe.wait_ge(S["weights_in"], 16 * (N_WEIGHTS - 1))
            pe.transpose(TA[0][0:QUAD, 0:P], cw1[:, :], ident[:, :]).then_inc(S["comp_pe"], 1)
            for i in range(3):
                pe.wait_ge(S["comp_dve"], 2 + 2 * i)
                pe.matmul(TA[1][0:QUAD, 0:P + 1], cw1_blocks[:, i, :], comp_d[:, i, 0:P + 1],
                          start=True, stop=True).then_inc(S["comp_pe"], 1)
            pe.wait_ge(S["comp_dve"], 7)
            for i in range(4):
                last = pe.transpose(MB[0][:, QUAD * i:QUAD * (i + 1)], comp[:, i, 0:P], ident[0:QUAD, 0:QUAD])
            last.then_inc(S["comp_pe"], 1)
            pe.wait_ge(S["comp_dve"], 8)

            def norm_step1(g):
                for k in range(CHUNKS + 1):
                    n, j = g * 2 * CHUNKS + k, g * CHUNKS + k - 1
                    if k < CHUNKS:
                        transpose_chunk(n)
                    if k >= 1:
                        pe.wait_ge(S["yt_out"], n)
                        if k >= 3:
                            pe.wait_ge(S["a1_out"], j - 1)
                        elif g:
                            pe.wait_ge(S["node_out_done"], g * CHUNKS)
                        pe.matmul(MB[j % 2][:, :], E1[:, :], YT[(n - 1) % 2], start=True, stop=True
                                  ).then_inc(S["step1_ready"], 1)

            def norm_nodes(g):
                for k in range(CHUNKS + 1):
                    n, j = g * 2 * CHUNKS + CHUNKS + k, g * CHUNKS + k - 1
                    if k < CHUNKS:
                        transpose_chunk(n)
                    if k >= 1:
                        pe.wait_ge(S["yt_out"], n)
                        if k >= 3:
                            pe.wait_ge(S["node_out_done"], j - 1)
                        else:
                            pe.wait_ge(S["x1_ready"], (g + 1) * CHUNKS)
                        for t in range(TPC):
                            tok = (j * TPC + t) * P
                            last = pe.matmul(MB[j % 2][:, t * P:t * P + 2 * HEADS + HE], XT[:, tok:tok + P],
                                             node_w[:, :], start=True, stop=True)
                        last.then_inc(S["node_ready"], 1)

            def transpose_chunk(n):
                pe.wait_ge(S["y_ready"], n + 1)
                if n >= 2:
                    pe.wait_ge(S["yt_out"], n - 1)
                for t in range(TPC):
                    last = pe.transpose(TA[n % 2][:, t * P:(t + 1) * P], Y[n % 2][:, t, :], ident[:, :])
                last.then_inc(S["yt_ready"], 1)

            def convolution(g):
                pe.wait_ge(S["a1_out"], CHUNKS * (g + 1))
                for i in range(4):
                    if i:
                        pe.wait_ge(S["dz_out"], g * 12 + 4 * i)
                        pe.wait_ge(S["relu_out"], g * 16 + 4 * i)
                    elif g:
                        pe.wait_ge(S["relu_out"], g * 16)
                    for half in range(2):
                        for t, (dy, dx) in enumerate(TAPS):
                            y0 = half * (IMG_H // 2) + dy
                            for q in range(IMGS):
                                if i == 0:
                                    last = pe.matmul(Z[QUAD * q:QUAD * (q + 1), half, :], cw2[:, t, :],
                                                     A1[:, q, y0:y0 + IMG_H // 2, dx:dx + IMG_W],
                                                     start=t == 0, stop=True, skip_group_check=True)
                                else:
                                    k0 = QUAD * (i - 1)
                                    last = pe.matmul(Z[QUAD * q:QUAD * (q + 1), half, :], cw2[k0:k0 + QUAD, t, :],
                                                     DZ[k0:k0 + QUAD, q, y0:y0 + IMG_H // 2, dx:dx + IMG_W],
                                                     start=False, stop=True, skip_group_check=True)
                    last.then_inc(S["conv_stage"], 1)

            def step3(g):
                pe.wait_ge(S["relu_out"], g * 16 + 16)
                for c in range(CHUNKS):
                    j = g * CHUNKS + c
                    if c >= 2:
                        pe.wait_ge(S["x1_ready"], j - 1)
                    for t in range(TPC):
                        tok = (j * TPC + t) * P
                        pe.matmul(MB[j % 2][:, t * P:(t + 1) * P], XT[:, tok:tok + P], T3[:, :],
                                  start=True, stop=False, skip_group_check=True)
                        last = pe.matmul(MB[j % 2][:, t * P:(t + 1) * P], ones[0:1, :], b3_row[:, :],
                                         start=False, stop=True, skip_group_check=True)
                    last.then_inc(S["step3_ready"], 1)

            for g in range(GROUPS):
                norm_step1(g)
                convolution(g)
                step3(g)
                norm_nodes(g)
                if g == 0:
                    pe.wait_ge(S["counted"], 1)
                    pe.wait_ge(S["node_out_done"], CHUNKS)
                    pe.matmul(MB[0][:, 0:2], ones[:, :], key_counts[:, :], start=True, stop=True
                              ).then_inc(S["totals_ready"], 1)

            def experts(n):
                for m in range(8):
                    pe.wait_ge(S["hid_out"], n * 8 + m + 1)
                    pe.matmul(PF[m % 2][:, :], W1[:, m // 2, (m % 2) * P:(m % 2) * P + P],
                              XT[:, bass.ds(n * CHUNK, CHUNK)], start=True, stop=True).then_inc(S["hid_ready"], 1)
                pe.wait_ge(S["hid_out"], n * 8 + 10)
                for t in range(TPC):
                    pe.wait_ge(S["exp_out"], n * TPC + t + 1)
                    pe.matmul(Z[:, t % 2, :], ones[0:1, :], b2r[:, :], start=True, stop=False, skip_group_check=True)
                    for x_ in range(EXPERTS):
                        for kk in range(2):
                            last = pe.matmul(Z[:, t % 2, x_ * C:(x_ + 1) * C], HH[:, 2 * x_ + kk, t * P:(t + 1) * P],
                                             W2[:, 2 * x_ + kk, :], start=False, stop=True, skip_group_check=True)
                    last.then_inc(S["exp_ready"], 1)

            pe.wait_ge(S["yt_out"], NORMS)
            pe.wait_ge(S["rows_sorted"], 1)
            for n in range(EVACS):
                if n >= 2:
                    pe.wait_ge(S["keys_evacuated"], n - 1)
                for q in range(BANK_T):
                    j = BANK_T * n + q
                    last = pe.transpose(TA[n % 2][:, q * P:(q + 1) * P], KA[:, j * P:(j + 1) * P], ident[:, :])
                last.then_inc(S["keys_transposed"], 1)

            for t in range(PIVOTS):
                pe.wait_ge(S["hot_ready"], t + 1)
                for g in range(2):
                    last = pe.matmul(H[:, g, :], hot_hi[:, t % 2, g * P:(g + 1) * P], hot_lo[:, t % 2, :],
                                     start=t == 0 and g == 0, stop=t == PIVOTS - 1, skip_group_check=True)
                last.then_inc(S["hist_done"], 1)
            pe.wait_ge(S["hist_tot_ready"], 1)
            pe.matmul(PO[:, 0:2], before[:, :], hist_tot[:, :], start=True, stop=False, skip_group_check=True)
            pe.matmul(PO[:, 1:2], ones[:, :], hist_tot[:, 0:1], start=False, stop=True, skip_group_check=True
                      ).then_inc(S["offsets_ready"], 1)

            with pe.Fori(0, FFN_CHUNKS) as n:
                experts(n)

            pe.wait_ge(S["max_deg_ready"], 1)
            pe.transpose(PO[0:1, 0:P], max_deg[:, 0:1], ident[:, :]).then_inc(S["max_deg_t"], 1)
            pe.wait_ge(S["gate_ready"], 1)
            for x_ in range(EXPERTS):
                last = pe.transpose(TA[0][:, x_ * P:(x_ + 1) * P], gate[:, :, x_], ident[:, :])
            last.then_inc(S["gate_tr"], 1)

        @block.scalar
        def _(act):
            act.wait_ge(S["consts"], 11)

            def norm_chunk(n, k):
                if n >= 2:
                    act.wait_ge(S["yt_ready"], n - 1)
                for t in range(TPC):
                    tt = TPC * k + t
                    last = act.activation(Y[n % 2][:, t, :], x_tiles[:, tt, :], ACT.Identity,
                                          scale=rstd[:, tt:tt + 1], bias=shift[:, tt:tt + 1])
                last.then_inc(S["y_ready"], 1)

            def norm_step1(g):
                act.wait_ge(S["norm_ready"], 2 * g + 1)
                for k in range(CHUNKS + 2):
                    n = g * 2 * CHUNKS + k
                    if k < CHUNKS:
                        norm_chunk(n, k)
                        for t in range(TPC):
                            tt = TPC * k + t
                            last = act.activation(x_tiles[:, tt, :], x_tiles[:, tt, :], ACT.Identity,
                                                  scale=rstd1[:, tt:tt + 1], bias=shift[:, tt:tt + 1])
                        last.then_inc(S["xres_ready"], 1)
                    if 1 <= k <= CHUNKS:
                        act.wait_ge(S["yt_ready"], n)
                        if k >= 3:
                            act.wait_ge(S["step1_ready"], g * CHUNKS + k - 2)
                        act.activation(YT[(n - 1) % 2], TA[(n - 1) % 2][:, :], ACT.Copy).then_inc(S["yt_out"], 1)
                    if k >= 2:
                        c = k - 2
                        j = g * CHUNKS + c
                        act.wait_ge(S["step1_ready"], j + 1)
                        if c == 0 and g:
                            act.wait_ge(S["dz_out"], g * 12)
                        r0 = 1 + (IMG_H // 2) * (c % 2)
                        act.activation(A1[:, c // 2, r0:r0 + IMG_H // 2, 1:1 + IMG_W],
                                       MB[j % 2][:, :].rearrange("p (a b) -> p a b", b=IMG_W),
                                       ACT.Relu, bias=e1_bias[:, :]).then_inc(S["a1_out"], 1)

            def norm_nodes(g):
                act.wait_ge(S["norm_ready"], 2 * g + 2)
                for k in range(CHUNKS + 2):
                    n = g * 2 * CHUNKS + CHUNKS + k
                    if k < CHUNKS:
                        norm_chunk(n, k)
                    if 1 <= k <= CHUNKS:
                        tok = (g * CHUNKS + k - 1) * CHUNK
                        act.wait_ge(S["yt_ready"], n)
                        act.activation(XT[:, tok:tok + CHUNK], TA[(n - 1) % 2][:, :], ACT.Copy
                                       ).then_inc(S["yt_out"], 1)
                    if k >= 2:
                        c = k - 2
                        j = g * CHUNKS + c
                        act.wait_ge(S["node_ready"], j + 1)
                        if c == 0 and g:
                            act.wait_ge(S["node_stored"], 32 * g)
                        act.activation(node_out[:, TPC * c:TPC * (c + 1), :],
                                       MB[j % 2][:, :].rearrange("p (t n) -> p t n", n=P)[:, :, 0:2 * HEADS + HE],
                                       ACT.Copy).then_inc(S["node_out_done"], 1)

            def roots(n):
                act.wait_ge(S["var_ready"], n + 1)
                act.activation(std[:, :], std[:, :], ACT.Sqrt).then_inc(S["std_ready"], 1)

            for g in range(GROUPS):
                roots(2 * g)
                norm_step1(g)
                for i in range(4):
                    act.wait_ge(S["conv_stage"], g * 4 + i + 1)
                    if i == 0 and g == GROUPS - 1:
                        act.wait_ge(S["zeros_stored"], 32)
                    for q in range(IMGS):
                        if i < 3:
                            act.wait_ge(S["dz_out"], g * 12 + 4 * i + q + 1)
                        tok = g * TILES * P + q * IMG_H * IMG_W
                        act.activation(XT[QUAD * i:QUAD * (i + 1), tok:tok + IMG_H * IMG_W],
                                       Z[QUAD * q:QUAD * (q + 1), :, :].rearrange("p h n -> p (h n)"),
                                       ACT.Relu, bias=cb2[QUAD * q:QUAD * (q + 1), :]).then_inc(S["relu_out"], 1)
                roots(2 * g + 1)
                norm_nodes(g)

            def experts(n):
                for m in range(8):
                    act.wait_ge(S["hid_ready"], n * 8 + m + 1)
                    act.activation(HH[:, m, :], PF[m % 2][:, :], ACT.Gelu, bias=b1c[:, m:m + 1]
                                   ).then_inc(S["hid_out"], 1)
                act.wait_ge(S["exp_stored"], 16 + n * 16)
                for t in range(TPC):
                    act.wait_ge(S["exp_ready"], n * TPC + t + 1)
                    act.activation(YE[:, t, :], Z[:, t % 2, :], ACT.Copy).then_inc(S["exp_out"], 1)
                act.wait_ge(S["exp_out"], 2 + (n + 1) * TPC)
                act.dma_start(exp_chunks[n], YE).then_inc(S["exp_stored"], 16)

            for n in range(EVACS):
                act.wait_ge(S["keys_transposed"], n + 1)
                act.activation(keys_t[:, BANK_T * n:BANK_T * (n + 1), :],
                               TA[n % 2][:, :].rearrange("p (q c) -> p q c", c=P), ACT.Copy
                               ).then_inc(S["keys_evacuated"], 1)

            act.sem_inc(S["hid_out"], 2)
            act.sem_inc(S["exp_out"], 2)
            act.sem_inc(S["exp_stored"], 16)
            with act.Fori(0, FFN_CHUNKS) as n:
                experts(n)

            act.wait_ge(S["init_args"], 1)
            act.activation(tmp_a, tmp_a, ACT.Exp)
            act.activation(tmp_b, tmp_b, ACT.Exp).then_inc(S["init_exps"], 1)

            rounds = slot_rounds(act)
            with act.Fori(0, rounds) as r:
                with act.Fori(0, STEPS) as i:
                    for h in range(2):
                        act.wait_ge(e_ready[h], r * STEPS + i + 1)
                        act.activation(e_buf[h], e_buf[h], ACT.Exp).then_inc(e_exp[h], 1)
            act.wait_ge(S["score_var"], 1)
            act.activation(node1[:, :], node1[:, :], ACT.Sqrt).then_inc(S["score_std"], 1)
            act.wait_ge(S["logits_ready"], 1)
            act.activation(tmp_a, tmp_a, ACT.Exp).then_inc(S["logits_exp"], 1)

        @block.vector
        def _(dve):
            chain = [0]

            def link(ins):
                chain[0] += 1
                ins.then_inc(S["dve_chain"], 1)
                dve.wait_ge(S["dve_chain"], chain[0])

            tt, ts, stt, cp, red = (dve.tensor_tensor, dve.tensor_scalar, dve.scalar_tensor_tensor,
                                    dve.tensor_copy, dve.tensor_reduce)
            dve.wait_ge(S["consts"], 11)

            def normalise(n, eps):
                for t in range(TILES):
                    last = dve.bn_aggr(mean_var[:, t, :], bn[:, t, :])
                link(last)
                ts(std[:, :], mean_var[:, :, 1], eps, None, ALU.add).then_inc(S["var_ready"], 1)
                dve.wait_ge(S["std_ready"], n + 1)
                link(dve.reciprocal(rstd[:, :], std[:, :]))
                link(ts(rstd1[:, :], rstd[:, :], 1.0, None, ALU.add))
                link(tt(shift[:, :], mean_var[:, :, 0], rstd[:, :], ALU.mult))
                ts(shift[:, :], shift[:, :], -1.0, None, ALU.mult).then_inc(S["norm_ready"], 1)

            def token_stats(g):
                dve.wait_ge(S["x_in"], 16 * (g + 1))
                for t in range(TILES):
                    last = dve.bn_stats(bn[:, t, :], x_tiles[:, t, :])
                link(last)
                if g:
                    dve.wait_ge(S["y_ready"], 2 * CHUNKS * g)
                normalise(2 * g, 1e-6)

            def small_weights():
                dve.wait_ge(S["weights_in"], 16 * (N_WEIGHTS - 1))
                dve.wait_ge(S["comp_pe"], 1)
                cp(comp[:, 0, 0:P], TA[0][0:QUAD, 0:P]).then_inc(S["comp_dve"], 1)
                for i in range(3):
                    dve.wait_ge(S["comp_dve"], 1 + 2 * i)
                    link(cp(comp_d[:, i, 0:P + 1], comp[:, i, 0:P + 1]))
                    blk = comp_d[:, i, QUAD * i:QUAD * (i + 1)]
                    tt(blk, blk, ident[0:QUAD, 0:QUAD], ALU.subtract).then_inc(S["comp_dve"], 1)
                    dve.wait_ge(S["comp_pe"], 2 + i)
                    tt(comp[:, i + 1, 0:P + 1], comp[:, i, 0:P + 1], TA[1][0:QUAD, 0:P + 1], ALU.add
                       ).then_inc(S["comp_dve"], 1)
                dve.wait_ge(S["comp_dve"], 7)
                for i in range(4):
                    link(cp(e1_bias[QUAD * i:QUAD * (i + 1), :], comp[:, i, P:P + 1]))
                dve.wait_ge(S["comp_pe"], 5)
                link(cp(E1[:, :], MB[0][:, 0:P]))
                link(tt(rec_b[:, 1:P], ident[:, 0:P - 1], w3_row[:, 0:P - 1], ALU.mult))
                link(ts(rec_b[:, 1:P], rec_b[:, 1:P], -1.0, None, ALU.mult))
                link(cp(rec_b[:, 0:1], w3_col[:, :]))
                link(dve.memset(rec_a[:, 0:1], 0.0))
                link(ts(rec_a[:, 1:P], w3_row[:, 0:P - 1], 1.0, None, ALU.add))
                link(dve.tensor_tensor_scan(T3[:, :], rec_a, rec_b, 0.0, ALU.mult, ALU.add))
                link(dve.memset(b3_in[0:1, 1:P], 0.0))
                link(dve.tensor_tensor_scan(b3_row[:, :], rec_a[0:1, :], b3_in[:, :], 0.0, ALU.mult, ALU.add))
                for i in range(2):
                    link(tt(att_w[:, i, :], node_w[:, HEADS:HEADS + HE], att[:, i, :], ALU.mult))
                heads = lambda i: att_w[:, i, :].rearrange("p (g x) -> p g x", g=HEADS)
                link(red(node_w[:, 0:HEADS], heads(0), AX.X, ALU.add))
                red(node_w[:, HEADS + HE:], heads(1), AX.X, ALU.add).then_inc(S["comp_dve"], 1)

            def make_keys():
                A, B, Cc = KA[:, :], KB[:, :], KC[:, :]
                Ai, Bi, Ci = A.bitcast(I32), B.bitcast(I32), Cc.bitcast(I32)
                for m in range(8):
                    link(ts(sign_bits[:, m:m + 1], part_i[:, 0:1], m, 1, ALU.logical_shift_right, ALU.bitwise_and))
                link(ts(signs[:, 0:8], sign_bits[:, :], -2.0, 1.0, ALU.mult, ALU.add))
                link(tt(signs[:, 7:9], signs[:, 4:6], signs[:, 5:7], ALU.mult))
                dve.wait_ge(S["edges_in"], 32)
                link(ts(Cc, Ai, 0.0, float(M), ALU.is_lt, ALU.mult))
                link(tt(A, Ai, Cc, ALU.add))
                link(ts(A, A, 0.0, float(M - 1), ALU.max, ALU.min))
                link(ts(Cc, Bi, 0.0, float(4 * M), ALU.is_lt, ALU.mult))
                link(tt(B, Bi, Cc, ALU.max))
                link(ts(Cc, B, float(M), float(2 * M), ALU.is_ge, ALU.mult))
                link(tt(B, B, Cc, ALU.add))
                link(ts(Cc, A, float(M - 1), float(M), ALU.is_equal, ALU.mult))
                link(tt(B, B, Cc, ALU.add))
                link(ts(Bi, B, float(VALID_END), float(KEY_BIAS), ALU.min, ALU.add))
                link(ts(Bi, Bi, SRC_BITS, None, ALU.logical_shift_left))
                link(cp(Ci, A))
                link(tt(Ai, Bi, Ci, ALU.bitwise_or))
                for i, end in enumerate((REAL_END, VALID_END)):
                    link(ts(B, A, key_bits_as_float(end), 0.0, ALU.is_lt, ALU.add, accum_out=key_counts[:, i:i + 1]))
                dve.memset(counts_f[:, :], 0.0).then_inc(S["counted"], 1)

            def gather_count():
                dve.wait_ge(S["totals_ready"], 1)
                link(cp(key_totals[:, :], MB[0][:, 0:2]))
                n = counts_f[0:1, 0:1]
                per = 2 * COLS * P
                link(ts(n, key_totals[0:1, 0:1], 1.0 / per, 0.5 - 0.5 / per, ALU.mult, ALU.add))
                link(ts(n, n, ROUND_MAGIC, None, ALU.add))
                link(ts(n, n, -ROUND_MAGIC, 1.0, ALU.add, ALU.max))
                cp(counts_i[0:1, 0:1], n).then_inc(S["counts_ready"], 1)

            def exchange(src, dst, run, stride, n=ROW):
                if 2 * run <= n:
                    def part(b, d, h):
                        return b.rearrange("p (b d g h j) -> p b d g h j", d=2, g=run // (2 * stride), h=2,
                                           j=stride)[:, :, d, :, h, :]
                    turns = (0, 1)
                else:
                    def part(b, d, h):
                        return b.rearrange("p (g h j) -> p g h j", h=2, j=stride)[:, :, h, :]
                    turns = (0,)
                for d in turns:
                    tt(part(dst, d, 0), part(src, d, 0), part(src, d, 1), ALU.max if d else ALU.min)
                    last = tt(part(dst, d, 1), part(src, d, 0), part(src, d, 1), ALU.min if d else ALU.max)
                link(last)

            def row_steps():
                a, b = KA[:, :], KC[:, :]
                stride = ROW // 2
                while stride:
                    exchange(a, b, 2 * ROW, stride)
                    a, b = b, a
                    stride //= 2
                    yield

            def times_sign(col):
                link(ts(KA[:, :], KA[:, :], signs[:, col:col + 1], None, ALU.mult))

            swaps = [0]

            def quadrant_step():
                swaps[0] += 1
                dve.sem_inc(S["swap_ready"], 1)
                yield
                dve.wait_ge(S["swapped"], 64 * swaps[0])
                link(stt(KA[:, :], KB[:, :], -1.0, KA[:, :], ALU.mult, ALU.min))

            def sort_keys():
                a, b = KA[:, :], KC[:, :]
                run = 2
                while run < ROW:
                    stride = run // 2
                    while stride:
                        exchange(a, b, run, stride)
                        a, b = b, a
                        stride //= 2
                        yield
                    run *= 2
                times_sign(0)
                yield from row_steps()
                for m in range(1, LEVELS + 1):
                    if m <= 4:
                        times_sign(m - 1)
                    elif m == 5:
                        times_sign(7)
                    elif m == 6:
                        times_sign(6)
                        yield from quadrant_step()
                        times_sign(5)
                    else:
                        yield from quadrant_step()
                        times_sign(8)
                        yield from quadrant_step()
                        times_sign(5)
                    link(dve.transpose(KC[:, :], KA[:, :]))
                    a, b = KC[:, :], KB[:, :]
                    for s in range(min(m, 5) - 1, -1, -1):
                        exchange(a, b, (1 << m) if m < 5 else ROW, 1 << s)
                        a, b = b, a
                        yield
                    link(dve.transpose(KA[:, :], a))
                    if m <= 4:
                        times_sign(m)
                    yield from row_steps()
                dve.sem_inc(S["rows_sorted"], 1)

            sorting = sort_keys()

            def sort_steps(n):
                for _ in range(n):
                    next(sorting, None)

            small_weights()
            token_stats(0)
            make_keys()
            for g in range(GROUPS):
                if g:
                    token_stats(g)
                sort_steps(18)
                for i in range(3):
                    dve.wait_ge(S["conv_stage"], g * 4 + i + 1)
                    if i == 0:
                        dve.wait_ge(S["a1_out"], CHUNKS * (g + 1))
                    for q in range(IMGS):
                        r = slice(QUAD * i, QUAD * (i + 1))
                        stt(DZ[r, q, 1:1 + IMG_H, 1:1 + IMG_W],
                            Z[QUAD * q:QUAD * (q + 1), :, :].rearrange("p h (a b) -> p (h a) b", b=IMG_W),
                            cb2[QUAD * q:QUAD * (q + 1), :], A1[r, q, 1:1 + IMG_H, 1:1 + IMG_W],
                            ALU.add, ALU.subtract).then_inc(S["dz_out"], 1)
                    sort_steps(7)
                for c in range(CHUNKS):
                    j = g * CHUNKS + c
                    dve.wait_ge(S["step3_ready"], j + 1)
                    dve.wait_ge(S["xres_ready"], j + 1)
                    flat = XG[:, c * CHUNK:(c + 1) * CHUNK]
                    tt(flat, flat, MB[j % 2][:, :], ALU.add).then_inc(S["x1_ready"], 1)
                    dve.wait_ge(S["x1_ready"], j + 1)
                    for t in range(TPC):
                        last = dve.bn_stats(bn[:, TPC * c + t, :], x_tiles[:, TPC * c + t, :])
                link(last)
                dve.wait_ge(S["y_ready"], 2 * CHUNKS * g + CHUNKS)
                normalise(2 * g + 1, 1e-5)
                if g == 0:
                    gather_count()
                sort_steps(8)
            sort_steps(ROW)

            dve.wait_ge(S["keys_evacuated"], EVACS)
            ts(KB[:, :].bitcast(I32), KB[:, :].bitcast(I32), (1 << SRC_BITS) - 1, None, ALU.bitwise_and
               ).then_inc(S["sources_ready"], 1)

            link(cp(iota_f[:, :], iota_i[:, :]))
            link(ts(thresholds[:, :].bitcast(I32), win_i[:, :], SRC_BITS, None, ALU.logical_shift_left))
            link(ts(piv_i[:, 0, :], KA[:, ::STRIDE].bitcast(I32), SRC_BITS, None, ALU.logical_shift_right))
            link(ts(piv_i[:, 1, :], piv_i[:, 0, :], float(-KEY_BIAS), None, ALU.add))
            link(ts(piv_i[:, 0, :], piv_i[:, 1, :], 7, None, ALU.logical_shift_right))
            link(ts(piv_i[:, 2, :], piv_i[:, 1, :], P - 1, None, ALU.bitwise_and))
            link(cp(piv_f[:, 0, :], piv_i[:, 0, :]))
            link(cp(piv_f[:, 1, :], piv_i[:, 2, :]))
            for t in range(PIVOTS):
                if t >= 2:
                    dve.wait_ge(S["hist_done"], t - 1)
                ts(hot_hi[:, t % 2, :], iota_f[:, :], piv_f[:, 0, t:t + 1], None, ALU.is_equal)
                ts(hot_lo[:, t % 2, :], iota_f[:, 0:P], piv_f[:, 1, t:t + 1], None, ALU.is_equal
                   ).then_inc(S["hot_ready"], 1)
            dve.wait_ge(S["hist_done"], PIVOTS)
            link(cp(hist[:, :, :], H))
            for g in range(2):
                link(dve.tensor_tensor_scan(cum[:, g, :], ones[:, :], hist[:, g, :], 0.0, ALU.mult, ALU.add))
            cp(hist_tot[:, :], cum[:, :, P - 1]).then_inc(S["hist_tot_ready"], 1)
            dve.wait_ge(S["offsets_ready"], 1)
            link(cp(hist_off[:, :], PO[:, 0:2]))
            for g in range(2):
                link(stt(cum[:, g, :], cum[:, g, :], hist_off[:, g:g + 1], hist[:, g, :], ALU.add, ALU.subtract))
            link(ts(win_f[:, :], cum[:, :, :].rearrange("p g l -> p (g l)"), -1.0, 0.0, ALU.add, ALU.max))
            cp(win_i[:, :], win_f[:, :]).then_inc(S["win_idx_ready"], 1)

            dve.wait_ge(S["nodes_in"], 48)
            link(tt(tmp_a, node_rows[:, :, 0:HEADS], a_dst, ALU.add))
            link(tt(tmp_b, bc(last_row[:, 0:HEADS], 1, [P, P, HEADS]), a_dst, ALU.add))
            link(stt(tmp_a, tmp_a, 0.2, tmp_a, ALU.mult, ALU.max))
            link(stt(tmp_b, tmp_b, 0.2, tmp_b, ALU.mult, ALU.max))

            counted = hist[:, :, :].rearrange("p g l -> p (g l)")
            for b in range(WIN_BATCHES):
                dve.wait_ge(win_in[b], 16 * WIN_COLS)
                w = windows[b % 2]
                cols = slice(WIN_COLS * b, WIN_COLS * (b + 1))
                link(tt(w, w, bc(thresholds[:, cols], 2, [P, WIN_COLS, STRIDE]), ALU.is_lt))
                red(counted[:, cols], w, AX.X, ALU.add).then_inc(S["windows_counted"], 1)
            dve.wait_ge(S["windows_counted"], WIN_BATCHES)
            for g in range(2):
                last = stt(starts[:, g, 0:P], win_f[:, g * P:(g + 1) * P], float(STRIDE), hist[:, g, :],
                           ALU.mult, ALU.add)
            last.then_inc(S["starts_ready"], 1)
            dve.wait_ge(S["starts_ready"], 1)
            dve.wait_ge(S["boundary_in"], 48)
            link(tt(degree[:, :, :], starts[:, :, 1:P + 1], starts[:, :, 0:P], ALU.subtract))
            red(max_deg[:, :], degree[:, 0, :], AX.X, ALU.max).then_inc(S["max_deg_ready"], 1)
            dve.wait_ge(S["max_deg_t"], 1)
            n = counts_f[0:1, 1:2]
            link(red(n, PO[0:1, 0:P], AX.X, ALU.max))
            link(ts(n, n, 1.0 / SLOTS, 0.5 - 0.5 / SLOTS, ALU.mult, ALU.add))
            link(ts(n, n, ROUND_MAGIC, None, ALU.add))
            link(ts(n, n, -ROUND_MAGIC, 1.0, ALU.add, ALU.max))
            cp(counts_i[0:1, 1:2], n).then_inc(S["rounds_ready"], 1)

            link(ts(beat[:, :], degree[:, 1, :], 0.5, -2 * NEG, ALU.is_gt, ALU.mult))
            link(ts(beat[:, :], beat[:, :], NEG, None, ALU.add))
            link(tt(tmp_b, tmp_b, bc(beat[:, :], 2, [P, P, HEADS]), ALU.min))
            link(tt(run_max, tmp_a, tmp_b, ALU.max))
            link(tt(tmp_a, tmp_a, run_max, ALU.subtract))
            tt(tmp_b, tmp_b, run_max, ALU.subtract).then_inc(S["init_args"], 1)
            dve.wait_ge(S["init_exps"], 1)
            dve.wait_ge(S["yt_ready"], NORMS)
            dve.wait_ge(S["step1_ready"], GROUPS * CHUNKS)
            per_head = [P, P, HEADS, EXPERTS]
            link(tt(tmp_b, tmp_b, bc(degree[:, 1, :], 2, [P, P, HEADS]), ALU.mult))
            link(tt(denom, tmp_a, tmp_b, ALU.add))
            link(tt(by_head(agg), by_head(node_rows[:, :, HEADS:]), bc(tmp_a, 3, per_head), ALU.mult))
            link(tt(by_head(tmp16), by_head(bc(last_row[:, HEADS:], 1, [P, P, HE])), bc(tmp_b, 3, per_head),
                    ALU.mult))
            link(tt(agg, agg, tmp16, ALU.add))
            link(cp(slot_iota[:, :], iota_f[:, 0:SLOTS]))
            link(cp(slot_at[:, :], starts[:, 0, 0:P]))
            link(tt(slot_end[:, :], slot_at[:, :], degree[:, 0, :], ALU.add))
            link(dve.memset(slot_i[:, P:], 0))

            rounds = slot_rounds(dve)
            for h in range(2):
                dve.sem_inc(slots_used[h], 1)
            ROUND_OPS, SLOT_OPS = 4, 30
            with dve.Fori(0, rounds) as r:
                done = [0]

                def round_link(ins):
                    done[0] += 1
                    ins.then_inc(S["round_chain"], 1)
                    dve.wait_ge(S["round_chain"], r * ROUND_OPS + done[0])

                round_link(tt(slot_left[:, :], slot_end[:, :], slot_at[:, :], ALU.subtract))
                round_link(tt(node1[:, :], slot_end[:, :], slot_at[:, :], ALU.min))
                round_link(cp(slot_i[:, 0:P], node1[:, :]))
                round_link(ts(slot_at[:, :], slot_at[:, :], float(SLOTS), None, ALU.add))
                assert done[0] == ROUND_OPS
                for h in range(2):
                    cp(slot_idx[h][:, :], slot_i[:, h * NODES:(h + 1) * NODES]).then_inc(slot_idx_ready[h], 1)
                with dve.Fori(0, STEPS) as i:
                    step = r * STEPS + i
                    ops = [0]

                    def slot_link(ins):
                        ops[0] += 1
                        ins.then_inc(S["slot_chain"], 1)
                        dve.wait_ge(S["slot_chain"], step * SLOT_OPS + ops[0])

                    full = [P, NODES, SLOTS, HEADS]
                    exps = [e_buf[h][:, 0:NODES * SLOTS * HEADS].rearrange("p (c k g) -> p c k g", c=NODES, g=HEADS)
                            for h in range(2)]
                    keep = [e_buf[h][:, NODES * SLOTS * HEADS:].rearrange("p (c g) -> p c g", g=HEADS)
                            for h in range(2)]
                    rows = [slot_rows[h].rearrange("p (c k w) -> p c k w", c=NODES, w=WIDTH) for h in range(2)]

                    def mine(state, h):
                        return state[:, bass.ds(i * (2 * NODES) + h * NODES, NODES), :]

                    for h in range(2):
                        dve.wait_ge(slots_gathered[h], (step + 1) * (16 * NODES))
                        ts(slot_idx[h][:, :], slot_i[:, bass.ds(i * (2 * NODES) + (2 + h) * NODES, NODES)],
                           0.0, None, ALU.add).then_inc(slot_idx_ready[h], 1)
                        slot_link(tt(exps[h], rows[h][:, :, :, 0:HEADS], bc(mine(a_dst, h), 2, full), ALU.add))
                        slot_link(tt(slot_mask[h], bc(slot_iota[:, :], 1, [P, NODES, SLOTS]),
                                     bc(slot_left[:, bass.ds(i * (2 * NODES) + h * NODES, NODES)], 2,
                                        [P, NODES, SLOTS]), ALU.is_lt))
                        slot_link(stt(exps[h], exps[h], 0.2, exps[h], ALU.mult, ALU.max))
                        slot_link(ts(slot_mask[h], slot_mask[h], -2 * NEG, NEG, ALU.mult, ALU.add))
                        slot_link(tt(exps[h], exps[h], bc(slot_mask[h], 3, full), ALU.min))
                        slot_link(red(step_max[h], exps[h].rearrange("p c k g -> p c g k"), AX.X, ALU.max))
                        slot_link(tt(step_max[h], step_max[h], mine(run_max, h), ALU.max))
                        slot_link(tt(keep[h], mine(run_max, h), step_max[h], ALU.subtract))
                        slot_link(ts(mine(run_max, h), step_max[h], 0.0, None, ALU.add))
                        tt(exps[h], exps[h], bc(step_max[h], 2, full), ALU.subtract).then_inc(e_ready[h], 1)
                    for h in range(2):
                        dve.wait_ge(e_exp[h], step + 1)
                        slot_link(red(step_sum, exps[h].rearrange("p c k g -> p c g k"), AX.X, ALU.add))
                        split = lambda ap: ap.rearrange("p c k (g x) -> p (c k) g x", g=HEADS)
                        slot_link(tt(split(msg), split(rows[h][:, :, :, HEADS:]),
                                     bc(exps[h].rearrange("p c k g -> p (c k) g"), 3,
                                        [P, NODES * SLOTS, HEADS, EXPERTS]), ALU.mult))
                        red(step_agg, msg.rearrange("p c k f -> p c f k"), AX.X, ALU.add).then_inc(slots_used[h], 1)
                        dve.wait_ge(slots_used[h], step + 2)
                        slot_link(tt(mine(denom, h), mine(denom, h), keep[h], ALU.mult))
                        slot_link(tt(mine(denom, h), mine(denom, h), step_sum, ALU.add))
                        mine_agg = mine(agg, h).rearrange("p c (g x) -> p c g x", g=HEADS)
                        slot_link(tt(mine_agg, mine_agg, bc(keep[h], 3, [P, NODES, HEADS, EXPERTS]), ALU.mult))
                        slot_link(tt(mine(agg, h), mine(agg, h), step_agg, ALU.add))
                    assert ops[0] == SLOT_OPS

            link(ts(tmp_a, denom, 1e-16, None, ALU.add))
            link(dve.reciprocal(tmp_a, tmp_a))
            link(tt(by_head(agg), by_head(agg), bc(tmp_a, 3, per_head), ALU.mult))
            par = lambda k: bc(gat_par[:, k, :], 1, [P, P, HE])
            link(tt(agg, agg, par(0), ALU.add))
            link(red(node1[:, :], agg, AX.X, ALU.add))
            link(ts(node1[:, :], node1[:, :], 1.0 / HE, None, ALU.mult))
            link(tt(agg, agg, bc(node1[:, :], 2, [P, P, HE]), ALU.subtract))
            link(tt(tmp16, agg, agg, ALU.mult))
            link(red(node1[:, :], tmp16, AX.X, ALU.add))
            ts(node1[:, :], node1[:, :], 1.0 / HE, 1e-5, ALU.mult, ALU.add).then_inc(S["score_var"], 1)
            dve.wait_ge(S["score_std"], 1)
            link(dve.reciprocal(node1[:, :], node1[:, :]))
            link(tt(agg, agg, bc(node1[:, :], 2, [P, P, HE]), ALU.mult))
            link(tt(agg, agg, par(1), ALU.mult))
            link(tt(agg, agg, par(2), ALU.add))
            link(red(tmp_b, agg.rearrange("p l (g x) -> p l x g", g=HEADS), AX.X, ALU.add))
            link(ts(tmp_b, tmp_b, 1.0 / HEADS, None, ALU.mult))
            for i in range(EXPERTS):
                link(dve.memset(rank[:, i, :], float(i)))
            for i in range(EXPERTS):
                for j in range(i + 1, EXPERTS):
                    link(tt(beat[:, :], tmp_b[:, :, j], tmp_b[:, :, i], ALU.is_gt))
                    link(tt(rank[:, i, :], rank[:, i, :], beat[:, :], ALU.add))
                    link(tt(rank[:, j, :], rank[:, j, :], beat[:, :], ALU.subtract))
            link(ts(rank[:, :, :], rank[:, :, :], 1.5, None, ALU.is_lt))
            link(red(node2[:, :], tmp_b, AX.X, ALU.max))
            tt(tmp_a, tmp_b, bc(node2[:, :], 2, [P, P, EXPERTS]), ALU.subtract).then_inc(S["logits_ready"], 1)
            dve.wait_ge(S["logits_exp"], 1)
            link(tt(tmp_a, tmp_a, rank[:, :, :].rearrange("p x l -> p l x"), ALU.mult))
            link(red(node2[:, :], tmp_a, AX.X, ALU.add))
            link(dve.reciprocal(node2[:, :], node2[:, :]))
            tt(gate[:, :, :], tmp_a, bc(node2[:, :], 2, [P, P, EXPERTS]), ALU.mult).then_inc(S["gate_ready"], 1)
            dve.wait_ge(S["gate_tr"], 1)
            link(cp(KC[:, 1024:1536], TA[0][:, :]))
            for s in range(FFN_CHUNKS):
                dve.wait_ge(tail_in[s % 2], 32 * (s // 2 + 1))
                for x_ in range(EXPERTS):
                    for t in range(TPC):
                        tile = TPC * s + t
                        last = stt(tail_x[s % 2][:, t, :], tail_y[s % 2][:, t, x_ * C:(x_ + 1) * C],
                                   gate_t[:, x_, tile:tile + 1], tail_x[s % 2][:, t, :], ALU.mult, ALU.add)
                    if x_ < EXPERTS - 1:
                        link(last)
                last.then_inc(S["tail_done"], 1)


_INS = ['x', 'L0_conv_w1', 'L0_conv_b1', 'L0_conv_w2', 'L0_conv_b2', 'L0_conv_w3', 'L0_conv_b3', 'L0_ffn_W_gat',
        'L0_ffn_att_src', 'L0_ffn_att_dst', 'L0_ffn_b_gat', 'L0_ffn_ln_gamma', 'L0_ffn_ln_beta', 'L0_ffn_W1',
        'L0_ffn_b1', 'L0_ffn_W2', 'L0_ffn_b2', 'L0_ffn_edge_index']


def kernel(**inputs):
    import numpy as _np
    import concourse.bacc as _bacc
    from concourse import mybir as _mybir
    from concourse.bass_utils import run_bass_kernel_spmd as _run

    nc = _bacc.Bacc("TRN2", target_bir_lowering=False, num_devices=1)
    arrays, args = {}, []
    for name in _INS:
        a = _np.ascontiguousarray(inputs[name])
        arrays[f"in_{name}_dram"] = a
        args.append(nc.dram_tensor(f"in_{name}_dram", a.shape, _mybir.dt.from_np(a.dtype), kind="ExternalInput").ap())
    out = nc.dram_tensor("out_dram", (16, 32, 32, 128), _mybir.dt.float32, kind="ExternalOutput").ap()
    program(nc, *args, out)
    r = _run(nc, [arrays], core_ids=[0])
    return r.results[0]["out_dram"]
```

```python
from contextlib import ExitStack

import concourse.bass as bass
from concourse import mybir

F32, I32, BF16 = mybir.dt.float32, mybir.dt.int32, mybir.dt.bfloat16
ALU, ACT, AX = mybir.AluOpType, mybir.ActivationFunctionType, mybir.AxisListType

P = 128
N_IMG, IMG_H, IMG_W, C = 16, 32, 32, 128
M = N_IMG * IMG_H * IMG_W
E = 524288
HEADS, EXPERTS = 4, 4
HE = HEADS * EXPERTS
HID = 2 * C

GROUPS, IMGS = 4, 4
TILES = IMGS * IMG_H * IMG_W // P
CHUNK = 512
CHUNKS = TILES * P // CHUNK
TPC = CHUNK // P
PADH, PADW = IMG_H + 2, IMG_W + 2
QUAD = 32
TAPS = [(dy, dx) for dy in range(3) for dx in range(3)]
FFN_CHUNKS = M // CHUNK

ROW = E // P
SRC_BITS = 14
KEY_BIAS = 512
REAL_END, VALID_END = M, 2 * M
BLOCKS = ROW // P
LEVELS = 7
BANK_T = 4
EVACS = BLOCKS // BANK_T
STRIDE = 64
PIVOTS = ROW // STRIDE
SHARE = 4
SPAN = 2
WINDOW = SPAN * STRIDE
GROUPS_OF_NODES = 2 * P // SHARE
WIN_COLS = 16
WIN_BATCHES = GROUPS_OF_NODES // WIN_COLS

WIDTH = HEADS + HE
COLS = 8
TRIPS = ROW // (2 * COLS)
PER_TRIP = 2 * COLS * P
EARLY, MIDDLE = 3, 3
SLOTS = 24
NODES = 4
NODE_GROUPS = P // NODES
TERMS = SLOTS + 1
NEG = -1e30
ROUND_MAGIC = 12582912.0


def key_bits_as_float(j):
    import numpy as np
    return float(np.array((j + KEY_BIAS) << SRC_BITS, np.int32).view(np.float32))


def program(nc, x, w1, b1, w2, b2, w3, b3, w_gat, att_src, att_dst, b_gat, ln_gamma, ln_beta,
            ffn_w1, ffn_b1, ffn_w2, ffn_b2, edge_index, out):
    ctx = ExitStack()
    with ctx:
        def sb(name, shape, dt=F32):
            return ctx.enter_context(nc.sbuf_tensor(name, shape, dt))

        def ps(name, shape, dt=F32):
            return ctx.enter_context(nc.psum_tensor(name, shape, dt))

        def sem(name):
            return ctx.enter_context(nc.semaphore(name))

        def bc(ap, axis, shape):
            return ap.unsqueeze(axis).to_broadcast(shape)

        x1_dram = nc.dram_tensor("x1_dram", [M, C], F32).ap()
        node_dram = nc.dram_tensor("node_dram", [M, WIDTH], F32).ap()
        adst_dram = nc.dram_tensor("adst_dram", [M, HEADS], F32).ap()
        keys_dram = nc.dram_tensor("keys_dram", [E + WINDOW], F32).ap()
        payload = nc.dram_tensor("payload", [E + SLOTS, WIDTH], F32).ap()

        KA, KB, KC = sb("KA", [P, ROW]), sb("KB", [P, ROW]), sb("KC", [P, ROW])
        XT = sb("XT", [P, M])
        XG = sb("XG", [P, TILES * C])
        ARENA_A = sb("ARENA_A", [P, IMGS * PADH * PADW])
        ARENA_D = sb("ARENA_D", [P, IMGS * PADH * PADW])
        ARENA_Y = sb("ARENA_Y", [P, 4 * CHUNK])
        x_tiles = XG[:, :].rearrange("p (t c) -> p t c", c=C)
        A1 = ARENA_A[:, :].rearrange("p (i a b) -> p i a b", i=IMGS, b=PADW)
        DZ = ARENA_D[:, :].rearrange("p (i a b) -> p i a b", i=IMGS, b=PADW)
        Y = [ARENA_Y[:, i * CHUNK:(i + 1) * CHUNK].rearrange("p (t c) -> p t c", c=C) for i in range(2)]
        YT = [ARENA_Y[:, (2 + i) * CHUNK:(3 + i) * CHUNK] for i in range(2)]
        HH = ARENA_A[:, 0:8 * CHUNK].rearrange("p (m n) -> p m n", n=CHUNK)
        YE = [ARENA_D[:, h * 2048:(h + 1) * 2048].rearrange("p (t n) -> p t n", n=CHUNK) for h in range(2)]
        zeros = XT[:, (GROUPS - 1) * TILES * P:(GROUPS - 1) * TILES * P + P * WIDTH]
        node_rows = XG[:, 0:P * WIDTH].rearrange("p (l f) -> p l f", f=WIDTH)

        def node4(arena, at):
            return arena[:, at:at + P * HEADS].rearrange("p (l g) -> p l g", g=HEADS)

        a_dst, run_max, denom = (node4(XG, P * WIDTH + i * P * HEADS) for i in range(3))
        agg = ARENA_Y[:, 0:P * HE].rearrange("p (l f) -> p l f", f=HE)
        tmp16 = KA[:, 0:P * HE].rearrange("p (l f) -> p l f", f=HE)
        tmp_a, tmp_b = node4(KA, P * HE), node4(KA, P * HE + P * HEADS)
        slot_rows = [KA[:, h * 2048:h * 2048 + NODES * TERMS * WIDTH].rearrange("p (c k w) -> p c k w", c=NODES, w=WIDTH)
                     for h in range(2)]
        tail_x = [KC[:, (1 + h) * CHUNK:(2 + h) * CHUNK].rearrange("p (t c) -> p t c", c=C) for h in range(2)]
        msg = KC[:, 1536:1536 + NODES * TERMS * HE].rearrange("p (c k f) -> p c k f", c=NODES, f=HE)
        e_buf = KC[:, 3136:3136 + NODES * TERMS * HEADS]
        exps = e_buf.rearrange("p (c k g) -> p c k g", c=NODES, g=HEADS)
        unused = KC[:, 3600:3600 + NODES * SLOTS].rearrange("p (c k) -> p c k", k=SLOTS)
        g4 = [KC[:, 3712 + 4 * i:3716 + 4 * i] for i in range(3)]
        den_g, score_g, weight_g, gate_g = (KC[:, 3728 + 16 * i:3744 + 16 * i].rearrange("p (c x) -> p c x", c=NODES)
                                            for i in range(4))
        agg_g, sq_g, greater, equal = (KC[:, 3792 + 64 * i:3856 + 64 * i].rearrange("p (c f) -> p c f", c=NODES)
                                       for i in range(4))
        windows = [KA[:, i * 2048:(i + 1) * 2048].rearrange("p (c w) -> p c w", w=WINDOW) for i in range(2)]
        below = KC[:, 1024:1024 + WIN_COLS * WINDOW].rearrange("p (c w) -> p c w", w=WINDOW)
        win_at = KC[:, 3072:3072 + GROUPS_OF_NODES]
        found = KC[:, 3200:3200 + WIN_COLS * SHARE].rearrange("p (c j) -> p c j", j=SHARE)
        end_keys = KC[0:1, 3328:3328 + WINDOW]

        ident, ones = sb("ident", [P, P]), sb("ones", [P, P])
        before = sb("before", [P, P])
        signs, part_i = sb("signs", [P, 9]), sb("part_i", [P, 1], I32)
        sign_bits = sb("sign_bits", [P, 8], I32)
        cw1, cw1_blocks = sb("cw1", [P, QUAD]), sb("cw1_blocks", [QUAD, 4, QUAD])
        comp, comp_d = (KC[0:QUAD, i * 1024:i * 1024 + 4 * (P + 4)].rearrange("p (i n) -> p i n", i=4) for i in range(2))
        w3_row, rec_a, rec_b = (KC[:, 2048 + i * P:2048 + (i + 1) * P] for i in range(3))
        E1, e1_bias = sb("E1", [P, P]), sb("e1_bias", [P, 1])
        cw2, cb2 = sb("cw2", [P, 9, QUAD]), sb("cb2", [P, 1])
        w3_col, b3_in = sb("w3_col", [P, 1]), sb("b3_in", [1, P])
        T3, b3_row = sb("T3", [P, P]), sb("b3_row", [1, P])
        node_w = sb("node_w", [P, 2 * HEADS + HE])
        att, att_w = sb("att", [P, 2, HE]), sb("att_w", [P, 2, HE])
        W1, b1c = sb("W1", [P, EXPERTS, HID]), sb("b1c", [P, 8])
        W2, b2r = sb("W2", [P, 8, C]), sb("b2r", [1, EXPERTS * C])
        bn, mean_var = sb("bn", [P, TILES, 6]), sb("mean_var", [P, TILES, 2])
        rstd, rstd1, shift, std = (sb(n, [P, TILES]) for n in ("rstd", "rstd1", "shift", "std"))
        node_out = sb("node_out", [P, TILES, 2 * HEADS + HE])
        key_counts, key_totals = sb("key_counts", [P, 2]), sb("key_totals", [P, 2])
        counts_f, counts_i = sb("counts_f", [1, 4]), sb("counts_i", [1, 4], I32)
        iota_i, iota_f = sb("iota_i", [P, 2 * P], I32), sb("iota_f", [P, 2 * P])
        piv_i, piv_f = sb("piv_i", [P, 3, PIVOTS], I32), sb("piv_f", [P, 2, PIVOTS])
        hot_hi, hot_lo = sb("hot_hi", [P, 2, 2 * P], BF16), sb("hot_lo", [P, 2, P], BF16)
        hist = sb("hist", [P, 2, P])
        cum = KC[:, 3584:3584 + 2 * P].rearrange("p (g l) -> p g l", l=P)
        hist_tot, hist_off = sb("hist_tot", [P, 2]), sb("hist_off", [P, 2])
        win_i, win_f, thresholds = sb("win_i", [P, 2 * P], I32), sb("win_f", [P, 2 * P]), sb("thresholds", [P, 2 * P])
        starts, degree, max_deg = sb("starts", [P, 2, P + 1]), sb("degree", [P, 2, P]), sb("max_deg", [P, 1])
        src_buf = [sb(f"src_buf{h}", [P, COLS], I32) for h in range(2)]
        row_buf = [KC[:, h * COLS * WIDTH:(h + 1) * COLS * WIDTH].rearrange("p (t f) -> p t f", f=WIDTH) for h in range(2)]
        last_row = sb("last_row", [P, WIDTH])
        slot_iota = sb("slot_iota", [P, SLOTS])
        starts_t = sb("starts_t", [P, P + NODES])
        ends_t = sb("ends_t", [P, P + NODES])
        slot_at, slot_end = ([sb(f"{n}{h}", [P, NODES]) for h in range(2)] for n in ("slot_at", "slot_end"))
        slot_left, slot_next = sb("slot_left", [P, NODES]), sb("slot_next", [P, NODES])
        slot_idx = [sb(f"slot_idx{h}", [P, NODES], I32) for h in range(2)]
        trip_f, trip_i = sb("trip_f", [1, NODE_GROUPS + 1]), sb("trip_i", [1, NODE_GROUPS + 1], I32)
        spread = sb("spread", [1, NODE_GROUPS])
        lower_i, lower = sb("lower_i", [P, 2, HE], I32), sb("lower", [P, HE])
        gat_par = sb("gat_par", [P, 3, HE])
        beat = sb("beat", [P, P])

        TA = [ps(f"TA{i}", [P, CHUNK]) for i in range(2)]
        MB = [ps(f"MB{i}", [P, CHUNK]) for i in range(2)]
        Z = ps("Z", [P, 2, CHUNK])
        PF = [ps(f"PF{i}", [P, CHUNK]) for i in range(2)]
        H = MB[0][:, 0:2 * P].rearrange("p (g l) -> p g l", l=P)
        PO = MB[1]

        names = """weights_in consts edges_in x_in comp_pe comp_dve
            var_ready std_ready norm_ready y_ready xres_ready yt_ready yt_out step1_ready a1_out
            conv_stage dz_out relu_out step3_ready x1_ready node_ready node_out_done node_stored x1_stored
            zeros_stored hid_ready hid_out exp_ready exp_out
            dve_chain counted totals_ready
            swap_ready swapped rows_sorted keys_transposed keys_evacuated keys_stored sources_ready
            hot_ready hist_done hist_tot_ready offsets_ready spread_ready spread_t window_rounds_ready win_idx_ready
            windows_counted window_chain starts_ready end_keys_ready
            boundary_ready max_deg_ready max_deg_t rounds_ready
            gpsimd_turns nodes_in init_args init_exps slot_chain group_chain vector_turns sync_turns
            degree_ready starts_turned table_ready e_ready e_exp
            score_var score_std logits_ready logits_exp""".split()
        S = {n: sem(n) for n in names}
        src_copied, rows_gathered, rows_stored = (
            [sem(f"{n}{h}") for h in range(2)] for n in ("src_copied", "rows_gathered", "rows_stored"))
        slot_idx_ready, slots_gathered, slots_used, tail_in, tail_done, tail_out = (
            [sem(f"{n}{h}") for h in range(2)]
            for n in ("slot_idx_ready", "slots_gathered", "slots_used", "tail_in", "tail_done", "tail_out"))
        win_in = [sem(f"win_in{i}") for i in range(2)]
        block = ctx.enter_context(nc.Block())

        x_groups = x.rearrange("b h w c -> (b h w) c").rearrange("(g t p) c -> g p t c", t=TILES, p=P)
        x1_groups = x1_dram.rearrange("(g t p) c -> g p t c", t=TILES, p=P)
        x1_chunks = x1_dram.rearrange("(s t p) c -> s p t c", t=TPC, p=P)
        out_chunks = out.rearrange("b h w c -> (b h w) c").rearrange("(s t p) c -> s p t c", t=TPC, p=P)
        node_groups = node_dram.rearrange("(g t p) c -> g p t c", t=TILES, p=P)
        adst_groups = adst_dram.rearrange("(g t p) c -> g p t c", t=TILES, p=P)
        payload_cols = payload[0:E].rearrange("(c t q) f -> c q t f", t=COLS, q=P)
        key_windows = keys_dram.rearrange("(r w) -> r w", w=STRIDE)
        keys_t = KB[:, :].rearrange("q (p j) -> q j p", j=BLOCKS)
        by_head = lambda ap: ap.rearrange("p l (g x) -> p l g x", g=HEADS)
        PAIRS = NODE_GROUPS // 2
        N_WEIGHTS = 24
        NORMS = GROUPS * 2 * CHUNKS

        def group_trips(eng, g):
            lo, hi = (eng.value_load(trip_i[0:1, bass.ds(g + k, 1)], min_val=EARLY + MIDDLE + k,
                                     max_val=TRIPS + 1 + NODE_GROUPS) for k in range(2))
            return lo, hi

        def window_rounds(eng):
            eng.wait_ge(S["window_rounds_ready"], 1)
            return eng.value_load(counts_i[0:1, 2:3], min_val=1, max_val=E // WINDOW + 1)

        def slot_rounds(eng):
            eng.wait_ge(S["rounds_ready"], 1)
            return eng.value_load(counts_i[0:1, 1:2], min_val=1, max_val=-(-E // SLOTS))

        @block.sync
        def _(sp):
            sp.dma_start(x_tiles, x_groups[0]).then_inc(S["x_in"], 16)
            edge_rows = edge_index.rearrange("a (p f) -> a p f", p=P)
            sp.dma_start(KA[:, :].bitcast(I32), edge_rows[0]).then_inc(S["edges_in"], 16)
            sp.dma_start(KB[:, :].bitcast(I32), edge_rows[1]).then_inc(S["edges_in"], 16)
            loads = [
                (cw1[:, :], w1.rearrange("a b c n -> (a b c) n")),
                (cw1_blocks[:, :, :], w1.rearrange("a b (j k) n -> k (a b j) n", k=QUAD)),
                (comp[:, 0, P:P + 1], b1.rearrange("a b c n -> n (a b c)")),
                (cw2[:, :, :], w2.rearrange("a b c n -> c (a b) n")),
            ] + [(cb2[QUAD * q:QUAD * (q + 1), :], b2.rearrange("a b c n -> n (a b c)")) for q in range(4)] + [
                (w3_row, w3.rearrange("a b c n -> (a b n) c").to_broadcast([P, P])),
                (w3_col[:, :], w3.rearrange("a b c n -> c (a b n)")),
                (b3_in[0:1, 0:1], b3.rearrange("a b c n -> (a b c) n")),
                (node_w[:, HEADS:HEADS + HE], w_gat),
                (att[:, 0, :], att_src.rearrange("a b -> (a b)").unsqueeze(0).to_broadcast([P, HE])),
                (att[:, 1, :], att_dst.rearrange("a b -> (a b)").unsqueeze(0).to_broadcast([P, HE])),
                (W1[:, :, :], ffn_w1.rearrange("e k n -> k e n")),
                (b1c[:, :], ffn_b1.rearrange("e (m p) -> p (e m)", p=P)),
                (W2[:, 0:4, :], ffn_w2[0:2].rearrange("e (k p) n -> p (e k) n", p=P)),
                (W2[:, 4:8, :], ffn_w2[2:4].rearrange("e (k p) n -> p (e k) n", p=P)),
                (b2r[:, 0:2 * C], ffn_b2[0:2].rearrange("e n -> (e n)").unsqueeze(0)),
                (b2r[:, 2 * C:], ffn_b2[2:4].rearrange("e n -> (e n)").unsqueeze(0)),
            ] + [(gat_par[:, i, :], a.unsqueeze(0).to_broadcast([P, HE]))
                 for i, a in enumerate((b_gat, ln_gamma, ln_beta))]
            for dst, src in loads:
                sp.dma_start(dst, src, allow_slow_non_contiguous=True).then_inc(S["weights_in"], 16)
            assert len(loads) == N_WEIGHTS - 1
            sp.wait_ge(S["consts"], 1)
            sp.dma_start(payload[0:E].rearrange("(a p b) f -> p a (b f)", p=P, b=P),
                         bc(zeros, 1, [P, E // (P * P), P * WIDTH])).then_inc(S["zeros_stored"], 16)
            sp.dma_start(payload[E:E + SLOTS], zeros[0:SLOTS, 0:WIDTH]).then_inc(S["zeros_stored"], 16)
            for g in range(GROUPS):
                sp.wait_ge(S["x1_ready"], CHUNKS * (g + 1))
                sp.dma_start(x1_groups[g], x_tiles).then_inc(S["x1_stored"], 16)
                sp.wait_ge(S["node_out_done"], CHUNKS * (g + 1))
                sp.dma_start(node_groups[g], node_out[:, :, 0:WIDTH]).then_inc(S["node_stored"], 16)
                sp.dma_start(adst_groups[g], node_out[:, :, WIDTH:]).then_inc(S["node_stored"], 16)
                sp.wait_ge(S["x1_stored"], 16 * (g + 1))
                sp.wait_ge(S["y_ready"], 2 * CHUNKS * (g + 1))
                if g + 1 < GROUPS:
                    sp.dma_start(x_tiles, x_groups[g + 1]).then_inc(S["x_in"], 16)
            sp.wait_ge(S["node_stored"], 32 * GROUPS)
            sp.dma_start(node_rows, node_dram.rearrange("(l p) f -> p l f", p=P)).then_inc(S["nodes_in"], 16)
            sp.dma_start(a_dst, adst_dram.rearrange("(l p) f -> p l f", p=P)).then_inc(S["nodes_in"], 16)
            sp.dma_start(last_row[:, :], node_dram[M - 1:M, :].to_broadcast([P, WIDTH])).then_inc(S["nodes_in"], 16)
            sp.wait_ge(S["rows_sorted"], 1)
            sp.dma_start(keys_dram[0:E].rearrange("(p f) -> p f", p=P), KA[:, :]).then_inc(S["keys_stored"], 16)
            sp.wait_ge(S["end_keys_ready"], 1)
            sp.dma_start(keys_dram[E:].unsqueeze(0), end_keys).then_inc(S["keys_stored"], 16)
            sp.wait_ge(S["zeros_stored"], 32)
            for h in range(2):
                sp.sem_inc(rows_stored[h], 16)

            def waited():
                sp.sem_inc(S["sync_turns"], 1)

            def store_rows(trip, h):
                sp.wait_ge(rows_gathered[h], (trip + 1) * (16 * COLS))
                waited()
                sp.dma_start(payload_cols[(trip & (TRIPS - 1)) * 2 + h], row_buf[h][:, :, :]
                             ).then_inc(rows_stored[h], 16)

            store_rows(0, 0)
            with sp.Fori(1, EARLY + MIDDLE) as i:
                store_rows(i - 1, 1)
                store_rows(i, 0)
            rounds = slot_rounds(sp)
            sp.wait_ge(S["table_ready"], 1)
            for h in range(2):
                sp.sem_inc(tail_out[h], 16)
            with sp.Fori(0, PAIRS) as gg:
                for h in range(2):
                    sp.wait_ge(tail_out[h], gg * 16 + 16)
                    waited()
                    sp.dma_start(tail_x[h], x1_chunks[gg * 2 + h]).then_inc(tail_in[h], 16)
                    lo, hi = group_trips(sp, gg * 2 + h)
                    with sp.Fori(lo, hi) as i:
                        store_rows(i - 1, 1)
                        store_rows(i, 0)
                    sp.wait_ge(slots_gathered[h], (gg + 1) * rounds * (16 * NODES))
                    waited()
            store_rows(hi - 1, 1)
            sp.wait_ge(rows_stored[1], 16 + hi * 16)
            waited()

        @block.gpsimd
        def _(pool):
            pool.memset(zeros, 0.0).then_inc(S["consts"], 1)
            pool.memset(ident[:, :], 0.0).then_inc(S["consts"], 1)
            pool.memset(before[:, :], 1.0).then_inc(S["consts"], 1)
            pool.wait_ge(S["consts"], 3)
            pool.affine_select(out=ident[:, :], in_=ident[:, :], compare_op=ALU.not_equal, fill=1.0,
                               base=0, pattern=[[-1, P]], channel_multiplier=1).then_inc(S["consts"], 1)
            pool.affine_select(out=before[:, :], in_=before[:, :], compare_op=ALU.is_gt, fill=0.0,
                               base=0, pattern=[[1, P]], channel_multiplier=-1).then_inc(S["consts"], 1)
            pool.memset(ones[:, :], 1.0).then_inc(S["consts"], 1)
            pool.iota(part_i[:, :], [[0, 1]], 0, 1).then_inc(S["consts"], 1)
            pool.iota(iota_i[:, :], [[1, 2 * P]], 0, 0).then_inc(S["consts"], 1)
            pool.iota(win_i[:, :], [[M, 2], [1, P]], KEY_BIAS, P).then_inc(S["consts"], 1)
            pool.memset(ARENA_A[:, :], 0.0).then_inc(S["consts"], 1)
            pool.memset(ARENA_D[:, :], 0.0).then_inc(S["consts"], 1)

            for n, dist in enumerate((1, 2, 1)):
                pool.wait_ge(S["swap_ready"], n + 1)
                for q in range(4):
                    a, b = QUAD * q, QUAD * (q ^ dist)
                    pool.dma_start(KB[a:a + QUAD, :], KA[b:b + QUAD, :]).then_inc(S["swapped"], 16)

            def settled(eng):
                eng.sem_inc(S["gpsimd_turns"], 1)

            def gather_rows(trip):
                for h in range(2):
                    col = pool.snap((trip & (TRIPS - 1)) * (2 * COLS) + h * COLS)
                    pool.wait_ge(rows_stored[h], 16 + trip * 16)
                    settled(pool)
                    pool.tensor_copy(src_buf[h][:, :], KB[:, bass.ds(col, COLS)].bitcast(I32)
                                     ).then_inc(src_copied[h], 1)
                    pool.wait_ge(src_copied[h], trip + 1)
                    settled(pool)
                    for t in range(COLS):
                        pool.indirect_dma_start(
                            row_buf[h][:, t, :], None, node_dram,
                            bass.IndirectOffsetOnAxis(ap=src_buf[h][:, t:t + 1], axis=0)).then_inc(rows_gathered[h], 16)

            pool.wait_ge(S["sources_ready"], 1)
            pool.wait_ge(S["node_stored"], 32 * GROUPS)
            with pool.Fori(0, EARLY) as i:
                gather_rows(i)

            pool.wait_ge(S["keys_stored"], 32)
            with pool.Fori(0, window_rounds(pool)) as r:
                pool.wait_ge(S["win_idx_ready"], r + 1)
                for b in range(WIN_BATCHES):
                    pool.wait_ge(S["windows_counted"], r * WIN_BATCHES + b + 1)
                    settled(pool)
                    for k in range(WIN_COLS):
                        col = b * WIN_COLS + k
                        pool.indirect_dma_start(
                            windows[b % 2][:, k, :], None, key_windows,
                            bass.IndirectOffsetOnAxis(ap=win_i[:, col:col + 1], axis=0)).then_inc(win_in[b % 2], 16)

            with pool.Fori(EARLY, EARLY + MIDDLE) as i:
                gather_rows(i)

            rounds = slot_rounds(pool)
            pool.wait_ge(S["table_ready"], 1)
            with pool.Fori(0, PAIRS) as gg:
                for h in range(2):
                    lo, hi = group_trips(pool, gg * 2 + h)
                    with pool.Fori(lo, hi) as i:
                        gather_rows(i)
                    pool.wait_ge(rows_stored[0], 16 + hi * 16)
                    pool.wait_ge(rows_stored[1], hi * 16)
                    settled(pool)
                    with pool.Fori(0, rounds) as r:
                        pool.wait_ge(slot_idx_ready[h], gg * (rounds + 1) + r + 1)
                        pool.wait_ge(slots_used[h], gg * rounds + r + 1)
                        settled(pool)
                        for t in range(NODES):
                            pool.indirect_dma_start(
                                slot_rows[h][:, t, 0:SLOTS, :].rearrange("p k w -> p (k w)"), None, payload,
                                bass.IndirectOffsetOnAxis(ap=slot_idx[h][:, t:t + 1], axis=0)
                            ).then_inc(slots_gathered[h], 16)

        @block.tensor
        def _(pe):
            pe.wait_ge(S["consts"], 11)
            pe.wait_ge(S["weights_in"], 16 * (N_WEIGHTS - 1))
            pe.transpose(TA[0][0:QUAD, 0:P], cw1[:, :], ident[:, :]).then_inc(S["comp_pe"], 1)
            for i in range(3):
                pe.wait_ge(S["comp_dve"], 2 + 2 * i)
                pe.matmul(TA[1][0:QUAD, 0:P + 1], cw1_blocks[:, i, :], comp_d[:, i, 0:P + 1],
                          start=True, stop=True).then_inc(S["comp_pe"], 1)
            pe.wait_ge(S["comp_dve"], 7)
            for i in range(4):
                last = pe.transpose(MB[0][:, QUAD * i:QUAD * (i + 1)], comp[:, i, 0:P], ident[0:QUAD, 0:QUAD])
            last.then_inc(S["comp_pe"], 1)
            pe.wait_ge(S["comp_dve"], 8)

            def norm_step1(g):
                for k in range(CHUNKS + 1):
                    n, j = g * 2 * CHUNKS + k, g * CHUNKS + k - 1
                    if k < CHUNKS:
                        transpose_chunk(n)
                    if k >= 1:
                        pe.wait_ge(S["yt_out"], n)
                        if k >= 3:
                            pe.wait_ge(S["a1_out"], j - 1)
                        elif g:
                            pe.wait_ge(S["node_out_done"], g * CHUNKS)
                        pe.matmul(MB[j % 2][:, :], E1[:, :], YT[(n - 1) % 2], start=True, stop=True
                                  ).then_inc(S["step1_ready"], 1)

            def norm_nodes(g):
                for k in range(CHUNKS + 1):
                    n, j = g * 2 * CHUNKS + CHUNKS + k, g * CHUNKS + k - 1
                    if k < CHUNKS:
                        transpose_chunk(n)
                    if k >= 1:
                        pe.wait_ge(S["yt_out"], n)
                        if k >= 3:
                            pe.wait_ge(S["node_out_done"], j - 1)
                        else:
                            pe.wait_ge(S["x1_ready"], (g + 1) * CHUNKS)
                        for t in range(TPC):
                            tok = (j * TPC + t) * P
                            last = pe.matmul(MB[j % 2][:, t * P:t * P + 2 * HEADS + HE], XT[:, tok:tok + P],
                                             node_w[:, :], start=True, stop=True)
                        last.then_inc(S["node_ready"], 1)

            def transpose_chunk(n):
                pe.wait_ge(S["y_ready"], n + 1)
                if n >= 2:
                    pe.wait_ge(S["yt_out"], n - 1)
                for t in range(TPC):
                    last = pe.transpose(TA[n % 2][:, t * P:(t + 1) * P], Y[n % 2][:, t, :], ident[:, :])
                last.then_inc(S["yt_ready"], 1)

            def convolution(g):
                pe.wait_ge(S["a1_out"], CHUNKS * (g + 1))
                for i in range(4):
                    if i:
                        pe.wait_ge(S["dz_out"], g * 12 + 4 * i)
                        pe.wait_ge(S["relu_out"], g * 16 + 4 * i)
                    elif g:
                        pe.wait_ge(S["relu_out"], g * 16)
                    for half in range(2):
                        for t, (dy, dx) in enumerate(TAPS):
                            y0 = half * (IMG_H // 2) + dy
                            for q in range(IMGS):
                                if i == 0:
                                    last = pe.matmul(Z[QUAD * q:QUAD * (q + 1), half, :], cw2[:, t, :],
                                                     A1[:, q, y0:y0 + IMG_H // 2, dx:dx + IMG_W],
                                                     start=t == 0, stop=True, skip_group_check=True)
                                else:
                                    k0 = QUAD * (i - 1)
                                    last = pe.matmul(Z[QUAD * q:QUAD * (q + 1), half, :], cw2[k0:k0 + QUAD, t, :],
                                                     DZ[k0:k0 + QUAD, q, y0:y0 + IMG_H // 2, dx:dx + IMG_W],
                                                     start=False, stop=True, skip_group_check=True)
                    last.then_inc(S["conv_stage"], 1)

            def step3(g):
                pe.wait_ge(S["relu_out"], g * 16 + 16)
                for c in range(CHUNKS):
                    j = g * CHUNKS + c
                    if c >= 2:
                        pe.wait_ge(S["x1_ready"], j - 1)
                    for t in range(TPC):
                        tok = (j * TPC + t) * P
                        pe.matmul(MB[j % 2][:, t * P:(t + 1) * P], XT[:, tok:tok + P], T3[:, :],
                                  start=True, stop=False, skip_group_check=True)
                        last = pe.matmul(MB[j % 2][:, t * P:(t + 1) * P], ones[0:1, :], b3_row[:, :],
                                         start=False, stop=True, skip_group_check=True)
                    last.then_inc(S["step3_ready"], 1)

            for g in range(GROUPS):
                norm_step1(g)
                convolution(g)
                step3(g)
                norm_nodes(g)
                if g == 0:
                    pe.wait_ge(S["counted"], 1)
                    pe.wait_ge(S["node_out_done"], CHUNKS)
                    pe.matmul(MB[0][:, 0:2], ones[:, :], key_counts[:, :], start=True, stop=True
                              ).then_inc(S["totals_ready"], 1)

            def experts(n):
                for m in range(8):
                    pe.wait_ge(S["hid_out"], n * 8 + m + 1)
                    pe.matmul(PF[m % 2][:, :], W1[:, m // 2, (m % 2) * P:(m % 2) * P + P],
                              XT[:, bass.ds(n * CHUNK, CHUNK)], start=True, stop=True).then_inc(S["hid_ready"], 1)
                pe.wait_ge(S["hid_out"], n * 8 + 10)
                for t in range(TPC):
                    pe.wait_ge(S["exp_out"], n * TPC + t + 1)
                    pe.matmul(Z[:, t % 2, :], ones[0:1, :], b2r[:, :], start=True, stop=False, skip_group_check=True)
                    for x_ in range(EXPERTS):
                        for kk in range(2):
                            last = pe.matmul(Z[:, t % 2, x_ * C:(x_ + 1) * C], HH[:, 2 * x_ + kk, t * P:(t + 1) * P],
                                             W2[:, 2 * x_ + kk, :], start=False, stop=True, skip_group_check=True)
                    last.then_inc(S["exp_ready"], 1)

            pe.wait_ge(S["yt_out"], NORMS)
            pe.wait_ge(S["rows_sorted"], 1)
            for n in range(EVACS):
                if n >= 2:
                    pe.wait_ge(S["keys_evacuated"], n - 1)
                for q in range(BANK_T):
                    j = BANK_T * n + q
                    last = pe.transpose(TA[n % 2][:, q * P:(q + 1) * P], KA[:, j * P:(j + 1) * P], ident[:, :])
                last.then_inc(S["keys_transposed"], 1)

            for t in range(PIVOTS):
                pe.wait_ge(S["hot_ready"], t + 1)
                for g in range(2):
                    last = pe.matmul(H[:, g, :], hot_hi[:, t % 2, g * P:(g + 1) * P], hot_lo[:, t % 2, :],
                                     start=t == 0 and g == 0, stop=t == PIVOTS - 1, skip_group_check=True)
                last.then_inc(S["hist_done"], 1)
            pe.wait_ge(S["hist_tot_ready"], 1)
            pe.matmul(PO[:, 0:2], before[:, :], hist_tot[:, :], start=True, stop=False, skip_group_check=True)
            pe.matmul(PO[:, 1:2], ones[:, :], hist_tot[:, 0:1], start=False, stop=True, skip_group_check=True
                      ).then_inc(S["offsets_ready"], 1)

            pe.wait_ge(S["spread_ready"], 1)
            pe.transpose(PO[0:1, 0:P], max_deg[:, 0:1], ident[:, :]).then_inc(S["spread_t"], 1)

            pe.wait_ge(S["starts_ready"], 1)
            for g in range(2):
                last = pe.matmul(PO[0:P - 1, g:g + 1], ident[:, 1:P], starts[:, g, 0:1], start=g == 0, stop=g == 1,
                                 skip_group_check=True)
            last.then_inc(S["boundary_ready"], 1)
            pe.wait_ge(S["degree_ready"], 1)
            pe.transpose(TA[0][:, 0:P], starts[:, 0, 0:P], ident[:, :])
            for g in range(2):
                last = pe.transpose(TA[0][:, (1 + g) * P:(2 + g) * P], degree[:, g, :], ident[:, :])
            last.then_inc(S["starts_turned"], 1)
            pe.wait_ge(S["max_deg_ready"], 1)
            pe.transpose(PO[0:1, 0:P], max_deg[:, 0:1], ident[:, :]).then_inc(S["max_deg_t"], 1)

            with pe.Fori(0, FFN_CHUNKS) as n:
                experts(n)

        @block.scalar
        def _(act):
            act.wait_ge(S["consts"], 11)

            def norm_chunk(n, k):
                if n >= 2:
                    act.wait_ge(S["yt_ready"], n - 1)
                for t in range(TPC):
                    tt = TPC * k + t
                    last = act.activation(Y[n % 2][:, t, :], x_tiles[:, tt, :], ACT.Identity,
                                          scale=rstd[:, tt:tt + 1], bias=shift[:, tt:tt + 1])
                last.then_inc(S["y_ready"], 1)

            def norm_step1(g):
                act.wait_ge(S["norm_ready"], 2 * g + 1)
                for k in range(CHUNKS + 2):
                    n = g * 2 * CHUNKS + k
                    if k < CHUNKS:
                        norm_chunk(n, k)
                        for t in range(TPC):
                            tt = TPC * k + t
                            last = act.activation(x_tiles[:, tt, :], x_tiles[:, tt, :], ACT.Identity,
                                                  scale=rstd1[:, tt:tt + 1], bias=shift[:, tt:tt + 1])
                        last.then_inc(S["xres_ready"], 1)
                    if 1 <= k <= CHUNKS:
                        act.wait_ge(S["yt_ready"], n)
                        if k >= 3:
                            act.wait_ge(S["step1_ready"], g * CHUNKS + k - 2)
                        act.activation(YT[(n - 1) % 2], TA[(n - 1) % 2][:, :], ACT.Copy).then_inc(S["yt_out"], 1)
                    if k >= 2:
                        c = k - 2
                        j = g * CHUNKS + c
                        act.wait_ge(S["step1_ready"], j + 1)
                        if c == 0 and g:
                            act.wait_ge(S["dz_out"], g * 12)
                        r0 = 1 + (IMG_H // 2) * (c % 2)
                        act.activation(A1[:, c // 2, r0:r0 + IMG_H // 2, 1:1 + IMG_W],
                                       MB[j % 2][:, :].rearrange("p (a b) -> p a b", b=IMG_W),
                                       ACT.Relu, bias=e1_bias[:, :]).then_inc(S["a1_out"], 1)

            def norm_nodes(g):
                act.wait_ge(S["norm_ready"], 2 * g + 2)
                for k in range(CHUNKS + 2):
                    n = g * 2 * CHUNKS + CHUNKS + k
                    if k < CHUNKS:
                        norm_chunk(n, k)
                    if 1 <= k <= CHUNKS:
                        tok = (g * CHUNKS + k - 1) * CHUNK
                        act.wait_ge(S["yt_ready"], n)
                        act.activation(XT[:, tok:tok + CHUNK], TA[(n - 1) % 2][:, :], ACT.Copy
                                       ).then_inc(S["yt_out"], 1)
                    if k >= 2:
                        c = k - 2
                        j = g * CHUNKS + c
                        act.wait_ge(S["node_ready"], j + 1)
                        if c == 0 and g:
                            act.wait_ge(S["node_stored"], 32 * g)
                        act.activation(node_out[:, TPC * c:TPC * (c + 1), :],
                                       MB[j % 2][:, :].rearrange("p (t n) -> p t n", n=P)[:, :, 0:2 * HEADS + HE],
                                       ACT.Copy).then_inc(S["node_out_done"], 1)

            def roots(n):
                act.wait_ge(S["var_ready"], n + 1)
                act.activation(std[:, :], std[:, :], ACT.Sqrt).then_inc(S["std_ready"], 1)

            for g in range(GROUPS):
                roots(2 * g)
                norm_step1(g)
                for i in range(4):
                    act.wait_ge(S["conv_stage"], g * 4 + i + 1)
                    if i == 0 and g == GROUPS - 1:
                        act.wait_ge(S["zeros_stored"], 32)
                    for q in range(IMGS):
                        if i < 3:
                            act.wait_ge(S["dz_out"], g * 12 + 4 * i + q + 1)
                        tok = g * TILES * P + q * IMG_H * IMG_W
                        act.activation(XT[QUAD * i:QUAD * (i + 1), tok:tok + IMG_H * IMG_W],
                                       Z[QUAD * q:QUAD * (q + 1), :, :].rearrange("p h n -> p (h n)"),
                                       ACT.Relu, bias=cb2[QUAD * q:QUAD * (q + 1), :]).then_inc(S["relu_out"], 1)
                roots(2 * g + 1)
                norm_nodes(g)

            def experts(gg, h):
                n = gg * 2 + h
                for m in range(8):
                    act.wait_ge(S["hid_ready"], n * 8 + m + 1)
                    act.activation(HH[:, m, :], PF[m % 2][:, :], ACT.Gelu, bias=b1c[:, m:m + 1]
                                   ).then_inc(S["hid_out"], 1)
                act.wait_ge(tail_done[h], gg + 1)
                for t in range(TPC):
                    act.wait_ge(S["exp_ready"], n * TPC + t + 1)
                    act.activation(YE[h][:, t, :], Z[:, t % 2, :], ACT.Copy).then_inc(S["exp_out"], 1)

            for n in range(EVACS):
                act.wait_ge(S["keys_transposed"], n + 1)
                act.activation(keys_t[:, BANK_T * n:BANK_T * (n + 1), :],
                               TA[n % 2][:, :].rearrange("p (q c) -> p q c", c=P), ACT.Copy
                               ).then_inc(S["keys_evacuated"], 1)

            act.wait_ge(S["init_args"], 1)
            act.activation(tmp_a, tmp_a, ACT.Exp)
            act.activation(tmp_b, tmp_b, ACT.Exp).then_inc(S["init_exps"], 1)

            def store_result(gg, h):
                act.wait_ge(tail_done[h], gg + 2)
                act.dma_start(out_chunks[gg * 2 + h], tail_x[h]).then_inc(tail_out[h], 16)

            act.sem_inc(S["hid_out"], 2)
            act.sem_inc(S["exp_out"], 2)
            rounds = slot_rounds(act)
            with act.Fori(0, PAIRS) as gg:
                for h in range(2):
                    experts(gg, h)
                    if h:
                        store_result(gg, 0)
                    n = gg * 2 + h
                    with act.Fori(0, rounds) as r:
                        act.wait_ge(S["e_ready"], n * rounds + r + 1)
                        act.activation(e_buf, e_buf, ACT.Exp).then_inc(S["e_exp"], 1)
                    act.wait_ge(S["score_var"], n + 1)
                    act.activation(g4[0], g4[0], ACT.Sqrt).then_inc(S["score_std"], 1)
                    act.wait_ge(S["logits_ready"], n + 1)
                    act.activation(weight_g, weight_g, ACT.Exp).then_inc(S["logits_exp"], 1)
                store_result(gg, 1)
            for h in range(2):
                act.wait_ge(tail_out[h], 16 * (1 + PAIRS))

        @block.vector
        def _(dve):
            chain = [0]

            def link(ins):
                chain[0] += 1
                ins.then_inc(S["dve_chain"], 1)
                dve.wait_ge(S["dve_chain"], chain[0])

            tt, ts, stt, cp, red = (dve.tensor_tensor, dve.tensor_scalar, dve.scalar_tensor_tensor,
                                    dve.tensor_copy, dve.tensor_reduce)
            dve.wait_ge(S["consts"], 11)

            def normalise(n, eps):
                for t in range(TILES):
                    last = dve.bn_aggr(mean_var[:, t, :], bn[:, t, :])
                link(last)
                ts(std[:, :], mean_var[:, :, 1], eps, None, ALU.add).then_inc(S["var_ready"], 1)
                dve.wait_ge(S["std_ready"], n + 1)
                link(dve.reciprocal(rstd[:, :], std[:, :]))
                link(ts(rstd1[:, :], rstd[:, :], 1.0, None, ALU.add))
                link(tt(shift[:, :], mean_var[:, :, 0], rstd[:, :], ALU.mult))
                ts(shift[:, :], shift[:, :], -1.0, None, ALU.mult).then_inc(S["norm_ready"], 1)

            def token_stats(g):
                dve.wait_ge(S["x_in"], 16 * (g + 1))
                for t in range(TILES):
                    last = dve.bn_stats(bn[:, t, :], x_tiles[:, t, :])
                link(last)
                if g:
                    dve.wait_ge(S["y_ready"], 2 * CHUNKS * g)
                normalise(2 * g, 1e-6)

            def small_weights():
                dve.wait_ge(S["weights_in"], 16 * (N_WEIGHTS - 1))
                dve.wait_ge(S["comp_pe"], 1)
                cp(comp[:, 0, 0:P], TA[0][0:QUAD, 0:P]).then_inc(S["comp_dve"], 1)
                for i in range(3):
                    dve.wait_ge(S["comp_dve"], 1 + 2 * i)
                    link(cp(comp_d[:, i, 0:P + 1], comp[:, i, 0:P + 1]))
                    blk = comp_d[:, i, QUAD * i:QUAD * (i + 1)]
                    tt(blk, blk, ident[0:QUAD, 0:QUAD], ALU.subtract).then_inc(S["comp_dve"], 1)
                    dve.wait_ge(S["comp_pe"], 2 + i)
                    tt(comp[:, i + 1, 0:P + 1], comp[:, i, 0:P + 1], TA[1][0:QUAD, 0:P + 1], ALU.add
                       ).then_inc(S["comp_dve"], 1)
                dve.wait_ge(S["comp_dve"], 7)
                for i in range(4):
                    link(cp(e1_bias[QUAD * i:QUAD * (i + 1), :], comp[:, i, P:P + 1]))
                dve.wait_ge(S["comp_pe"], 5)
                link(cp(E1[:, :], MB[0][:, 0:P]))
                link(tt(rec_b[:, 1:P], ident[:, 0:P - 1], w3_row[:, 0:P - 1], ALU.mult))
                link(ts(rec_b[:, 1:P], rec_b[:, 1:P], -1.0, None, ALU.mult))
                link(cp(rec_b[:, 0:1], w3_col[:, :]))
                link(dve.memset(rec_a[:, 0:1], 0.0))
                link(ts(rec_a[:, 1:P], w3_row[:, 0:P - 1], 1.0, None, ALU.add))
                link(dve.tensor_tensor_scan(T3[:, :], rec_a, rec_b, 0.0, ALU.mult, ALU.add))
                link(dve.memset(b3_in[0:1, 1:P], 0.0))
                link(dve.tensor_tensor_scan(b3_row[:, :], rec_a[0:1, :], b3_in[:, :], 0.0, ALU.mult, ALU.add))
                for i in range(2):
                    link(tt(att_w[:, i, :], node_w[:, HEADS:HEADS + HE], att[:, i, :], ALU.mult))
                heads = lambda i: att_w[:, i, :].rearrange("p (g x) -> p g x", g=HEADS)
                link(red(node_w[:, 0:HEADS], heads(0), AX.X, ALU.add))
                red(node_w[:, HEADS + HE:], heads(1), AX.X, ALU.add).then_inc(S["comp_dve"], 1)

            def make_keys():
                A, B, Cc = KA[:, :], KB[:, :], KC[:, :]
                Ai, Bi, Ci = A.bitcast(I32), B.bitcast(I32), Cc.bitcast(I32)
                for m in range(8):
                    link(ts(sign_bits[:, m:m + 1], part_i[:, 0:1], m, 1, ALU.logical_shift_right, ALU.bitwise_and))
                link(ts(signs[:, 0:8], sign_bits[:, :], -2.0, 1.0, ALU.mult, ALU.add))
                link(tt(signs[:, 7:9], signs[:, 4:6], signs[:, 5:7], ALU.mult))
                dve.wait_ge(S["edges_in"], 32)
                link(ts(Cc, Ai, 0.0, float(M), ALU.is_lt, ALU.mult))
                link(tt(A, Ai, Cc, ALU.add))
                link(ts(A, A, 0.0, float(M - 1), ALU.max, ALU.min))
                link(ts(Cc, Bi, 0.0, float(4 * M), ALU.is_lt, ALU.mult))
                link(tt(B, Bi, Cc, ALU.max))
                link(ts(Cc, B, float(M), float(2 * M), ALU.is_ge, ALU.mult))
                link(tt(B, B, Cc, ALU.add))
                link(ts(Cc, A, float(M - 1), float(M), ALU.is_equal, ALU.mult))
                link(tt(B, B, Cc, ALU.add))
                link(ts(Bi, B, float(VALID_END), float(KEY_BIAS), ALU.min, ALU.add))
                link(ts(Bi, Bi, SRC_BITS, None, ALU.logical_shift_left))
                link(cp(Ci, A))
                link(tt(Ai, Bi, Ci, ALU.bitwise_or))
                for i, end in enumerate((REAL_END, VALID_END)):
                    link(ts(B, A, key_bits_as_float(end), 0.0, ALU.is_lt, ALU.add, accum_out=key_counts[:, i:i + 1]))
                dve.memset(counts_f[:, :], 0.0).then_inc(S["counted"], 1)

            def totals():
                dve.wait_ge(S["totals_ready"], 1)
                link(cp(key_totals[:, :], MB[0][:, 0:2]))

            def exchange(src, dst, run, stride, n=ROW):
                if 2 * run <= n:
                    def part(b, d, h):
                        return b.rearrange("p (b d g h j) -> p b d g h j", d=2, g=run // (2 * stride), h=2,
                                           j=stride)[:, :, d, :, h, :]
                    turns = (0, 1)
                else:
                    def part(b, d, h):
                        return b.rearrange("p (g h j) -> p g h j", h=2, j=stride)[:, :, h, :]
                    turns = (0,)
                for d in turns:
                    tt(part(dst, d, 0), part(src, d, 0), part(src, d, 1), ALU.max if d else ALU.min)
                    last = tt(part(dst, d, 1), part(src, d, 0), part(src, d, 1), ALU.min if d else ALU.max)
                link(last)

            def row_steps():
                a, b = KA[:, :], KC[:, :]
                stride = ROW // 2
                while stride:
                    exchange(a, b, 2 * ROW, stride)
                    a, b = b, a
                    stride //= 2
                    yield

            def times_sign(col):
                link(ts(KA[:, :], KA[:, :], signs[:, col:col + 1], None, ALU.mult))

            swaps = [0]

            def quadrant_step():
                swaps[0] += 1
                dve.sem_inc(S["swap_ready"], 1)
                yield
                dve.wait_ge(S["swapped"], 64 * swaps[0])
                link(stt(KA[:, :], KB[:, :], -1.0, KA[:, :], ALU.mult, ALU.min))

            def sort_keys():
                a, b = KA[:, :], KC[:, :]
                run = 2
                while run < ROW:
                    stride = run // 2
                    while stride:
                        exchange(a, b, run, stride)
                        a, b = b, a
                        stride //= 2
                        yield
                    run *= 2
                times_sign(0)
                yield from row_steps()
                for m in range(1, LEVELS + 1):
                    if m <= 4:
                        times_sign(m - 1)
                    elif m == 5:
                        times_sign(7)
                    elif m == 6:
                        times_sign(6)
                        yield from quadrant_step()
                        times_sign(5)
                    else:
                        yield from quadrant_step()
                        times_sign(8)
                        yield from quadrant_step()
                        times_sign(5)
                    link(dve.transpose(KC[:, :], KA[:, :]))
                    a, b = KC[:, :], KB[:, :]
                    for s in range(min(m, 5) - 1, -1, -1):
                        exchange(a, b, (1 << m) if m < 5 else ROW, 1 << s)
                        a, b = b, a
                        yield
                    link(dve.transpose(KA[:, :], a))
                    if m <= 4:
                        times_sign(m)
                    yield from row_steps()
                dve.sem_inc(S["rows_sorted"], 1)

            sorting = sort_keys()

            def sort_steps(n):
                for _ in range(n):
                    next(sorting, None)

            small_weights()
            token_stats(0)
            make_keys()
            for g in range(GROUPS):
                if g:
                    token_stats(g)
                sort_steps(18)
                for i in range(3):
                    dve.wait_ge(S["conv_stage"], g * 4 + i + 1)
                    if i == 0:
                        dve.wait_ge(S["a1_out"], CHUNKS * (g + 1))
                    for q in range(IMGS):
                        r = slice(QUAD * i, QUAD * (i + 1))
                        stt(DZ[r, q, 1:1 + IMG_H, 1:1 + IMG_W],
                            Z[QUAD * q:QUAD * (q + 1), :, :].rearrange("p h (a b) -> p (h a) b", b=IMG_W),
                            cb2[QUAD * q:QUAD * (q + 1), :], A1[r, q, 1:1 + IMG_H, 1:1 + IMG_W],
                            ALU.add, ALU.subtract).then_inc(S["dz_out"], 1)
                    sort_steps(7)
                for c in range(CHUNKS):
                    j = g * CHUNKS + c
                    dve.wait_ge(S["step3_ready"], j + 1)
                    dve.wait_ge(S["xres_ready"], j + 1)
                    flat = XG[:, c * CHUNK:(c + 1) * CHUNK]
                    tt(flat, flat, MB[j % 2][:, :], ALU.add).then_inc(S["x1_ready"], 1)
                    dve.wait_ge(S["x1_ready"], j + 1)
                    for t in range(TPC):
                        last = dve.bn_stats(bn[:, TPC * c + t, :], x_tiles[:, TPC * c + t, :])
                link(last)
                dve.wait_ge(S["y_ready"], 2 * CHUNKS * g + CHUNKS)
                normalise(2 * g + 1, 1e-5)
                if g == 0:
                    totals()
                sort_steps(8)
            sort_steps(ROW)

            dve.wait_ge(S["keys_evacuated"], EVACS)
            ts(KB[:, :].bitcast(I32), KB[:, :].bitcast(I32), (1 << SRC_BITS) - 1, None, ALU.bitwise_and
               ).then_inc(S["sources_ready"], 1)

            dve.memset(end_keys, key_bits_as_float(VALID_END)).then_inc(S["end_keys_ready"], 1)
            link(cp(iota_f[:, :], iota_i[:, :]))
            link(ts(thresholds[:, :].bitcast(I32), win_i[:, :], SRC_BITS, None, ALU.logical_shift_left))
            link(ts(piv_i[:, 0, :], KA[:, ::STRIDE].bitcast(I32), SRC_BITS, None, ALU.logical_shift_right))
            link(ts(piv_i[:, 1, :], piv_i[:, 0, :], float(-KEY_BIAS), None, ALU.add))
            link(ts(piv_i[:, 0, :], piv_i[:, 1, :], 7, None, ALU.logical_shift_right))
            link(ts(piv_i[:, 2, :], piv_i[:, 1, :], P - 1, None, ALU.bitwise_and))
            link(cp(piv_f[:, 0, :], piv_i[:, 0, :]))
            link(cp(piv_f[:, 1, :], piv_i[:, 2, :]))
            for t in range(PIVOTS):
                if t >= 2:
                    dve.wait_ge(S["hist_done"], t - 1)
                ts(hot_hi[:, t % 2, :], iota_f[:, :], piv_f[:, 0, t:t + 1], None, ALU.is_equal)
                ts(hot_lo[:, t % 2, :], iota_f[:, 0:P], piv_f[:, 1, t:t + 1], None, ALU.is_equal
                   ).then_inc(S["hot_ready"], 1)
            dve.wait_ge(S["hist_done"], PIVOTS)
            link(cp(hist[:, :, :], H))
            for g in range(2):
                link(dve.tensor_tensor_scan(cum[:, g, :], ones[:, :], hist[:, g, :], 0.0, ALU.mult, ALU.add))
            cp(hist_tot[:, :], cum[:, :, P - 1]).then_inc(S["hist_tot_ready"], 1)
            dve.wait_ge(S["offsets_ready"], 1)
            link(cp(hist_off[:, :], PO[:, 0:2]))
            for g in range(2):
                link(stt(cum[:, g, :], cum[:, g, :], hist_off[:, g:g + 1], hist[:, g, :], ALU.add, ALU.subtract))
            link(ts(win_f[:, :], cum[:, :, :].rearrange("p g l -> p (g l)"), -1.0, 0.0, ALU.add, ALU.max))
            shared = lambda ap: ap.rearrange("p (c j) -> p c j", j=SHARE)
            first_win = shared(win_f[:, :])[:, :, 0]
            link(cp(win_at, first_win))
            link(tt(win_i[:, 0:GROUPS_OF_NODES], shared(win_f[:, :])[:, :, SHARE - 1], first_win, ALU.subtract))
            red(max_deg[:, :], win_i[:, 0:GROUPS_OF_NODES], AX.X, ALU.max).then_inc(S["spread_ready"], 1)
            dve.wait_ge(S["spread_ready"], 1)
            cp(win_i[:, 0:GROUPS_OF_NODES], win_at).then_inc(S["win_idx_ready"], 1)
            dve.wait_ge(S["spread_t"], 1)
            n = counts_f[0:1, 2:3]
            link(red(n, PO[0:1, 0:P], AX.X, ALU.max))
            link(ts(n, n, 1.0 / SPAN, 0.5 + 0.5 / SPAN, ALU.mult, ALU.add))
            link(ts(n, n, ROUND_MAGIC, None, ALU.add))
            link(ts(n, n, -ROUND_MAGIC, 1.0, ALU.add, ALU.max))
            cp(counts_i[0:1, 2:3], n).then_inc(S["window_rounds_ready"], 1)

            counted = hist[:, :, :].rearrange("p g l -> p (g l)")
            link(dve.memset(counted, 0.0))
            dve.sem_inc(S["windows_counted"], 2)
            WINDOW_OPS = WIN_BATCHES * (2 * SHARE + 1) + 2
            with dve.Fori(0, window_rounds(dve)) as r:
                done = [0]

                def window_link(ins):
                    done[0] += 1
                    ins.then_inc(S["window_chain"], 1)
                    dve.wait_ge(S["window_chain"], r * WINDOW_OPS + done[0])

                for b in range(WIN_BATCHES):
                    dve.wait_ge(win_in[b % 2], r * (WIN_BATCHES // 2 * 16 * WIN_COLS) + (b // 2 + 1) * 16 * WIN_COLS)
                    cols = slice(WIN_COLS * SHARE * b, WIN_COLS * SHARE * (b + 1))
                    for j in range(SHARE):
                        window_link(tt(below, windows[b % 2], bc(shared(thresholds[:, cols])[:, :, j], 2,
                                                                 [P, WIN_COLS, WINDOW]), ALU.is_lt))
                        window_link(red(found[:, :, j], below, AX.X, ALU.add))
                    dve.sem_inc(S["windows_counted"], 1)
                    window_link(tt(shared(counted[:, cols]), shared(counted[:, cols]), found, ALU.add))
                window_link(ts(win_at, win_at, float(SPAN), float(E // STRIDE), ALU.add, ALU.min))
                window_link(cp(win_i[:, 0:GROUPS_OF_NODES], win_at))
                assert done[0] == WINDOW_OPS
                dve.sem_inc(S["win_idx_ready"], 1)
            for g in range(2):
                cp(starts[:, g, P:P + 1], key_totals[:, g:g + 1])
                last = stt(shared(starts[:, g, 0:P]),
                           bc(shared(win_f[:, g * P:(g + 1) * P])[:, :, 0], 2, [P, P // SHARE, SHARE]), float(STRIDE),
                           shared(hist[:, g, :]), ALU.mult, ALU.add)
            last.then_inc(S["starts_ready"], 1)

            dve.wait_ge(S["nodes_in"], 48)
            link(tt(tmp_a, node_rows[:, :, 0:HEADS], a_dst, ALU.add))
            link(tt(tmp_b, bc(last_row[:, 0:HEADS], 1, [P, P, HEADS]), a_dst, ALU.add))
            link(stt(tmp_a, tmp_a, 0.2, tmp_a, ALU.mult, ALU.max))
            link(stt(tmp_b, tmp_b, 0.2, tmp_b, ALU.mult, ALU.max))
            dve.wait_ge(S["boundary_ready"], 1)
            link(cp(starts[0:P - 1, :, P], PO[0:P - 1, 0:2]))
            tt(degree[:, :, :], starts[:, :, 1:P + 1], starts[:, :, 0:P], ALU.subtract).then_inc(S["degree_ready"], 1)
            dve.wait_ge(S["degree_ready"], 1)
            red(max_deg[:, :], degree[:, 0, :], AX.X, ALU.max).then_inc(S["max_deg_ready"], 1)
            dve.wait_ge(S["max_deg_t"], 1)
            n = counts_f[0:1, 1:2]
            link(red(n, PO[0:1, 0:P], AX.X, ALU.max))
            link(ts(n, n, 1.0 / SLOTS, 0.5 - 0.5 / SLOTS, ALU.mult, ALU.add))
            link(ts(n, n, ROUND_MAGIC, None, ALU.add))
            link(ts(n, n, -ROUND_MAGIC, 1.0, ALU.add, ALU.max))
            cp(counts_i[0:1, 1:2], n).then_inc(S["rounds_ready"], 1)
            dve.wait_ge(S["starts_turned"], 1)
            link(dve.memset(starts_t[:, P:], 0.0))
            cp(degree[:, :, :], TA[0][:, P:3 * P].rearrange("p (g l) -> p g l", l=P))
            cp(starts_t[:, 0:P], TA[0][:, 0:P])
            link(cp(starts_t[:, P:P + 1], key_totals[:, 0:1]))
            ends = trip_f[:, 1:]
            link(ts(ends, starts_t[0:1, NODES::NODES], 1.0 / PER_TRIP, 0.5 - 0.5 / PER_TRIP, ALU.mult, ALU.add))
            link(ts(ends, ends, ROUND_MAGIC, None, ALU.add))
            link(ts(ends, ends, -ROUND_MAGIC, 1.0, ALU.add, ALU.add))
            n = counts_f[0:1, 0:1]
            link(ts(n, trip_f[:, NODE_GROUPS:], float(-EARLY - MIDDLE), 0.0, ALU.add, ALU.max))
            link(ts(n, n, 1.0 / NODE_GROUPS, None, ALU.mult))
            link(ts(spread[:, :], iota_f[0:1, 1:NODE_GROUPS + 1], n, float(EARLY + MIDDLE), ALU.mult, ALU.add))
            link(ts(spread[:, :], spread[:, :], ROUND_MAGIC, None, ALU.add))
            link(ts(spread[:, :], spread[:, :], -ROUND_MAGIC, None, ALU.add))
            link(tt(spread[:, :], spread[:, :], ends, ALU.max))
            link(dve.memset(trip_f[:, 0:1], float(EARLY + MIDDLE)))
            link(dve.tensor_tensor_scan(ends, ones[0:1, 0:NODE_GROUPS], spread[:, :], float(EARLY + MIDDLE),
                                        ALU.add, ALU.max))
            cp(trip_i[:, :], trip_f[:, :]).then_inc(S["table_ready"], 1)

            link(ts(beat[:, :], degree[:, 1, :], 0.5, -2 * NEG, ALU.is_gt, ALU.mult))
            link(ts(beat[:, :], beat[:, :], NEG, None, ALU.add))
            link(tt(tmp_b, tmp_b, bc(beat[:, :], 2, [P, P, HEADS]), ALU.min))
            link(tt(run_max, tmp_a, tmp_b, ALU.max))
            link(tt(tmp_a, tmp_a, run_max, ALU.subtract))
            tt(tmp_b, tmp_b, run_max, ALU.subtract).then_inc(S["init_args"], 1)
            dve.wait_ge(S["init_exps"], 1)
            per_head = [P, P, HEADS, EXPERTS]
            link(tt(tmp_b, tmp_b, bc(degree[:, 1, :], 2, [P, P, HEADS]), ALU.mult))
            link(tt(denom, tmp_a, tmp_b, ALU.add))
            link(tt(by_head(agg), by_head(node_rows[:, :, HEADS:]), bc(tmp_a, 3, per_head), ALU.mult))
            link(tt(by_head(tmp16), by_head(bc(last_row[:, HEADS:], 1, [P, P, HE])), bc(tmp_b, 3, per_head),
                    ALU.mult))
            link(tt(agg, agg, tmp16, ALU.add))
            link(cp(slot_iota[:, :], iota_f[:, 0:SLOTS]))
            link(ts(lower_i[:, 0, :], iota_i[:, 0:HE], 2, None, ALU.logical_shift_right))
            link(ts(lower_i[:, 1, :], iota_i[:, 0:HE], EXPERTS - 1, None, ALU.bitwise_and))
            link(tt(lower[:, :], lower_i[:, 1, :], lower_i[:, 0, :], ALU.is_lt))

            rounds = slot_rounds(dve)

            def waits_done():
                dve.sem_inc(S["vector_turns"], 1)

            def chained(sem_, base):
                done = [0]

                def chain_link(ins):
                    done[0] += 1
                    ins.then_inc(sem_, 1)
                    dve.wait_ge(sem_, base + done[0])

                return chain_link, done

            for h in range(2):
                dve.sem_inc(slots_used[h], 1)
                dve.sem_inc(tail_done[h], 1)
            link(dve.memset(ends_t[:, P:], 0.0))
            link(tt(ends_t[:, 0:P], starts_t[:, 0:P], degree[:, 0, :], ALU.add))
            cp(slot_end[0][:, :], ends_t[:, 0:NODES])
            link(cp(slot_at[0][:, :], starts_t[:, 0:NODES]))
            cp(slot_idx[0][:, :], slot_at[0][:, :]).then_inc(slot_idx_ready[0], 1)
            SLOT_OPS, GROUP_OPS = 11, 28
            with dve.Fori(0, PAIRS) as gg:
                for h in range(2):
                    n = gg * 2 + h
                    cols = bass.ds(n * NODES, NODES)
                    group_link, group_done = chained(S["group_chain"], n * GROUP_OPS)
                    nxt = bass.ds(n * NODES + NODES, NODES)
                    ts(slot_at[1 - h][:, :], starts_t[:, nxt], 0.0, None, ALU.add)
                    group_link(ts(slot_end[1 - h][:, :], ends_t[:, nxt], 0.0, None, ALU.add))
                    cp(slot_idx[1 - h][:, :], slot_at[1 - h][:, :]).then_inc(slot_idx_ready[1 - h], 1)
                    waits_done()
                    with dve.Fori(0, rounds) as r:
                        step = n * rounds + r
                        slot_link, slot_done = chained(S["slot_chain"], step * SLOT_OPS)
                        by_slot = [P, NODES, SLOTS, HEADS]
                        rows = slot_rows[h]
                        e = exps[:, :, 0:SLOTS, :]
                        slot_link(tt(slot_left[:, :], slot_end[h][:, :], slot_at[h][:, :], ALU.subtract))
                        tt(unused, bc(slot_iota[:, :], 1, [P, NODES, SLOTS]), bc(slot_left[:, :], 2, [P, NODES, SLOTS]),
                           ALU.is_ge)
                        slot_link(ts(slot_at[h][:, :], slot_at[h][:, :], float(SLOTS), None, ALU.add))
                        slot_link(tt(slot_next[:, :], slot_end[h][:, :], slot_at[h][:, :], ALU.min))
                        ts(exps[:, :, SLOTS, :], run_max[:, cols, :], 0.0, None, ALU.add)
                        dve.wait_ge(slots_gathered[h], (gg * rounds + r + 1) * (16 * NODES))
                        cp(slot_idx[h][:, :], slot_next[:, :]).then_inc(slot_idx_ready[h], 1)
                        slot_link(tt(e, rows[:, :, 0:SLOTS, 0:HEADS], bc(a_dst[:, cols, :], 2, by_slot), ALU.add))
                        ts(rows[:, :, SLOTS, HEADS:], agg[:, cols, :], 0.0, None, ALU.add)
                        slot_link(stt(e, e, 0.2, e, ALU.mult, ALU.max))
                        slot_link(stt(e, bc(unused, 3, by_slot), NEG, e, ALU.mult, ALU.add))
                        waits_done()
                        slot_link(red(run_max[:, cols, :], exps.rearrange("p c k g -> p c g k"), AX.X, ALU.max))
                        tt(exps, exps, bc(run_max[:, cols, :], 2, [P, NODES, TERMS, HEADS]), ALU.subtract
                           ).then_inc(S["e_ready"], 1)
                        dve.wait_ge(S["e_exp"], step + 1)
                        split = lambda ap: ap.rearrange("p c k (g x) -> p (c k) g x", g=HEADS)
                        slot_link(tt(split(msg), split(rows[:, :, :, HEADS:]),
                                     bc(exps.rearrange("p c k g -> p (c k) g"), 3,
                                        [P, NODES * TERMS, HEADS, EXPERTS]), ALU.mult))
                        so_far = exps[:, :, SLOTS, :]
                        slot_link(tt(so_far, so_far, denom[:, cols, :], ALU.mult))
                        waits_done()
                        red(agg[:, cols, :], msg.rearrange("p c k f -> p c f k"), AX.X, ALU.add
                            ).then_inc(slots_used[h], 1)
                        slot_link(red(denom[:, cols, :], exps.rearrange("p c k g -> p c g k"), AX.X, ALU.add))
                        slot_link(ts(den_g, denom[:, cols, :], 1e-16, None, ALU.add))
                        waits_done()
                    assert slot_done[0] == SLOT_OPS, slot_done

                    per_head = [P, NODES, HEADS, EXPERTS]
                    heads = lambda ap: ap.rearrange("p c (g x) -> p c g x", g=HEADS)
                    par = lambda k: bc(gat_par[:, k, :], 1, [P, NODES, HE])
                    per_node = lambda ap, width: bc(ap, 2, [P, NODES, width])
                    mean, top, total = g4
                    group_link(dve.reciprocal(den_g, den_g))
                    group_link(tt(heads(agg_g), heads(agg[:, cols, :]), bc(den_g, 3, per_head), ALU.mult))
                    group_link(tt(agg_g, agg_g, par(0), ALU.add))
                    group_link(red(mean, agg_g, AX.X, ALU.add))
                    group_link(ts(mean, mean, 1.0 / HE, None, ALU.mult))
                    group_link(tt(agg_g, agg_g, per_node(mean, HE), ALU.subtract))
                    group_link(tt(sq_g, agg_g, agg_g, ALU.mult))
                    group_link(red(mean, sq_g, AX.X, ALU.add))
                    ts(mean, mean, 1.0 / HE, 1e-5, ALU.mult, ALU.add).then_inc(S["score_var"], 1)
                    dve.wait_ge(S["score_std"], n + 1)
                    group_link(dve.reciprocal(mean, mean))
                    group_link(tt(agg_g, agg_g, per_node(mean, HE), ALU.mult))
                    group_link(tt(agg_g, agg_g, par(1), ALU.mult))
                    group_link(tt(agg_g, agg_g, par(2), ALU.add))
                    group_link(red(score_g, agg_g.rearrange("p c (g x) -> p c x g", g=HEADS), AX.X, ALU.add))
                    group_link(ts(score_g, score_g, 1.0 / HEADS, None, ALU.mult))
                    group_link(red(top, score_g, AX.X, ALU.max))
                    tt(weight_g, score_g, per_node(top, EXPERTS), ALU.subtract).then_inc(S["logits_ready"], 1)
                    square = [P, NODES, EXPERTS, EXPERTS]
                    pairs = lambda ap: ap.rearrange("p c (i j) -> p c i j", j=EXPERTS)
                    tt(pairs(greater), bc(score_g, 2, square), bc(score_g, 3, square), ALU.is_gt)
                    group_link(tt(pairs(equal), bc(score_g, 2, square), bc(score_g, 3, square), ALU.is_equal))
                    group_link(tt(equal, equal, bc(lower[:, :], 1, [P, NODES, HE]), ALU.mult))
                    group_link(tt(greater, greater, equal, ALU.add))
                    group_link(red(gate_g, pairs(greater), AX.X, ALU.add))
                    group_link(ts(gate_g, gate_g, 1.5, None, ALU.is_lt))
                    dve.wait_ge(S["logits_exp"], n + 1)
                    group_link(tt(gate_g, gate_g, weight_g, ALU.mult))
                    group_link(red(total, gate_g, AX.X, ALU.add))
                    group_link(dve.reciprocal(total, total))
                    group_link(tt(gate_g, gate_g, per_node(total, EXPERTS), ALU.mult))
                    dve.wait_ge(S["exp_out"], 2 + (n + 1) * TPC)
                    dve.wait_ge(tail_in[h], gg * 16 + 16)
                    for x_ in range(EXPERTS):
                        for t in range(TPC):
                            last = stt(tail_x[h][:, t, :], YE[h][:, t, x_ * C:(x_ + 1) * C],
                                       gate_g[:, t, x_:x_ + 1], tail_x[h][:, t, :], ALU.mult, ALU.add)
                        if x_ < EXPERTS - 1:
                            group_link(last)
                    last.then_inc(tail_done[h], 1)
                    assert group_done[0] == GROUP_OPS, group_done


_INS = ['x', 'L0_conv_w1', 'L0_conv_b1', 'L0_conv_w2', 'L0_conv_b2', 'L0_conv_w3', 'L0_conv_b3', 'L0_ffn_W_gat',
        'L0_ffn_att_src', 'L0_ffn_att_dst', 'L0_ffn_b_gat', 'L0_ffn_ln_gamma', 'L0_ffn_ln_beta', 'L0_ffn_W1',
        'L0_ffn_b1', 'L0_ffn_W2', 'L0_ffn_b2', 'L0_ffn_edge_index']


def kernel(**inputs):
    import numpy as _np
    import concourse.bacc as _bacc
    from concourse import mybir as _mybir
    from concourse.bass_utils import run_bass_kernel_spmd as _run

    nc = _bacc.Bacc("TRN2", target_bir_lowering=False, num_devices=1)
    arrays, args = {}, []
    for name in _INS:
        a = _np.ascontiguousarray(inputs[name])
        arrays[f"in_{name}_dram"] = a
        args.append(nc.dram_tensor(f"in_{name}_dram", a.shape, _mybir.dt.from_np(a.dtype), kind="ExternalInput").ap())
    out = nc.dram_tensor("out_dram", (16, 32, 32, 128), _mybir.dt.float32, kind="ExternalOutput").ap()
    program(nc, *args, out)
    r = _run(nc, [arrays], core_ids=[0])
    return r.results[0]["out_dram"]
```

```python
from contextlib import ExitStack
from itertools import chain

import concourse.bass as bass
from concourse import mybir

F32, I32, BF16 = mybir.dt.float32, mybir.dt.int32, mybir.dt.bfloat16
ALU, ACT, AX = mybir.AluOpType, mybir.ActivationFunctionType, mybir.AxisListType

P = 128
N_IMG, IMG_H, IMG_W, C = 16, 32, 32, 128
M = N_IMG * IMG_H * IMG_W
E = 524288
HEADS, EXPERTS = 4, 4
HE = HEADS * EXPERTS
HID = 2 * C

GROUPS, IMGS = 4, 4
TILES = IMGS * IMG_H * IMG_W // P
CHUNK = 512
CHUNKS = TILES * P // CHUNK
TPC = CHUNK // P
PADH, PADW = IMG_H + 2, IMG_W + 2
QUAD = 32
TAPS = [(dy, dx) for dy in range(3) for dx in range(3)]
FFN_CHUNKS = M // CHUNK

LAST_STEPS = 6
ROW = E // P
LISTS = 2
LROW = ROW // LISTS
LIST = E // LISTS
SRC_BITS = 14
KEY_BIAS = 512
REAL_END, VALID_END = M, 2 * M
BLOCKS = LROW // P
LEVELS = 7
BANK_T = 4
EVACS = BLOCKS // BANK_T
STRIDE = 64
PIVOTS = LROW // STRIDE
SHARE = 8
SPAN = 2
WINDOW = SPAN * STRIDE
GROUPS_OF_NODES = LISTS * 2 * P // SHARE
LIST_WINDOWS = (LIST + WINDOW) // STRIDE
WIN_COLS = 16
WIN_BATCHES = GROUPS_OF_NODES // WIN_COLS

WIDTH = HEADS + HE
COLS = 8
TRIPS = LROW // (2 * COLS)
PER_TRIP = 2 * COLS * P
AFTER_WINDOWS = 4
MIDDLE = 2
SLOTS = 16
NODES = 4
NODE_GROUPS = P // NODES
TERMS = LISTS * SLOTS + 1
NEG = -1e30
ROUND_MAGIC = 12582912.0


def key_bits_as_float(j):
    import numpy as np
    return float(np.array((j + KEY_BIAS) << SRC_BITS, np.int32).view(np.float32))


def program(nc, x, w1, b1, w2, b2, w3, b3, w_gat, att_src, att_dst, b_gat, ln_gamma, ln_beta,
            ffn_w1, ffn_b1, ffn_w2, ffn_b2, edge_index, out):
    ctx = ExitStack()
    with ctx:
        def sb(name, shape, dt=F32):
            return ctx.enter_context(nc.sbuf_tensor(name, shape, dt))

        def ps(name, shape, dt=F32):
            return ctx.enter_context(nc.psum_tensor(name, shape, dt))

        def sem(name):
            return ctx.enter_context(nc.semaphore(name))

        def bc(ap, axis, shape):
            return ap.unsqueeze(axis).to_broadcast(shape)

        x1_dram = nc.dram_tensor("x1_dram", [M, C], F32).ap()
        node_dram = nc.dram_tensor("node_dram", [M, WIDTH], F32).ap()
        adst_dram = nc.dram_tensor("adst_dram", [M, HEADS], F32).ap()
        keys_dram = nc.dram_tensor("keys_dram", [LISTS * (LIST + WINDOW)], F32).ap()
        payload = [nc.dram_tensor(f"payload{a}", [LIST + SLOTS, WIDTH], F32).ap() for a in range(LISTS)]

        KA, KB, KC = sb("KA", [P, ROW]), sb("KB", [P, ROW]), sb("KC", [P, ROW])
        XT = sb("XT", [P, M])
        XG = sb("XG", [P, TILES * C])
        ARENA_A = sb("ARENA_A", [P, IMGS * PADH * PADW])
        ARENA_D = sb("ARENA_D", [P, IMGS * PADH * PADW])
        ARENA_Y = sb("ARENA_Y", [P, 4 * CHUNK])
        x_tiles = XG[:, :].rearrange("p (t c) -> p t c", c=C)
        A1 = ARENA_A[:, :].rearrange("p (i a b) -> p i a b", i=IMGS, b=PADW)
        DZ = ARENA_D[:, :].rearrange("p (i a b) -> p i a b", i=IMGS, b=PADW)
        Y = [ARENA_Y[:, i * CHUNK:(i + 1) * CHUNK].rearrange("p (t c) -> p t c", c=C) for i in range(2)]
        YT = [ARENA_Y[:, (2 + i) * CHUNK:(3 + i) * CHUNK] for i in range(2)]
        HH = ARENA_A[:, 0:8 * CHUNK].rearrange("p (m n) -> p m n", n=CHUNK)
        YE = [ARENA_D[:, h * 2048:(h + 1) * 2048].rearrange("p (t n) -> p t n", n=CHUNK) for h in range(2)]
        zeros = XT[:, (GROUPS - 1) * TILES * P:(GROUPS - 1) * TILES * P + P * WIDTH]
        node_rows = XG[:, 0:P * WIDTH].rearrange("p (l f) -> p l f", f=WIDTH)

        def node4(arena, at):
            return arena[:, at:at + P * HEADS].rearrange("p (l g) -> p l g", g=HEADS)

        a_dst, run_max, denom = (node4(XG, P * WIDTH + i * P * HEADS) for i in range(3))
        agg = ARENA_Y[:, 0:P * HE].rearrange("p (l f) -> p l f", f=HE)
        tmp16 = KA[:, 0:P * HE].rearrange("p (l f) -> p l f", f=HE)
        tmp_a, tmp_b = node4(KA, P * HE), node4(KA, P * HE + P * HEADS)
        slot_rows = [k[:, at:at + NODES * TERMS * WIDTH].rearrange("p (c k w) -> p c k w", c=NODES, w=WIDTH)
                     for k, at in ((KA, 0), (KC, 320))]
        tail_x = [KC[:, 2960 + h * CHUNK:2960 + (h + 1) * CHUNK].rearrange("p (t c) -> p t c", c=C) for h in range(2)]
        e_buf = KB[:, 0:NODES * TERMS * HEADS]
        exps = e_buf.rearrange("p (c k g) -> p c k g", c=NODES, g=HEADS)
        unused = KB[:, 640:640 + NODES * LISTS * SLOTS].rearrange("p (c k) -> p c k", k=SLOTS)
        g4 = [KB[:, 1024 + 4 * i:1028 + 4 * i] for i in range(3)]
        den_g, score_g, weight_g, gate_g = (KB[:, 1040 + 16 * i:1056 + 16 * i].rearrange("p (c x) -> p c x", c=NODES)
                                            for i in range(4))
        agg_g, sq_g, greater, equal = (KB[:, 1104 + 64 * i:1168 + 64 * i].rearrange("p (c f) -> p c f", c=NODES)
                                       for i in range(4))
        starts = ARENA_D[:, 4096:4096 + LISTS * 2 * (P + 1)].rearrange("p (g l) -> p g l", l=P + 1)
        degree = KA[:, 3072:3072 + LISTS * 2 * P].rearrange("p (g l) -> p g l", l=P)
        win_f = KC[:, 320:320 + LISTS * 2 * P]
        windows = [KA[:, i * 2048:(i + 1) * 2048].rearrange("p (c w) -> p c w", w=WINDOW) for i in range(2)
                   ] + [ARENA_A[:, i * 2048:(i + 1) * 2048].rearrange("p (c w) -> p c w", w=WINDOW) for i in range(2)]
        below = KC[:, 1024:1024 + WIN_COLS * WINDOW].rearrange("p (c w) -> p c w", w=WINDOW)
        win_at = KC[:, 3072:3072 + GROUPS_OF_NODES]
        found = KC[:, 3200:3200 + WIN_COLS * SHARE].rearrange("p (c j) -> p c j", j=SHARE)
        end_keys = KC[0:1, 3328:3328 + WINDOW]

        ident, ones = sb("ident", [P, P]), sb("ones", [P, P])
        before = sb("before", [P, P])
        signs, part_i = sb("signs", [P, 9]), sb("part_i", [P, 1], I32)
        sign_bits = sb("sign_bits", [P, 8], I32)
        cw1, cw1_blocks = sb("cw1", [P, QUAD]), sb("cw1_blocks", [QUAD, 4, QUAD])
        comp, comp_d = (KC[0:QUAD, i * 1024:i * 1024 + 4 * (P + 4)].rearrange("p (i n) -> p i n", i=4) for i in range(2))
        w3_row, rec_a, rec_b = (KC[:, 2048 + i * P:2048 + (i + 1) * P] for i in range(3))
        E1, e1_bias = sb("E1", [P, P]), sb("e1_bias", [P, 1])
        cw2, cb2 = sb("cw2", [P, 9, QUAD]), sb("cb2", [P, 1])
        cw2_of = [sb(f"cw2_of{i}", [P, 9, QUAD]) for i in range(3)]
        w3_col, b3_in = sb("w3_col", [P, 1]), sb("b3_in", [1, P])
        T3, b3_row = sb("T3", [P, P]), sb("b3_row", [1, P])
        node_w = sb("node_w", [P, 2 * HEADS + HE])
        att, att_w = sb("att", [P, 2, HE]), sb("att_w", [P, 2, HE])
        W1, b1c = sb("W1", [P, EXPERTS, HID]), sb("b1c", [P, 8])
        W2, b2r = sb("W2", [P, 8, C]), sb("b2r", [1, EXPERTS * C])
        bn, mean_var = sb("bn", [P, TILES, 6]), sb("mean_var", [P, TILES, 2])
        rstd, rstd1, shift, std = (sb(n, [P, TILES]) for n in ("rstd", "rstd1", "shift", "std"))
        node_out = sb("node_out", [P, TILES, 2 * HEADS + HE])
        key_counts, key_totals = sb("key_counts", [P, 2 * LISTS]), sb("key_totals", [P, 2 * LISTS])
        counts_f, counts_i = sb("counts_f", [1, 4]), sb("counts_i", [1, 4], I32)
        iota_i, iota_f = sb("iota_i", [P, 2 * P], I32), sb("iota_f", [P, 2 * P])
        piv_i, piv_f = sb("piv_i", [P, 3, PIVOTS], I32), sb("piv_f", [P, 2, PIVOTS])
        hot_hi, hot_lo = sb("hot_hi", [P, 2, 2 * P], BF16), sb("hot_lo", [P, 2, P], BF16)
        hist = sb("hist", [P, 2, P])
        counted = [hist[:, :, :].rearrange("p g l -> p (g l)"), KC[:, 3840:3840 + 2 * P]]
        cum = KC[:, 3584:3584 + 2 * P].rearrange("p (g l) -> p g l", l=P)
        hist_tot, hist_off = sb("hist_tot", [P, 2]), sb("hist_off", [P, 2])
        win_i, thresholds = sb("win_i", [P, 2 * P], I32), sb("thresholds", [P, 2 * P])
        last_degree, max_deg = sb("last_degree", [P, P]), sb("max_deg", [P, 1])
        src_buf = [sb(f"src_buf{h}", [P, COLS], I32) for h in range(2)]
        row_buf = [KC[:, h * COLS * WIDTH:(h + 1) * COLS * WIDTH].rearrange("p (t f) -> p t f", f=WIDTH) for h in range(2)]
        last_row = sb("last_row", [P, WIDTH])
        slot_iota = sb("slot_iota", [P, SLOTS])
        starts_t, ends_t = (sb(n, [P, P + NODES, LISTS]) for n in ("starts_t", "ends_t"))
        slot_at, slot_end = ([sb(f"{n}{h}", [P, NODES * LISTS]) for h in range(2)] for n in ("slot_at", "slot_end"))
        slot_left, slot_next = sb("slot_left", [P, NODES * LISTS]), sb("slot_next", [P, NODES * LISTS])
        slot_idx = [sb(f"slot_idx{h}", [P, NODES * LISTS], I32) for h in range(2)]
        trip_f, trip_i = sb("trip_f", [1, NODE_GROUPS + 1]), sb("trip_i", [1, NODE_GROUPS + 1], I32)
        spread = sb("spread", [1, NODE_GROUPS])
        lower_i, lower = sb("lower_i", [P, 2, HE], I32), sb("lower", [P, HE])
        gat_par = sb("gat_par", [P, 3, HE])
        beat = sb("beat", [P, P])

        TA = [ps(f"TA{i}", [P, CHUNK]) for i in range(2)]
        MB = [ps(f"MB{i}", [P, CHUNK]) for i in range(2)]
        Z = ps("Z", [P, 2, CHUNK])
        PF = [ps(f"PF{i}", [P, CHUNK]) for i in range(2)]
        H = MB[0][:, 0:2 * P].rearrange("p (g l) -> p g l", l=P)
        PO = MB[1]

        names = """weights_in consts edges_in x_in comp_pe comp_dve
            var_ready std_ready norm_ready y_ready xres_ready yt_ready yt_out step1_ready a1_out
            conv_stage dz_out relu_out step3_ready x1_ready node_ready node_out_done node_stored x1_stored
            zeros_stored hid_ready hid_out exp_ready exp_out
            dve_chain counted totals_ready trips_ready
            rows_sorted keys_transposed keys_evacuated keys_stored sources_ready
            hot_ready hist_done hist_tot_ready offsets_ready spread_ready spread_t window_rounds_ready win_idx_ready
            windows_counted window_chain starts_ready end_keys_ready
            boundary_ready max_deg_ready max_deg_t rounds_ready
            gpsimd_turns nodes_in init_args init_exps slot_chain group_chain vector_turns sync_turns
            degree_ready starts_turned table_ready e_ready e_exp
            score_var score_std logits_ready logits_exp""".split()
        S = {n: sem(n) for n in names}
        swap_ready, swapped = ([sem(f"{n}{a}") for a in range(LISTS)] for n in ("swap_ready", "swapped"))
        src_copied, rows_gathered, rows_stored = (
            [[sem(f"{n}{a}{h}") for h in range(2)] for a in range(LISTS)]
            for n in ("src_copied", "rows_gathered", "rows_stored"))
        slot_idx_ready, slots_gathered, slots_used, tail_in, tail_done, tail_out = (
            [sem(f"{n}{h}") for h in range(2)]
            for n in ("slot_idx_ready", "slots_gathered", "slots_used", "tail_in", "tail_done", "tail_out"))
        win_in = [sem(f"win_in{i}") for i in range(WIN_BATCHES)]
        block = ctx.enter_context(nc.Block())

        x_groups = x.rearrange("b h w c -> (b h w) c").rearrange("(g t p) c -> g p t c", t=TILES, p=P)
        x1_groups = x1_dram.rearrange("(g t p) c -> g p t c", t=TILES, p=P)
        x1_chunks = x1_dram.rearrange("(s t p) c -> s p t c", t=TPC, p=P)
        out_chunks = out.rearrange("b h w c -> (b h w) c").rearrange("(s t p) c -> s p t c", t=TPC, p=P)
        node_groups = node_dram.rearrange("(g t p) c -> g p t c", t=TILES, p=P)
        adst_groups = adst_dram.rearrange("(g t p) c -> g p t c", t=TILES, p=P)
        payload_cols = [pl[0:LIST].rearrange("(c t q) f -> c q t f", t=COLS, q=P) for pl in payload]
        key_windows = keys_dram.rearrange("(r w) -> r w", w=STRIDE)
        half = lambda k, a: k[:, a * LROW:(a + 1) * LROW]
        keys_t = [half(KB, a).rearrange("q (p j) -> q j p", j=BLOCKS) for a in range(LISTS)]
        by_head = lambda ap: ap.rearrange("p l (g x) -> p l g x", g=HEADS)
        PAIRS = NODE_GROUPS // 2
        N_WEIGHTS = 24
        NORMS = GROUPS * 2 * CHUNKS

        def first_trips(eng):
            eng.wait_ge(S["trips_ready"], 1)
            return (eng.value_load(counts_i[0:1, 0:1], min_val=1, max_val=TRIPS),
                    eng.value_load(counts_i[0:1, 3:4], min_val=2, max_val=TRIPS + 1))

        def group_trips(eng, g):
            lo, hi = (eng.value_load(trip_i[0:1, bass.ds(g + k, 1)], min_val=MIDDLE + k,
                                     max_val=TRIPS + 1 + NODE_GROUPS) for k in range(2))
            return lo, hi

        def window_rounds(eng):
            eng.wait_ge(S["window_rounds_ready"], 1)
            return eng.value_load(counts_i[0:1, 2:3], min_val=1, max_val=LIST // WINDOW + 1)

        def slot_rounds(eng):
            eng.wait_ge(S["rounds_ready"], 1)
            return eng.value_load(counts_i[0:1, 1:2], min_val=1, max_val=-(-LIST // SLOTS))

        def swap_quadrants(eng, a):
            for n, dist in enumerate((1, 2, 1)):
                eng.wait_ge(swap_ready[a], n + 1)
                for q in range(4):
                    to, frm = QUAD * q, QUAD * (q ^ dist)
                    eng.dma_start(half(KB, a)[to:to + QUAD, :], half(KC if n == 1 else KA, a)[frm:frm + QUAD, :]
                                  ).then_inc(swapped[a], 16)

        @block.sync
        def _(sp):
            sp.dma_start(x_tiles, x_groups[0]).then_inc(S["x_in"], 16)
            edge_rows = edge_index.rearrange("a (p f) -> a p f", p=P)
            sp.dma_start(KA[:, :].bitcast(I32), edge_rows[0]).then_inc(S["edges_in"], 16)
            sp.dma_start(KB[:, :].bitcast(I32), edge_rows[1]).then_inc(S["edges_in"], 16)
            loads = [
                (cw1[:, :], w1.rearrange("a b c n -> (a b c) n")),
                (cw1_blocks[:, :, :], w1.rearrange("a b (j k) n -> k (a b j) n", k=QUAD)),
                (comp[:, 0, P:P + 1], b1.rearrange("a b c n -> n (a b c)")),
                (cw2[:, :, :], w2.rearrange("a b c n -> c (a b) n")),
            ] + [(cb2[QUAD * q:QUAD * (q + 1), :], b2.rearrange("a b c n -> n (a b c)")) for q in range(4)] + [
                (w3_row, w3.rearrange("a b c n -> (a b n) c").to_broadcast([P, P])),
                (w3_col[:, :], w3.rearrange("a b c n -> c (a b n)")),
                (b3_in[0:1, 0:1], b3.rearrange("a b c n -> (a b c) n")),
                (node_w[:, HEADS:HEADS + HE], w_gat),
                (att[:, 0, :], att_src.rearrange("a b -> (a b)").unsqueeze(0).to_broadcast([P, HE])),
                (att[:, 1, :], att_dst.rearrange("a b -> (a b)").unsqueeze(0).to_broadcast([P, HE])),
                (W1[:, :, :], ffn_w1.rearrange("e k n -> k e n")),
                (b1c[:, :], ffn_b1.rearrange("e (m p) -> p (e m)", p=P)),
                (W2[:, 0:4, :], ffn_w2[0:2].rearrange("e (k p) n -> p (e k) n", p=P)),
                (W2[:, 4:8, :], ffn_w2[2:4].rearrange("e (k p) n -> p (e k) n", p=P)),
                (b2r[:, 0:2 * C], ffn_b2[0:2].rearrange("e n -> (e n)").unsqueeze(0)),
                (b2r[:, 2 * C:], ffn_b2[2:4].rearrange("e n -> (e n)").unsqueeze(0)),
            ] + [(gat_par[:, i, :], a.unsqueeze(0).to_broadcast([P, HE]))
                 for i, a in enumerate((b_gat, ln_gamma, ln_beta))]
            for dst, src in loads:
                sp.dma_start(dst, src, allow_slow_non_contiguous=True).then_inc(S["weights_in"], 16)
            assert len(loads) == N_WEIGHTS - 1
            sp.wait_ge(S["consts"], 1)
            for a in range(LISTS):
                sp.dma_start(payload[a][0:LIST].rearrange("(a p b) f -> p a (b f)", p=P, b=P),
                             bc(zeros, 1, [P, LIST // (P * P), P * WIDTH])).then_inc(S["zeros_stored"], 16)
                sp.dma_start(payload[a][LIST:], zeros[0:SLOTS, 0:WIDTH]).then_inc(S["zeros_stored"], 16)
            for g in range(GROUPS):
                sp.wait_ge(S["x1_ready"], CHUNKS * (g + 1))
                sp.dma_start(x1_groups[g], x_tiles).then_inc(S["x1_stored"], 16)
                sp.wait_ge(S["node_out_done"], CHUNKS * (g + 1))
                sp.dma_start(node_groups[g], node_out[:, :, 0:WIDTH]).then_inc(S["node_stored"], 16)
                sp.dma_start(adst_groups[g], node_out[:, :, WIDTH:]).then_inc(S["node_stored"], 16)
                sp.wait_ge(S["x1_stored"], 16 * (g + 1))
                sp.wait_ge(S["y_ready"], 2 * CHUNKS * (g + 1))
                if g + 1 < GROUPS:
                    sp.dma_start(x_tiles, x_groups[g + 1]).then_inc(S["x_in"], 16)
            sp.wait_ge(S["node_stored"], 32 * GROUPS)
            sp.dma_start(node_rows, node_dram.rearrange("(l p) f -> p l f", p=P)).then_inc(S["nodes_in"], 16)
            sp.dma_start(a_dst, adst_dram.rearrange("(l p) f -> p l f", p=P)).then_inc(S["nodes_in"], 16)
            sp.dma_start(last_row[:, :], node_dram[M - 1:M, :].to_broadcast([P, WIDTH])).then_inc(S["nodes_in"], 16)
            sp.wait_ge(S["zeros_stored"], 32 * LISTS)
            for a in range(LISTS):
                for h in range(2):
                    sp.sem_inc(rows_stored[a][h], 16)

            def waited():
                sp.sem_inc(S["sync_turns"], 1)

            def store_rows(a, trip, h):
                sp.wait_ge(rows_gathered[a][h], (trip + 1) * (16 * COLS))
                waited()
                sp.dma_start(payload_cols[a][(trip & (TRIPS - 1)) * 2 + h], row_buf[h][:, :, :]
                             ).then_inc(rows_stored[a][h], 16)

            before_windows, trips = first_trips(sp)
            with sp.Fori(0, before_windows) as i:
                for h in range(2):
                    store_rows(0, i, h)
            sp.wait_ge(S["rows_sorted"], LISTS)
            sp.wait_ge(S["end_keys_ready"], 1)
            for a in range(LISTS):
                base = a * (LIST + WINDOW)
                sp.dma_start(keys_dram[base:base + LIST].rearrange("(p f) -> p f", p=P), half(KA, a)
                             ).then_inc(S["keys_stored"], 16)
                sp.dma_start(keys_dram[base + LIST:base + LIST + WINDOW].unsqueeze(0), end_keys
                             ).then_inc(S["keys_stored"], 16)
            with sp.Fori(before_windows, trips) as i:
                for h in range(2):
                    store_rows(0, i, h)
            store_rows(1, 0, 0)
            with sp.Fori(1, MIDDLE) as i:
                store_rows(1, i - 1, 1)
                store_rows(1, i, 0)
            rounds = slot_rounds(sp)
            sp.wait_ge(S["table_ready"], 1)
            for h in range(2):
                sp.sem_inc(tail_out[h], 16)
            with sp.Fori(0, PAIRS) as gg:
                for h in range(2):
                    lo, hi = group_trips(sp, gg * 2 + h)
                    with sp.Fori(lo, hi) as i:
                        store_rows(1, i - 1, 1)
                        store_rows(1, i, 0)
                    sp.wait_ge(slots_gathered[h], (gg + 1) * rounds * (16 * LISTS * NODES))
                    waited()
                    sp.wait_ge(tail_out[h], gg * 16 + 16)
                    waited()
                    sp.dma_start(tail_x[h], x1_chunks[gg * 2 + h]).then_inc(tail_in[h], 16)
            store_rows(1, hi - 1, 1)
            sp.wait_ge(rows_stored[1][1], 16 + hi * 16)
            waited()

        @block.gpsimd
        def _(pool):
            pool.memset(zeros, 0.0).then_inc(S["consts"], 1)
            pool.memset(ident[:, :], 0.0).then_inc(S["consts"], 1)
            pool.memset(before[:, :], 1.0).then_inc(S["consts"], 1)
            pool.wait_ge(S["consts"], 3)
            pool.affine_select(out=ident[:, :], in_=ident[:, :], compare_op=ALU.not_equal, fill=1.0,
                               base=0, pattern=[[-1, P]], channel_multiplier=1).then_inc(S["consts"], 1)
            pool.affine_select(out=before[:, :], in_=before[:, :], compare_op=ALU.is_gt, fill=0.0,
                               base=0, pattern=[[1, P]], channel_multiplier=-1).then_inc(S["consts"], 1)
            pool.memset(ones[:, :], 1.0).then_inc(S["consts"], 1)
            pool.iota(part_i[:, :], [[0, 1]], 0, 1).then_inc(S["consts"], 1)
            pool.iota(iota_i[:, :], [[1, 2 * P]], 0, 0).then_inc(S["consts"], 1)
            pool.iota(win_i[:, :], [[M, 2], [1, P]], KEY_BIAS, P).then_inc(S["consts"], 1)
            pool.memset(ARENA_A[:, :], 0.0).then_inc(S["consts"], 1)
            pool.memset(ARENA_D[:, :], 0.0).then_inc(S["consts"], 1)

            swap_quadrants(pool, 0)

            def settled(eng):
                eng.sem_inc(S["gpsimd_turns"], 1)

            def gather_rows(a, trip):
                for h in range(2):
                    col = pool.snap((trip & (TRIPS - 1)) * (2 * COLS) + (a * LROW + h * COLS))
                    pool.wait_ge(rows_stored[a][h], 16 + trip * 16)
                    settled(pool)
                    pool.tensor_copy(src_buf[h][:, :], KB[:, bass.ds(col, COLS)].bitcast(I32)
                                     ).then_inc(src_copied[a][h], 1)
                    pool.wait_ge(src_copied[a][h], trip + 1)
                    settled(pool)
                    for t in range(COLS):
                        pool.indirect_dma_start(
                            row_buf[h][:, t, :], None, node_dram,
                            bass.IndirectOffsetOnAxis(ap=src_buf[h][:, t:t + 1], axis=0)
                        ).then_inc(rows_gathered[a][h], 16)

            before_windows, trips = first_trips(pool)
            pool.wait_ge(S["sources_ready"], 1)
            pool.wait_ge(S["node_stored"], 32 * GROUPS)
            with pool.Fori(0, before_windows) as i:
                gather_rows(0, i)

            pool.wait_ge(S["keys_stored"], 32 * LISTS)
            with pool.Fori(0, window_rounds(pool)) as r:
                pool.wait_ge(S["win_idx_ready"], r + 1)
                for b in range(WIN_BATCHES):
                    pool.wait_ge(S["windows_counted"], r * WIN_BATCHES + b + 1)
                    settled(pool)
                    for k in range(WIN_COLS):
                        col = b * WIN_COLS + k
                        pool.indirect_dma_start(
                            windows[b][:, k, :], None, key_windows,
                            bass.IndirectOffsetOnAxis(ap=win_i[:, col:col + 1], axis=0)).then_inc(win_in[b], 16)

            with pool.Fori(before_windows, trips) as i:
                gather_rows(0, i)
            for h in range(2):
                pool.wait_ge(rows_stored[0][h], 16 + trips * 16)
            settled(pool)

            pool.wait_ge(S["sources_ready"], 2)
            with pool.Fori(0, MIDDLE) as i:
                gather_rows(1, i)

            rounds = slot_rounds(pool)
            pool.wait_ge(S["table_ready"], 1)
            with pool.Fori(0, PAIRS) as gg:
                for h in range(2):
                    lo, hi = group_trips(pool, gg * 2 + h)
                    with pool.Fori(lo, hi) as i:
                        gather_rows(1, i)
                    pool.wait_ge(rows_stored[1][0], 16 + hi * 16)
                    pool.wait_ge(rows_stored[1][1], hi * 16)
                    settled(pool)
                    with pool.Fori(0, rounds) as r:
                        pool.wait_ge(slot_idx_ready[h], gg * (rounds + 1) + r + 1)
                        pool.wait_ge(slots_used[h], gg * rounds + r + 1)
                        settled(pool)
                        for t in range(NODES):
                            for a in range(LISTS):
                                pool.indirect_dma_start(
                                    slot_rows[h][:, t, a * SLOTS:(a + 1) * SLOTS, :].rearrange("p k w -> p (k w)"),
                                    None, payload[a],
                                    bass.IndirectOffsetOnAxis(ap=slot_idx[h][:, LISTS * t + a:LISTS * t + a + 1], axis=0)
                                ).then_inc(slots_gathered[h], 16)

        @block.tensor
        def _(pe):
            pe.wait_ge(S["consts"], 11)
            pe.wait_ge(S["weights_in"], 16 * (N_WEIGHTS - 1))
            pe.transpose(TA[0][0:QUAD, 0:P], cw1[:, :], ident[:, :]).then_inc(S["comp_pe"], 1)
            for i in range(3):
                pe.wait_ge(S["comp_dve"], 2 + 2 * i)
                pe.matmul(TA[1][0:QUAD, 0:P + 1], cw1_blocks[:, i, :], comp_d[:, i, 0:P + 1],
                          start=True, stop=True).then_inc(S["comp_pe"], 1)
            pe.wait_ge(S["comp_dve"], 7)
            for i in range(4):
                last = pe.transpose(MB[0][:, QUAD * i:QUAD * (i + 1)], comp[:, i, 0:P], ident[0:QUAD, 0:QUAD])
            last.then_inc(S["comp_pe"], 1)
            pe.wait_ge(S["comp_dve"], 8)

            def norm_step1(g):
                for k in range(CHUNKS + 1):
                    n, j = g * 2 * CHUNKS + k, g * CHUNKS + k - 1
                    if k < CHUNKS:
                        transpose_chunk(n)
                    if k >= 1:
                        pe.wait_ge(S["yt_out"], n)
                        if k >= 3:
                            pe.wait_ge(S["a1_out"], j - 1)
                        elif g:
                            pe.wait_ge(S["node_out_done"], g * CHUNKS)
                        pe.matmul(MB[j % 2][:, :], E1[:, :], YT[(n - 1) % 2], start=True, stop=True
                                  ).then_inc(S["step1_ready"], 1)

            def norm_nodes(g):
                for k in range(CHUNKS + 1):
                    n, j = g * 2 * CHUNKS + CHUNKS + k, g * CHUNKS + k - 1
                    if k < CHUNKS:
                        transpose_chunk(n)
                    if k >= 1:
                        pe.wait_ge(S["yt_out"], n)
                        if k >= 3:
                            pe.wait_ge(S["node_out_done"], j - 1)
                        else:
                            pe.wait_ge(S["x1_ready"], (g + 1) * CHUNKS)
                        for t in range(TPC):
                            tok = (j * TPC + t) * P
                            last = pe.matmul(MB[j % 2][:, t * P:t * P + 2 * HEADS + HE], XT[:, tok:tok + P],
                                             node_w[:, :], start=True, stop=True)
                        last.then_inc(S["node_ready"], 1)

            def transpose_chunk(n):
                pe.wait_ge(S["y_ready"], n + 1)
                if n >= 2:
                    pe.wait_ge(S["yt_out"], n - 1)
                for t in range(TPC):
                    last = pe.transpose(TA[n % 2][:, t * P:(t + 1) * P], Y[n % 2][:, t, :], ident[:, :])
                last.then_inc(S["yt_ready"], 1)

            def convolution(g):
                pe.wait_ge(S["a1_out"], CHUNKS * (g + 1))
                for i in range(4):
                    if i:
                        pe.wait_ge(S["dz_out"], g * 12 + 4 * i)
                        pe.wait_ge(S["relu_out"], g * 16 + 4 * i)
                    elif g:
                        pe.wait_ge(S["relu_out"], g * 16)
                    for half in range(2):
                        for t, (dy, dx) in enumerate(TAPS):
                            y0 = half * (IMG_H // 2) + dy
                            for q in range(IMGS):
                                if i == 0:
                                    last = pe.matmul(Z[QUAD * q:QUAD * (q + 1), half, :], cw2[:, t, :],
                                                     A1[:, q, y0:y0 + IMG_H // 2, dx:dx + IMG_W],
                                                     start=t == 0, stop=True, skip_group_check=True)
                                else:
                                    last = pe.matmul(Z[QUAD * q:QUAD * (q + 1), half, :], cw2_of[i - 1][:, t, :],
                                                     DZ[:, q, y0:y0 + IMG_H // 2, dx:dx + IMG_W],
                                                     start=False, stop=True, skip_group_check=True)
                    last.then_inc(S["conv_stage"], 1)

            def step3(g):
                pe.wait_ge(S["relu_out"], g * 16 + 16)
                for c in range(CHUNKS):
                    j = g * CHUNKS + c
                    if c >= 2:
                        pe.wait_ge(S["x1_ready"], j - 1)
                    for t in range(TPC):
                        tok = (j * TPC + t) * P
                        pe.matmul(MB[j % 2][:, t * P:(t + 1) * P], XT[:, tok:tok + P], T3[:, :],
                                  start=True, stop=False, skip_group_check=True)
                        last = pe.matmul(MB[j % 2][:, t * P:(t + 1) * P], ones[0:1, :], b3_row[:, :],
                                         start=False, stop=True, skip_group_check=True)
                    last.then_inc(S["step3_ready"], 1)

            for g in range(GROUPS):
                norm_step1(g)
                convolution(g)
                step3(g)
                norm_nodes(g)
                if g == 0:
                    pe.wait_ge(S["counted"], 1)
                    pe.wait_ge(S["node_out_done"], CHUNKS)
                    pe.matmul(MB[0][:, 0:2 * LISTS], ones[:, :], key_counts[:, :], start=True, stop=True
                              ).then_inc(S["totals_ready"], 1)

            def experts(n):
                for m in range(8):
                    pe.wait_ge(S["hid_out"], n * 8 + m + 1)
                    pe.matmul(PF[m % 2][:, :], W1[:, m // 2, (m % 2) * P:(m % 2) * P + P],
                              XT[:, bass.ds(n * CHUNK, CHUNK)], start=True, stop=True).then_inc(S["hid_ready"], 1)
                pe.wait_ge(S["hid_out"], n * 8 + 10)
                for t in range(TPC):
                    pe.wait_ge(S["exp_out"], n * TPC + t + 1)
                    pe.matmul(Z[:, t % 2, :], ones[0:1, :], b2r[:, :], start=True, stop=False, skip_group_check=True)
                    for x_ in range(EXPERTS):
                        for kk in range(2):
                            last = pe.matmul(Z[:, t % 2, x_ * C:(x_ + 1) * C], HH[:, 2 * x_ + kk, t * P:(t + 1) * P],
                                             W2[:, 2 * x_ + kk, :], start=False, stop=True, skip_group_check=True)
                    last.then_inc(S["exp_ready"], 1)

            pe.wait_ge(S["yt_out"], NORMS)
            for n in range(LISTS * EVACS):
                if n % EVACS == 0:
                    pe.wait_ge(S["rows_sorted"], n // EVACS + 1)
                if n >= 2:
                    pe.wait_ge(S["keys_evacuated"], n - 1)
                for q in range(BANK_T):
                    j = BANK_T * n + q
                    last = pe.transpose(TA[n % 2][:, q * P:(q + 1) * P], KA[:, j * P:(j + 1) * P], ident[:, :])
                last.then_inc(S["keys_transposed"], 1)

            for a in range(LISTS):
                for t in range(PIVOTS):
                    n = a * PIVOTS + t
                    pe.wait_ge(S["hot_ready"], n + 1)
                    for g in range(2):
                        last = pe.matmul(H[:, g, :], hot_hi[:, n % 2, g * P:(g + 1) * P], hot_lo[:, n % 2, :],
                                         start=t == 0 and g == 0, stop=t == PIVOTS - 1, skip_group_check=True)
                    last.then_inc(S["hist_done"], 1)
                pe.wait_ge(S["hist_tot_ready"], a + 1)
                pe.matmul(PO[:, 0:2], before[:, :], hist_tot[:, :], start=True, stop=False, skip_group_check=True)
                pe.matmul(PO[:, 1:2], ones[:, :], hist_tot[:, 0:1], start=False, stop=True, skip_group_check=True
                          ).then_inc(S["offsets_ready"], 1)

            pe.wait_ge(S["spread_ready"], 1)
            pe.transpose(PO[0:1, 0:P], max_deg[:, 0:1], ident[:, :]).then_inc(S["spread_t"], 1)

            pe.wait_ge(S["starts_ready"], 1)
            for k in range(2 * LISTS):
                last = pe.matmul(PO[0:P - 1, k:k + 1], ident[:, 1:P], starts[:, k, 0:1], start=k == 0,
                                 stop=k == 2 * LISTS - 1, skip_group_check=True)
            last.then_inc(S["boundary_ready"], 1)
            pe.wait_ge(S["degree_ready"], 1)
            for a in range(LISTS):
                pe.transpose(TA[0][:, a * P:(a + 1) * P], starts[:, 2 * a, 0:P], ident[:, :])
                pe.transpose(TA[0][:, (2 + a) * P:(3 + a) * P], degree[:, 2 * a, :], ident[:, :])
            pe.transpose(TA[1][:, 0:P], degree[:, 1, :], ident[:, :]).then_inc(S["starts_turned"], 1)
            pe.wait_ge(S["max_deg_ready"], 1)
            pe.transpose(PO[0:1, 0:P], max_deg[:, 0:1], ident[:, :]).then_inc(S["max_deg_t"], 1)

            with pe.Fori(0, FFN_CHUNKS) as n:
                experts(n)

        @block.scalar
        def _(act):
            act.wait_ge(S["consts"], 11)

            def norm_chunk(n, k):
                if n >= 2:
                    act.wait_ge(S["yt_ready"], n - 1)
                for t in range(TPC):
                    tt = TPC * k + t
                    last = act.activation(Y[n % 2][:, t, :], x_tiles[:, tt, :], ACT.Identity,
                                          scale=rstd[:, tt:tt + 1], bias=shift[:, tt:tt + 1])
                last.then_inc(S["y_ready"], 1)

            def norm_step1(g):
                act.wait_ge(S["norm_ready"], 2 * g + 1)
                for k in range(CHUNKS + 2):
                    n = g * 2 * CHUNKS + k
                    if k < CHUNKS:
                        norm_chunk(n, k)
                        for t in range(TPC):
                            tt = TPC * k + t
                            last = act.activation(x_tiles[:, tt, :], x_tiles[:, tt, :], ACT.Identity,
                                                  scale=rstd1[:, tt:tt + 1], bias=shift[:, tt:tt + 1])
                        last.then_inc(S["xres_ready"], 1)
                    if 1 <= k <= CHUNKS:
                        act.wait_ge(S["yt_ready"], n)
                        if k >= 3:
                            act.wait_ge(S["step1_ready"], g * CHUNKS + k - 2)
                        act.activation(YT[(n - 1) % 2], TA[(n - 1) % 2][:, :], ACT.Copy).then_inc(S["yt_out"], 1)
                    if k >= 2:
                        c = k - 2
                        j = g * CHUNKS + c
                        act.wait_ge(S["step1_ready"], j + 1)
                        if c == 0 and g:
                            act.wait_ge(S["dz_out"], g * 12)
                        r0 = 1 + (IMG_H // 2) * (c % 2)
                        act.activation(A1[:, c // 2, r0:r0 + IMG_H // 2, 1:1 + IMG_W],
                                       MB[j % 2][:, :].rearrange("p (a b) -> p a b", b=IMG_W),
                                       ACT.Relu, bias=e1_bias[:, :]).then_inc(S["a1_out"], 1)

            def norm_nodes(g):
                act.wait_ge(S["norm_ready"], 2 * g + 2)
                for k in range(CHUNKS + 2):
                    n = g * 2 * CHUNKS + CHUNKS + k
                    if k < CHUNKS:
                        norm_chunk(n, k)
                    if 1 <= k <= CHUNKS:
                        tok = (g * CHUNKS + k - 1) * CHUNK
                        act.wait_ge(S["yt_ready"], n)
                        act.activation(XT[:, tok:tok + CHUNK], TA[(n - 1) % 2][:, :], ACT.Copy
                                       ).then_inc(S["yt_out"], 1)
                    if k >= 2:
                        c = k - 2
                        j = g * CHUNKS + c
                        act.wait_ge(S["node_ready"], j + 1)
                        if c == 0 and g:
                            act.wait_ge(S["node_stored"], 32 * g)
                        act.activation(node_out[:, TPC * c:TPC * (c + 1), :],
                                       MB[j % 2][:, :].rearrange("p (t n) -> p t n", n=P)[:, :, 0:2 * HEADS + HE],
                                       ACT.Copy).then_inc(S["node_out_done"], 1)

            def roots(n):
                act.wait_ge(S["var_ready"], n + 1)
                act.activation(std[:, :], std[:, :], ACT.Sqrt).then_inc(S["std_ready"], 1)

            for g in range(GROUPS):
                roots(2 * g)
                norm_step1(g)
                for i in range(4):
                    act.wait_ge(S["conv_stage"], g * 4 + i + 1)
                    if i == 0 and g == GROUPS - 1:
                        act.wait_ge(S["zeros_stored"], 32 * LISTS)
                    for q in range(IMGS):
                        if i < 3:
                            act.wait_ge(S["dz_out"], g * 12 + 4 * i + q + 1)
                        tok = g * TILES * P + q * IMG_H * IMG_W
                        act.activation(XT[QUAD * i:QUAD * (i + 1), tok:tok + IMG_H * IMG_W],
                                       Z[QUAD * q:QUAD * (q + 1), :, :].rearrange("p h n -> p (h n)"),
                                       ACT.Relu, bias=cb2[QUAD * q:QUAD * (q + 1), :]).then_inc(S["relu_out"], 1)
                roots(2 * g + 1)
                norm_nodes(g)

            def hidden(n):
                for m in range(8):
                    act.wait_ge(S["hid_ready"], n * 8 + m + 1)
                    act.activation(HH[:, m, :], PF[m % 2][:, :], ACT.Gelu, bias=b1c[:, m:m + 1]
                                   ).then_inc(S["hid_out"], 1)

            def outputs(n, tiles, h):
                for t in tiles:
                    act.wait_ge(S["exp_ready"], n * TPC + t + 1)
                    act.activation(YE[h][:, t, :], Z[:, t % 2, :], ACT.Copy).then_inc(S["exp_out"], 1)

            for a in range(LISTS):
                if a:
                    swap_quadrants(act, a)
                for n in range(a * EVACS, (a + 1) * EVACS):
                    act.wait_ge(S["keys_transposed"], n + 1)
                    k = BANK_T * (n % EVACS)
                    act.activation(keys_t[a][:, k:k + BANK_T, :], TA[n % 2][:, :].rearrange("p (q c) -> p q c", c=P),
                                   ACT.Copy).then_inc(S["keys_evacuated"], 1)

            act.wait_ge(S["init_args"], 1)
            act.activation(tmp_a, tmp_a, ACT.Exp)
            act.activation(tmp_b, tmp_b, ACT.Exp).then_inc(S["init_exps"], 1)

            def store_result(gg, h):
                act.wait_ge(tail_done[h], gg + 2)
                act.dma_start(out_chunks[gg * 2 + h], tail_x[h]).then_inc(tail_out[h], 16)

            act.sem_inc(S["hid_out"], 2)
            act.sem_inc(S["exp_out"], 2)
            rounds = slot_rounds(act)

            def router(gg, h, before=None):
                n = gg * 2 + h
                hidden(n)
                with act.Fori(0, rounds) as r:
                    act.wait_ge(S["e_ready"], n * rounds + r + 1)
                    act.activation(e_buf, e_buf, ACT.Exp).then_inc(S["e_exp"], 1)
                act.wait_ge(tail_done[h], gg + 1)
                outputs(n, range(TPC - 1), h)
                if before:
                    store_result(*before)
                act.wait_ge(S["score_var"], n + 1)
                act.activation(g4[0], g4[0], ACT.Sqrt).then_inc(S["score_std"], 1)
                outputs(n, (TPC - 1,), h)
                act.wait_ge(S["logits_ready"], n + 1)
                act.activation(weight_g, weight_g, ACT.Exp).then_inc(S["logits_exp"], 1)

            router(0, 0)
            with act.Fori(0, PAIRS - 1) as gg:
                router(gg, 1, (gg, 0))
                router(gg + 1, 0, (gg, 1))
            router(PAIRS - 1, 1, (PAIRS - 1, 0))
            store_result(PAIRS - 1, 1)
            for h in range(2):
                act.wait_ge(tail_out[h], 16 * (1 + PAIRS))

        @block.vector
        def _(dve):
            links = [0]

            def link(ins):
                links[0] += 1
                ins.then_inc(S["dve_chain"], 1)
                dve.wait_ge(S["dve_chain"], links[0])

            tt, ts, stt, cp, red = (dve.tensor_tensor, dve.tensor_scalar, dve.scalar_tensor_tensor,
                                    dve.tensor_copy, dve.tensor_reduce)
            dve.wait_ge(S["consts"], 11)

            def normalise(n, eps):
                for t in range(TILES):
                    last = dve.bn_aggr(mean_var[:, t, :], bn[:, t, :])
                link(last)
                ts(std[:, :], mean_var[:, :, 1], eps, None, ALU.add).then_inc(S["var_ready"], 1)
                dve.wait_ge(S["std_ready"], n + 1)
                link(dve.reciprocal(rstd[:, :], std[:, :]))
                link(ts(rstd1[:, :], rstd[:, :], 1.0, None, ALU.add))
                link(tt(shift[:, :], mean_var[:, :, 0], rstd[:, :], ALU.mult))
                ts(shift[:, :], shift[:, :], -1.0, None, ALU.mult).then_inc(S["norm_ready"], 1)

            def token_stats(g):
                dve.wait_ge(S["x_in"], 16 * (g + 1))
                for t in range(TILES):
                    last = dve.bn_stats(bn[:, t, :], x_tiles[:, t, :])
                link(last)
                if g:
                    dve.wait_ge(S["y_ready"], 2 * CHUNKS * g)
                normalise(2 * g, 1e-6)

            def small_weights():
                dve.wait_ge(S["weights_in"], 16 * (N_WEIGHTS - 1))
                dve.wait_ge(S["comp_pe"], 1)
                cp(comp[:, 0, 0:P], TA[0][0:QUAD, 0:P]).then_inc(S["comp_dve"], 1)
                for i in range(3):
                    dve.wait_ge(S["comp_dve"], 1 + 2 * i)
                    link(cp(comp_d[:, i, 0:P + 1], comp[:, i, 0:P + 1]))
                    blk = comp_d[:, i, QUAD * i:QUAD * (i + 1)]
                    tt(blk, blk, ident[0:QUAD, 0:QUAD], ALU.subtract).then_inc(S["comp_dve"], 1)
                    dve.wait_ge(S["comp_pe"], 2 + i)
                    tt(comp[:, i + 1, 0:P + 1], comp[:, i, 0:P + 1], TA[1][0:QUAD, 0:P + 1], ALU.add
                       ).then_inc(S["comp_dve"], 1)
                dve.wait_ge(S["comp_dve"], 7)
                for i in range(4):
                    link(cp(e1_bias[QUAD * i:QUAD * (i + 1), :], comp[:, i, P:P + 1]))
                dve.wait_ge(S["comp_pe"], 5)
                link(cp(E1[:, :], MB[0][:, 0:P]))
                link(tt(rec_b[:, 1:P], ident[:, 0:P - 1], w3_row[:, 0:P - 1], ALU.mult))
                link(ts(rec_b[:, 1:P], rec_b[:, 1:P], -1.0, None, ALU.mult))
                link(cp(rec_b[:, 0:1], w3_col[:, :]))
                link(dve.memset(rec_a[:, 0:1], 0.0))
                link(ts(rec_a[:, 1:P], w3_row[:, 0:P - 1], 1.0, None, ALU.add))
                link(dve.tensor_tensor_scan(T3[:, :], rec_a, rec_b, 0.0, ALU.mult, ALU.add))
                link(dve.memset(b3_in[0:1, 1:P], 0.0))
                link(dve.tensor_tensor_scan(b3_row[:, :], rec_a[0:1, :], b3_in[:, :], 0.0, ALU.mult, ALU.add))
                for i in range(3):
                    link(dve.memset(cw2_of[i][:, :, :], 0.0))
                    r = slice(QUAD * i, QUAD * (i + 1))
                    link(cp(cw2_of[i][r, :, :], cw2[r, :, :]))
                for i in range(2):
                    link(tt(att_w[:, i, :], node_w[:, HEADS:HEADS + HE], att[:, i, :], ALU.mult))
                heads = lambda i: att_w[:, i, :].rearrange("p (g x) -> p g x", g=HEADS)
                link(red(node_w[:, 0:HEADS], heads(0), AX.X, ALU.add))
                red(node_w[:, HEADS + HE:], heads(1), AX.X, ALU.add).then_inc(S["comp_dve"], 1)

            def make_keys():
                A, B, Cc = KA[:, :], KB[:, :], KC[:, :]
                Ai, Bi, Ci = A.bitcast(I32), B.bitcast(I32), Cc.bitcast(I32)
                for m in range(8):
                    link(ts(sign_bits[:, m:m + 1], part_i[:, 0:1], m, 1, ALU.logical_shift_right, ALU.bitwise_and))
                link(ts(signs[:, 0:8], sign_bits[:, :], -2.0, 1.0, ALU.mult, ALU.add))
                link(tt(signs[:, 7:9], signs[:, 4:6], signs[:, 5:7], ALU.mult))
                dve.wait_ge(S["edges_in"], 32)
                link(ts(Cc, Ai, 0.0, float(M), ALU.is_lt, ALU.mult))
                link(tt(A, Ai, Cc, ALU.add))
                link(ts(A, A, 0.0, float(M - 1), ALU.max, ALU.min))
                link(ts(Cc, Bi, 0.0, float(4 * M), ALU.is_lt, ALU.mult))
                link(tt(B, Bi, Cc, ALU.max))
                link(ts(Cc, B, float(M), float(2 * M), ALU.is_ge, ALU.mult))
                link(tt(B, B, Cc, ALU.add))
                link(ts(Cc, A, float(M - 1), float(M), ALU.is_equal, ALU.mult))
                link(tt(B, B, Cc, ALU.add))
                link(ts(Bi, B, float(VALID_END), float(KEY_BIAS), ALU.min, ALU.add))
                link(ts(Bi, Bi, SRC_BITS, None, ALU.logical_shift_left))
                link(cp(Ci, A))
                link(tt(Ai, Bi, Ci, ALU.bitwise_or))
                for k in range(2 * LISTS):
                    a, end = k // 2, (REAL_END, VALID_END)[k % 2]
                    link(ts(half(KB, a), half(KA, a), key_bits_as_float(end), 0.0, ALU.is_lt, ALU.add,
                            accum_out=key_counts[:, k:k + 1]))
                dve.memset(counts_f[:, :], 0.0).then_inc(S["counted"], 1)

            def totals():
                dve.wait_ge(S["totals_ready"], 1)
                link(cp(key_totals[:, :], MB[0][:, 0:2 * LISTS]))
                n = counts_f[0:1, 0:1]
                link(ts(n, key_totals[0:1, 0:1], 1.0 / PER_TRIP, 0.5 - 0.5 / PER_TRIP, ALU.mult, ALU.add))
                link(ts(n, n, ROUND_MAGIC, None, ALU.add))
                link(ts(n, n, -ROUND_MAGIC, 1.0, ALU.add, ALU.max))
                before_windows, m = counts_f[0:1, 1:2], counts_f[0:1, 2:3]
                link(ts(before_windows, n, -float(AFTER_WINDOWS), 1.0, ALU.add, ALU.max))
                link(ts(m, before_windows, 1.0, None, ALU.add))
                link(tt(m, m, n, ALU.max))
                cp(counts_i[0:1, 3:4], m)
                cp(counts_i[0:1, 0:1], before_windows).then_inc(S["trips_ready"], 1)

            def exchange(src, dst, run, stride, n=LROW):
                if 2 * run <= n:
                    def part(b, d, h):
                        return b.rearrange("p (b d g h j) -> p b d g h j", d=2, g=run // (2 * stride), h=2,
                                           j=stride)[:, :, d, :, h, :]
                    turns = (0, 1)
                else:
                    def part(b, d, h):
                        return b.rearrange("p (g h j) -> p g h j", h=2, j=stride)[:, :, h, :]
                    turns = (0,)
                for d in turns:
                    tt(part(dst, d, 0), part(src, d, 0), part(src, d, 1), ALU.max if d else ALU.min)
                    last = tt(part(dst, d, 1), part(src, d, 0), part(src, d, 1), ALU.min if d else ALU.max)
                link(last)

            def row_steps(keys, other):
                a, b = keys, other
                stride = LROW // 2
                while stride:
                    exchange(a, b, 2 * LROW, stride)
                    a, b = b, a
                    stride //= 2
                    yield

            def quadrant_step(which, keys, frm, copy):
                swaps[which] += 1
                dve.sem_inc(swap_ready[which], 1)
                yield
                dve.wait_ge(swapped[which], 64 * swaps[which])
                link(stt(keys, copy, -1.0, frm, ALU.mult, ALU.min))

            def sort_keys(which):
                keys, copy, other = (half(k, which) for k in (KA, KB, KC))

                def times_sign(col, frm=keys):
                    link(ts(keys, frm, signs[:, col:col + 1], None, ALU.mult))

                a, b = keys, other
                run = 2
                while run < LROW:
                    stride = run // 2
                    while stride:
                        exchange(a, b, run, stride)
                        a, b = b, a
                        stride //= 2
                        yield
                    run *= 2
                times_sign(0, a)
                yield from row_steps(keys, other)
                for m in range(1, LEVELS + 1):
                    if m <= 4:
                        times_sign(m - 1, other)
                    elif m == 5:
                        times_sign(7, other)
                    elif m == 6:
                        times_sign(6, other)
                        yield from quadrant_step(which, keys, keys, copy)
                        times_sign(5)
                    else:
                        yield from quadrant_step(which, keys, other, copy)
                        times_sign(8)
                        yield from quadrant_step(which, keys, keys, copy)
                        times_sign(5)
                    link(dve.transpose(other, keys))
                    a, b = other, copy
                    for s in range(min(m, 5) - 1, -1, -1):
                        exchange(a, b, (1 << m) if m < 5 else LROW, 1 << s)
                        a, b = b, a
                        yield
                    if m < LEVELS:
                        link(dve.transpose(keys, a))
                        if m <= 4:
                            times_sign(m)
                        yield from row_steps(keys, other)
                    else:
                        link(dve.transpose(other, a))
                        yield from row_steps(other, keys)
                dve.sem_inc(S["rows_sorted"], 1)

            swaps = [0] * LISTS
            sorting = chain(*(sort_keys(a) for a in range(LISTS)))

            def sort_steps(n):
                for _ in range(n):
                    next(sorting, None)

            small_weights()
            token_stats(0)
            make_keys()
            for g in range(GROUPS):
                if g:
                    token_stats(g)
                sort_steps(18)
                for i in range(3):
                    dve.wait_ge(S["conv_stage"], g * 4 + i + 1)
                    if i == 0:
                        dve.wait_ge(S["a1_out"], CHUNKS * (g + 1))
                    for q in range(IMGS):
                        r = slice(QUAD * i, QUAD * (i + 1))
                        stt(DZ[r, q, 1:1 + IMG_H, 1:1 + IMG_W],
                            Z[QUAD * q:QUAD * (q + 1), :, :].rearrange("p h (a b) -> p (h a) b", b=IMG_W),
                            cb2[QUAD * q:QUAD * (q + 1), :], A1[r, q, 1:1 + IMG_H, 1:1 + IMG_W],
                            ALU.add, ALU.subtract).then_inc(S["dz_out"], 1)
                    sort_steps(7)
                for c in range(CHUNKS):
                    j = g * CHUNKS + c
                    dve.wait_ge(S["step3_ready"], j + 1)
                    dve.wait_ge(S["xres_ready"], j + 1)
                    flat = XG[:, c * CHUNK:(c + 1) * CHUNK]
                    tt(flat, flat, MB[j % 2][:, :], ALU.add).then_inc(S["x1_ready"], 1)
                    dve.wait_ge(S["x1_ready"], j + 1)
                    for t in range(TPC):
                        last = dve.bn_stats(bn[:, TPC * c + t, :], x_tiles[:, TPC * c + t, :])
                link(last)
                dve.wait_ge(S["y_ready"], 2 * CHUNKS * g + CHUNKS)
                normalise(2 * g + 1, 1e-5)
                if g == 0:
                    totals()
                sort_steps(8)
            def sources(a):
                dve.wait_ge(S["keys_evacuated"], (a + 1) * EVACS)
                k = half(KB, a).bitcast(I32)
                ts(k, k, (1 << SRC_BITS) - 1, None, ALU.bitwise_and).then_inc(S["sources_ready"], 1)

            sort_steps(LAST_STEPS)
            sources(0)
            sort_steps(ROW)
            sources(1)

            dve.memset(end_keys, key_bits_as_float(VALID_END)).then_inc(S["end_keys_ready"], 1)
            link(cp(iota_f[:, :], iota_i[:, :]))
            link(ts(thresholds[:, :].bitcast(I32), win_i[:, :], SRC_BITS, None, ALU.logical_shift_left))
            for a in range(LISTS):
                link(ts(piv_i[:, 0, :], half(KA, a)[:, ::STRIDE].bitcast(I32), SRC_BITS, None, ALU.logical_shift_right))
                link(ts(piv_i[:, 1, :], piv_i[:, 0, :], float(-KEY_BIAS), None, ALU.add))
                link(ts(piv_i[:, 0, :], piv_i[:, 1, :], 7, None, ALU.logical_shift_right))
                link(ts(piv_i[:, 2, :], piv_i[:, 1, :], P - 1, None, ALU.bitwise_and))
                link(cp(piv_f[:, 0, :], piv_i[:, 0, :]))
                link(cp(piv_f[:, 1, :], piv_i[:, 2, :]))
                for t in range(PIVOTS):
                    n = a * PIVOTS + t
                    if n >= 2:
                        dve.wait_ge(S["hist_done"], n - 1)
                    ts(hot_hi[:, n % 2, :], iota_f[:, :], piv_f[:, 0, t:t + 1], None, ALU.is_equal)
                    ts(hot_lo[:, n % 2, :], iota_f[:, 0:P], piv_f[:, 1, t:t + 1], None, ALU.is_equal
                       ).then_inc(S["hot_ready"], 1)
                dve.wait_ge(S["hist_done"], (a + 1) * PIVOTS)
                link(cp(hist[:, :, :], H))
                for g in range(2):
                    link(dve.tensor_tensor_scan(cum[:, g, :], ones[:, :], hist[:, g, :], 0.0, ALU.mult, ALU.add))
                cp(hist_tot[:, :], cum[:, :, P - 1]).then_inc(S["hist_tot_ready"], 1)
                dve.wait_ge(S["offsets_ready"], a + 1)
                link(cp(hist_off[:, :], PO[:, 0:2]))
                for g in range(2):
                    link(stt(cum[:, g, :], cum[:, g, :], hist_off[:, g:g + 1], hist[:, g, :], ALU.add, ALU.subtract))
                link(ts(win_f[:, a * 2 * P:(a + 1) * 2 * P], cum[:, :, :].rearrange("p g l -> p (g l)"), -1.0, 0.0,
                        ALU.add, ALU.max))
            shared = lambda ap: ap.rearrange("p (c j) -> p c j", j=SHARE)
            first_win = shared(win_f)[:, :, 0]
            link(cp(win_at, first_win))
            link(tt(win_i[:, 0:GROUPS_OF_NODES], shared(win_f)[:, :, SHARE - 1], first_win, ALU.subtract))
            red(max_deg[:, :], win_i[:, 0:GROUPS_OF_NODES], AX.X, ALU.max).then_inc(S["spread_ready"], 1)
            dve.wait_ge(S["spread_ready"], 1)
            second = GROUPS_OF_NODES // LISTS
            link(ts(win_at[:, second:], win_at[:, second:], float(LIST_WINDOWS), None, ALU.add))
            cp(win_i[:, 0:GROUPS_OF_NODES], win_at).then_inc(S["win_idx_ready"], 1)
            dve.wait_ge(S["spread_t"], 1)
            n = counts_f[0:1, 2:3]
            link(red(n, PO[0:1, 0:P], AX.X, ALU.max))
            link(ts(n, n, 1.0 / SPAN, 0.5 + 0.5 / SPAN, ALU.mult, ALU.add))
            link(ts(n, n, ROUND_MAGIC, None, ALU.add))
            link(ts(n, n, -ROUND_MAGIC, 1.0, ALU.add, ALU.max))
            cp(counts_i[0:1, 2:3], n).then_inc(S["window_rounds_ready"], 1)

            for c in counted:
                link(dve.memset(c, 0.0))
            dve.sem_inc(S["windows_counted"], WIN_BATCHES)
            WINDOW_OPS = WIN_BATCHES * (2 * SHARE + 1) + LISTS + 1
            with dve.Fori(0, window_rounds(dve)) as r:
                done = [0]

                def window_link(ins):
                    done[0] += 1
                    ins.then_inc(S["window_chain"], 1)
                    dve.wait_ge(S["window_chain"], r * WINDOW_OPS + done[0])

                for b in range(WIN_BATCHES):
                    dve.wait_ge(win_in[b], (r + 1) * (16 * WIN_COLS))
                    a, k = divmod(b, WIN_BATCHES // LISTS)
                    cols = slice(WIN_COLS * SHARE * k, WIN_COLS * SHARE * (k + 1))
                    for j in range(SHARE):
                        window_link(tt(below, windows[b], bc(shared(thresholds[:, cols])[:, :, j], 2,
                                                                 [P, WIN_COLS, WINDOW]), ALU.is_lt))
                        window_link(red(found[:, :, j], below, AX.X, ALU.add))
                    dve.sem_inc(S["windows_counted"], 1)
                    window_link(tt(shared(counted[a][:, cols]), shared(counted[a][:, cols]), found, ALU.add))
                for a in range(LISTS):
                    w = win_at[:, a * second:(a + 1) * second]
                    window_link(ts(w, w, float(SPAN), float(a * LIST_WINDOWS + LIST // STRIDE), ALU.add, ALU.min))
                window_link(cp(win_i[:, 0:GROUPS_OF_NODES], win_at))
                assert done[0] == WINDOW_OPS
                dve.sem_inc(S["win_idx_ready"], 1)
            for k in range(2 * LISTS):
                a, g = divmod(k, 2)
                cp(starts[:, k, P:P + 1], key_totals[:, k:k + 1])
                last = stt(shared(starts[:, k, 0:P]),
                           bc(shared(win_f[:, k * P:(k + 1) * P])[:, :, 0], 2, [P, P // SHARE, SHARE]), float(STRIDE),
                           shared(counted[a][:, g * P:(g + 1) * P]), ALU.mult, ALU.add)
            last.then_inc(S["starts_ready"], 1)

            dve.wait_ge(S["nodes_in"], 48)
            link(tt(tmp_a, node_rows[:, :, 0:HEADS], a_dst, ALU.add))
            link(tt(tmp_b, bc(last_row[:, 0:HEADS], 1, [P, P, HEADS]), a_dst, ALU.add))
            link(stt(tmp_a, tmp_a, 0.2, tmp_a, ALU.mult, ALU.max))
            link(stt(tmp_b, tmp_b, 0.2, tmp_b, ALU.mult, ALU.max))
            dve.wait_ge(S["boundary_ready"], 1)
            link(cp(starts[0:P - 1, :, P], PO[0:P - 1, 0:2 * LISTS]))
            link(tt(degree, starts[:, :, 1:P + 1], starts[:, :, 0:P], ALU.subtract))
            tt(degree[:, 1, :], degree[:, 1, :], degree[:, 3, :], ALU.add).then_inc(S["degree_ready"], 1)
            for a in range(LISTS):
                last = red(hist_tot[:, a:a + 1], degree[:, 2 * a, :], AX.X, ALU.max)
            link(last)
            tt(max_deg[:, :], hist_tot[:, 0:1], hist_tot[:, 1:2], ALU.max).then_inc(S["max_deg_ready"], 1)
            dve.wait_ge(S["max_deg_t"], 1)
            n = counts_f[0:1, 1:2]
            link(red(n, PO[0:1, 0:P], AX.X, ALU.max))
            link(ts(n, n, 1.0 / SLOTS, 0.5 - 0.5 / SLOTS, ALU.mult, ALU.add))
            link(ts(n, n, ROUND_MAGIC, None, ALU.add))
            link(ts(n, n, -ROUND_MAGIC, 1.0, ALU.add, ALU.max))
            cp(counts_i[0:1, 1:2], n).then_inc(S["rounds_ready"], 1)
            dve.wait_ge(S["starts_turned"], 1)
            for a in range(LISTS):
                cp(starts_t[:, 0:P, a], TA[0][:, a * P:(a + 1) * P])
                cp(ends_t[:, 0:P, a], TA[0][:, (2 + a) * P:(3 + a) * P])
                for c in range(P, P + NODES):
                    cp(starts_t[:, c, a:a + 1], key_totals[:, 2 * a:2 * a + 1])
                    cp(ends_t[:, c, a:a + 1], key_totals[:, 2 * a:2 * a + 1])
            link(cp(last_degree[:, :], TA[1][:, 0:P]))
            link(tt(ends_t[:, 0:P, :], ends_t[:, 0:P, :], starts_t[:, 0:P, :], ALU.add))
            ends = trip_f[:, 1:]
            link(ts(ends, starts_t[0:1, NODES::NODES, 1], 1.0 / PER_TRIP, 0.5 - 0.5 / PER_TRIP, ALU.mult, ALU.add))
            link(ts(ends, ends, ROUND_MAGIC, None, ALU.add))
            link(ts(ends, ends, -ROUND_MAGIC, 1.0, ALU.add, ALU.add))
            n = counts_f[0:1, 0:1]
            link(ts(n, trip_f[:, NODE_GROUPS:], float(-MIDDLE), 0.0, ALU.add, ALU.max))
            link(ts(n, n, 1.0 / NODE_GROUPS, None, ALU.mult))
            link(ts(spread[:, :], iota_f[0:1, 1:NODE_GROUPS + 1], n, float(MIDDLE), ALU.mult, ALU.add))
            link(ts(spread[:, :], spread[:, :], ROUND_MAGIC, None, ALU.add))
            link(ts(spread[:, :], spread[:, :], -ROUND_MAGIC, None, ALU.add))
            link(tt(spread[:, :], spread[:, :], ends, ALU.max))
            link(dve.memset(trip_f[:, 0:1], float(MIDDLE)))
            link(dve.tensor_tensor_scan(ends, ones[0:1, 0:NODE_GROUPS], spread[:, :], float(MIDDLE),
                                        ALU.add, ALU.max))
            cp(trip_i[:, :], trip_f[:, :]).then_inc(S["table_ready"], 1)

            link(ts(beat[:, :], last_degree[:, :], 0.5, -2 * NEG, ALU.is_gt, ALU.mult))
            link(ts(beat[:, :], beat[:, :], NEG, None, ALU.add))
            link(tt(tmp_b, tmp_b, bc(beat[:, :], 2, [P, P, HEADS]), ALU.min))
            link(tt(run_max, tmp_a, tmp_b, ALU.max))
            link(tt(tmp_a, tmp_a, run_max, ALU.subtract))
            tt(tmp_b, tmp_b, run_max, ALU.subtract).then_inc(S["init_args"], 1)
            dve.wait_ge(S["init_exps"], 1)
            per_head = [P, P, HEADS, EXPERTS]
            link(tt(tmp_b, tmp_b, bc(last_degree[:, :], 2, [P, P, HEADS]), ALU.mult))
            link(tt(denom, tmp_a, tmp_b, ALU.add))
            link(tt(by_head(agg), by_head(node_rows[:, :, HEADS:]), bc(tmp_a, 3, per_head), ALU.mult))
            link(tt(by_head(tmp16), by_head(bc(last_row[:, HEADS:], 1, [P, P, HE])), bc(tmp_b, 3, per_head),
                    ALU.mult))
            link(tt(agg, agg, tmp16, ALU.add))
            link(cp(slot_iota[:, :], iota_f[:, 0:SLOTS]))
            link(ts(lower_i[:, 0, :], iota_i[:, 0:HE], 2, None, ALU.logical_shift_right))
            link(ts(lower_i[:, 1, :], iota_i[:, 0:HE], EXPERTS - 1, None, ALU.bitwise_and))
            link(tt(lower[:, :], lower_i[:, 1, :], lower_i[:, 0, :], ALU.is_lt))

            rounds = slot_rounds(dve)

            def waits_done():
                dve.sem_inc(S["vector_turns"], 1)

            def chained(sem_, base):
                done = [0]

                def chain_link(ins):
                    done[0] += 1
                    ins.then_inc(sem_, 1)
                    dve.wait_ge(sem_, base + done[0])

                return chain_link, done

            for h in range(2):
                dve.sem_inc(slots_used[h], 1)
                dve.sem_inc(tail_done[h], 1)
            of_group = lambda ap, k: ap[:, k, :].rearrange("p c a -> p (c a)")
            cp(slot_end[0][:, :], of_group(ends_t, slice(0, NODES)))
            link(cp(slot_at[0][:, :], of_group(starts_t, slice(0, NODES))))
            cp(slot_idx[0][:, :], slot_at[0][:, :]).then_inc(slot_idx_ready[0], 1)
            SLOT_OPS, GROUP_OPS = 11, 28
            with dve.Fori(0, PAIRS) as gg:
                for h in range(2):
                    n = gg * 2 + h
                    cols = bass.ds(n * NODES, NODES)
                    group_link, group_done = chained(S["group_chain"], n * GROUP_OPS)
                    nxt = bass.ds(n * NODES + NODES, NODES)
                    ts(slot_at[1 - h][:, :], of_group(starts_t, nxt), 0.0, None, ALU.add)
                    group_link(ts(slot_end[1 - h][:, :], of_group(ends_t, nxt), 0.0, None, ALU.add))
                    cp(slot_idx[1 - h][:, :], slot_at[1 - h][:, :]).then_inc(slot_idx_ready[1 - h], 1)
                    waits_done()
                    with dve.Fori(0, rounds) as r:
                        step = n * rounds + r
                        slot_link, slot_done = chained(S["slot_chain"], step * SLOT_OPS)
                        by_slot = [P, NODES, LISTS * SLOTS, HEADS]
                        end = LISTS * SLOTS
                        rows = slot_rows[h]
                        e = exps[:, :, 0:end, :]
                        slot_link(tt(slot_left[:, :], slot_end[h][:, :], slot_at[h][:, :], ALU.subtract))
                        tt(unused, bc(slot_iota[:, :], 1, [P, NODES * LISTS, SLOTS]), bc(slot_left[:, :], 2, [P, NODES * LISTS, SLOTS]),
                           ALU.is_ge)
                        slot_link(ts(slot_at[h][:, :], slot_at[h][:, :], float(SLOTS), None, ALU.add))
                        slot_link(tt(slot_next[:, :], slot_end[h][:, :], slot_at[h][:, :], ALU.min))
                        ts(exps[:, :, end, :], run_max[:, cols, :], 0.0, None, ALU.add)
                        dve.wait_ge(slots_gathered[h], (gg * rounds + r + 1) * (16 * LISTS * NODES))
                        cp(slot_idx[h][:, :], slot_next[:, :]).then_inc(slot_idx_ready[h], 1)
                        slot_link(tt(e, rows[:, :, 0:end, 0:HEADS], bc(a_dst[:, cols, :], 2, by_slot), ALU.add))
                        ts(rows[:, :, end, HEADS:], agg[:, cols, :], 0.0, None, ALU.add)
                        slot_link(stt(e, e, 0.2, e, ALU.mult, ALU.max))
                        slot_link(stt(e, bc(unused.rearrange("p (c a) k -> p c (a k)", a=LISTS), 3, by_slot), NEG, e, ALU.mult, ALU.add))
                        waits_done()
                        slot_link(red(run_max[:, cols, :], exps.rearrange("p c k g -> p c g k"), AX.X, ALU.max))
                        tt(exps, exps, bc(run_max[:, cols, :], 2, [P, NODES, TERMS, HEADS]), ALU.subtract
                           ).then_inc(S["e_ready"], 1)
                        dve.wait_ge(S["e_exp"], step + 1)
                        split = lambda ap: ap.rearrange("p c k (g x) -> p (c k) g x", g=HEADS)
                        slot_link(tt(split(rows[:, :, :, HEADS:]), split(rows[:, :, :, HEADS:]),
                                     bc(exps.rearrange("p c k g -> p (c k) g"), 3,
                                        [P, NODES * TERMS, HEADS, EXPERTS]), ALU.mult))
                        so_far = exps[:, :, end, :]
                        slot_link(tt(so_far, so_far, denom[:, cols, :], ALU.mult))
                        waits_done()
                        red(agg[:, cols, :], rows[:, :, :, HEADS:].rearrange("p c k f -> p c f k"), AX.X, ALU.add
                            ).then_inc(slots_used[h], 1)
                        slot_link(red(denom[:, cols, :], exps.rearrange("p c k g -> p c g k"), AX.X, ALU.add))
                        slot_link(ts(den_g, denom[:, cols, :], 1e-16, None, ALU.add))
                        waits_done()
                    assert slot_done[0] == SLOT_OPS, slot_done

                    per_head = [P, NODES, HEADS, EXPERTS]
                    heads = lambda ap: ap.rearrange("p c (g x) -> p c g x", g=HEADS)
                    par = lambda k: bc(gat_par[:, k, :], 1, [P, NODES, HE])
                    per_node = lambda ap, width: bc(ap, 2, [P, NODES, width])
                    mean, top, total = g4
                    group_link(dve.reciprocal(den_g, den_g))
                    group_link(tt(heads(agg_g), heads(agg[:, cols, :]), bc(den_g, 3, per_head), ALU.mult))
                    group_link(tt(agg_g, agg_g, par(0), ALU.add))
                    group_link(red(mean, agg_g, AX.X, ALU.add))
                    group_link(ts(mean, mean, 1.0 / HE, None, ALU.mult))
                    group_link(tt(agg_g, agg_g, per_node(mean, HE), ALU.subtract))
                    group_link(tt(sq_g, agg_g, agg_g, ALU.mult))
                    group_link(red(mean, sq_g, AX.X, ALU.add))
                    ts(mean, mean, 1.0 / HE, 1e-5, ALU.mult, ALU.add).then_inc(S["score_var"], 1)
                    dve.wait_ge(S["score_std"], n + 1)
                    group_link(dve.reciprocal(mean, mean))
                    group_link(tt(agg_g, agg_g, per_node(mean, HE), ALU.mult))
                    group_link(tt(agg_g, agg_g, par(1), ALU.mult))
                    group_link(tt(agg_g, agg_g, par(2), ALU.add))
                    group_link(red(score_g, agg_g.rearrange("p c (g x) -> p c x g", g=HEADS), AX.X, ALU.add))
                    group_link(ts(score_g, score_g, 1.0 / HEADS, None, ALU.mult))
                    group_link(red(top, score_g, AX.X, ALU.max))
                    tt(weight_g, score_g, per_node(top, EXPERTS), ALU.subtract).then_inc(S["logits_ready"], 1)
                    square = [P, NODES, EXPERTS, EXPERTS]
                    pairs = lambda ap: ap.rearrange("p c (i j) -> p c i j", j=EXPERTS)
                    tt(pairs(greater), bc(score_g, 2, square), bc(score_g, 3, square), ALU.is_gt)
                    group_link(tt(pairs(equal), bc(score_g, 2, square), bc(score_g, 3, square), ALU.is_equal))
                    group_link(tt(equal, equal, bc(lower[:, :], 1, [P, NODES, HE]), ALU.mult))
                    group_link(tt(greater, greater, equal, ALU.add))
                    group_link(red(gate_g, pairs(greater), AX.X, ALU.add))
                    group_link(ts(gate_g, gate_g, 1.5, None, ALU.is_lt))
                    dve.wait_ge(S["logits_exp"], n + 1)
                    group_link(tt(gate_g, gate_g, weight_g, ALU.mult))
                    group_link(red(total, gate_g, AX.X, ALU.add))
                    group_link(dve.reciprocal(total, total))
                    group_link(tt(gate_g, gate_g, per_node(total, EXPERTS), ALU.mult))
                    dve.wait_ge(S["exp_out"], 2 + (n + 1) * TPC)
                    dve.wait_ge(tail_in[h], gg * 16 + 16)
                    for x_ in range(EXPERTS):
                        for t in range(TPC):
                            last = stt(tail_x[h][:, t, :], YE[h][:, t, x_ * C:(x_ + 1) * C],
                                       gate_g[:, t, x_:x_ + 1], tail_x[h][:, t, :], ALU.mult, ALU.add)
                        if x_ < EXPERTS - 1:
                            group_link(last)
                    last.then_inc(tail_done[h], 1)
                    assert group_done[0] == GROUP_OPS, group_done


_INS = ['x', 'L0_conv_w1', 'L0_conv_b1', 'L0_conv_w2', 'L0_conv_b2', 'L0_conv_w3', 'L0_conv_b3', 'L0_ffn_W_gat',
        'L0_ffn_att_src', 'L0_ffn_att_dst', 'L0_ffn_b_gat', 'L0_ffn_ln_gamma', 'L0_ffn_ln_beta', 'L0_ffn_W1',
        'L0_ffn_b1', 'L0_ffn_W2', 'L0_ffn_b2', 'L0_ffn_edge_index']


def kernel(**inputs):
    import numpy as _np
    import concourse.bacc as _bacc
    from concourse import mybir as _mybir
    from concourse.bass_utils import run_bass_kernel_spmd as _run

    nc = _bacc.Bacc("TRN2", target_bir_lowering=False, num_devices=1)
    arrays, args = {}, []
    for name in _INS:
        a = _np.ascontiguousarray(inputs[name])
        arrays[f"in_{name}_dram"] = a
        args.append(nc.dram_tensor(f"in_{name}_dram", a.shape, _mybir.dt.from_np(a.dtype), kind="ExternalInput").ap())
    out = nc.dram_tensor("out_dram", (16, 32, 32, 128), _mybir.dt.float32, kind="ExternalOutput").ap()
    program(nc, *args, out)
    r = _run(nc, [arrays], core_ids=[0])
    return r.results[0]["out_dram"]
```
